# Optimizing a Trainium2 kernel written in Bass

```python
import numpy as np
import jax
import jax.numpy as jnp

def _softmax(x, axis=-1):
    return jax.nn.softmax(x, axis=axis)

def _gelu(x):
    return jax.nn.gelu(x, approximate=True)

def _silu(x):
    return jax.nn.silu(x)

def _sigmoid(x):
    return jax.nn.sigmoid(x)

def _layernorm(x, axis=-1, eps=1e-05):
    m = jnp.mean(x, axis=axis, keepdims=True)
    v = jnp.var(x, axis=axis, keepdims=True)
    return (x - m) / jnp.sqrt(v + eps)

def _scatter_add(tgt, idx, src, axis=0):
    return tgt.at[idx].add(src)

def _segment_sum(src, seg, n):
    return jax.ops.segment_sum(src, seg, n)
kernel_name = 'mk_seq_postln_d1_jaxref_r8_ddb7d6'

def setup_inputs(seed: int=0):
    np.random.seed(seed)
    _w = jnp.asarray

    def _L0_attn_setup():
        import jax, jax.numpy as jnp
        import numpy as np
        EPS = 1e-06
        N_HEADS = 4
        N_KV = 2

        def rmsnorm(x, w):
            xf = x.astype(jnp.float32)
            n = jax.lax.rsqrt(jnp.mean(jnp.square(xf), axis=-1, keepdims=True) + EPS)
            return (xf * n).astype(x.dtype) * w

        def selective_scan(x, delta, A, Bp, Cp, D_skip):
            Bb, L, D = x.shape
            N = A.shape[1]

            def step(h, inp):
                x_t, d_t, B_t, C_t = inp
                dA = jnp.exp(d_t[:, :, None] * A)
                h = dA * h + d_t[:, :, None] * B_t[:, None, :] * x_t[:, :, None]
                y_t = jnp.sum(h * C_t[:, None, :], axis=-1)
                return (h, y_t)
            h0 = jnp.zeros((Bb, D, N), x.dtype)
            xs = (x.transpose(1, 0, 2), delta.transpose(1, 0, 2), Bp.transpose(1, 0, 2), Cp.transpose(1, 0, 2))
            _, ys = jax.lax.scan(step, h0, xs)
            return ys.transpose(1, 0, 2) + x * D_skip

        def mamba_block(x, norm_m_w, in_proj_w, conv_w, conv_b, x_proj_w, dt_w, dt_b, A_log, D_skip, out_proj_w):
            d_inner = conv_w.shape[0]
            d_conv = conv_w.shape[-1]
            d_state = (x_proj_w.shape[0] - 1) // 2
            residual = x
            xn = rmsnorm(x, norm_m_w)
            xz = xn @ in_proj_w.T
            x_ssm, z = jnp.split(xz, 2, axis=-1)
            xc = x_ssm.transpose(0, 2, 1)
            xc = jax.lax.conv_general_dilated(xc, conv_w, window_strides=(1,), padding=[(d_conv - 1, 0)], feature_group_count=d_inner, dimension_numbers=('NCH', 'OIH', 'NCH')) + conv_b[None, :, None]
            x_ssm = jax.nn.silu(xc.transpose(0, 2, 1))
            ssm_p = x_ssm @ x_proj_w.T
            Bp = ssm_p[..., :d_state]
            Cp = ssm_p[..., d_state:2 * d_state]
            dt_raw = ssm_p[..., -1:]
            delta = jax.nn.softplus(dt_raw @ dt_w.T + dt_b)
            A = -jnp.exp(A_log)
            y = selective_scan(x_ssm, delta, A, Bp, Cp, D_skip)
            y = y * jax.nn.silu(z)
            return residual + y @ out_proj_w.T

        def attention_block(x, norm_attn_w, q_w, k_w, v_w, o_w, norm_ffn_w, gate_w, up_w, down_w):
            B, L, D = x.shape
            head_dim = D // N_HEADS
            scale = head_dim ** (-0.5)
            residual = x
            xn = rmsnorm(x, norm_attn_w)
            q = (xn @ q_w.T).reshape(B, L, N_HEADS, head_dim).transpose(0, 2, 1, 3)
            k = (xn @ k_w.T).reshape(B, L, N_KV, head_dim).transpose(0, 2, 1, 3)
            v = (xn @ v_w.T).reshape(B, L, N_KV, head_dim).transpose(0, 2, 1, 3)
            hpg = N_HEADS // N_KV
            k = jnp.repeat(k, hpg, axis=1)
            v = jnp.repeat(v, hpg, axis=1)
            attn = jnp.einsum('bhqd,bhkd->bhqk', q, k) * scale
            causal = jnp.triu(jnp.ones((L, L), dtype=bool), k=1)
            attn = jnp.where(causal[None, None], -jnp.inf, attn)
            attn = jax.nn.softmax(attn, axis=-1)
            out = jnp.einsum('bhqk,bhkd->bhqd', attn, v)
            out = out.transpose(0, 2, 1, 3).reshape(B, L, D) @ o_w.T
            x = residual + out
            residual = x
            xn = rmsnorm(x, norm_ffn_w)
            x_ffn = jax.nn.silu(xn @ gate_w.T) * (xn @ up_w.T) @ down_w.T
            return residual + x_ffn
        key = jax.random.key(seed)
        ks = jax.random.split(key, 16)
        d_model, d_state, d_conv, expand = (128, 16, 4, 2)
        d_inner = d_model * expand
        head_dim = d_model // N_HEADS
        ffn_h = int(d_model * 2.667)
        B, L = (4, 256)
        s = 0.02

        def rn(k, shape):
            return jax.random.normal(k, shape, jnp.float32) * s
        return {'x': jax.random.normal(ks[0], (B, L, d_model), jnp.float32), 'norm_m_w': jnp.ones(d_model, jnp.float32), 'in_proj_w': rn(ks[1], (d_inner * 2, d_model)), 'conv_w': rn(ks[2], (d_inner, 1, d_conv)), 'conv_b': jnp.zeros(d_inner, jnp.float32), 'x_proj_w': rn(ks[3], (d_state * 2 + 1, d_inner)), 'dt_w': rn(ks[4], (d_inner, 1)), 'dt_b': jnp.zeros(d_inner, jnp.float32), 'A_log': jnp.log(jnp.broadcast_to(jnp.arange(1, d_state + 1, dtype=jnp.float32), (d_inner, d_state))), 'D_skip': jnp.ones(d_inner, jnp.float32), 'out_proj_w': rn(ks[5], (d_model, d_inner)), 'norm_attn_w': jnp.ones(d_model, jnp.float32), 'q_w': rn(ks[6], (d_model, d_model)), 'k_w': rn(ks[7], (head_dim * N_KV, d_model)), 'v_w': rn(ks[8], (head_dim * N_KV, d_model)), 'o_w': rn(ks[9], (d_model, d_model)), 'norm_ffn_w': jnp.ones(d_model, jnp.float32), 'gate_w': rn(ks[10], (ffn_h, d_model)), 'up_w': rn(ks[11], (ffn_h, d_model)), 'down_w': rn(ks[12], (d_model, ffn_h))}
    _L0_attn_in = _L0_attn_setup()

    def _L0_ffn_setup():
        import jax, jax.numpy as jnp
        import numpy as np
        N_EMBD = 128
        N_STATE = 512
        key = jax.random.key(seed)
        k_x, k_w1, k_b1, k_w2, k_b2 = jax.random.split(key, 5)
        x = jax.random.normal(k_x, (4, 256, N_EMBD), dtype=jnp.float32)
        w1 = jax.random.normal(k_w1, (N_EMBD, N_STATE), dtype=jnp.float32) * (1.0 / np.sqrt(N_EMBD))
        b1 = jax.random.normal(k_b1, (N_STATE,), dtype=jnp.float32) * 0.02
        w2 = jax.random.normal(k_w2, (N_STATE, N_EMBD), dtype=jnp.float32) * (1.0 / np.sqrt(N_STATE))
        b2 = jax.random.normal(k_b2, (N_EMBD,), dtype=jnp.float32) * 0.02
        return {'x': x, 'w1': w1, 'b1': b1, 'w2': w2, 'b2': b2}
    _L0_ffn_in = _L0_ffn_setup()
    _d = {'L0_attn_x': _L0_attn_in['x'], 'L0_attn_norm_m_w': _L0_attn_in['norm_m_w'], 'L0_attn_in_proj_w': _L0_attn_in['in_proj_w'], 'L0_attn_conv_w': _L0_attn_in['conv_w'], 'L0_attn_conv_b': _L0_attn_in['conv_b'], 'L0_attn_x_proj_w': _L0_attn_in['x_proj_w'], 'L0_attn_dt_w': _L0_attn_in['dt_w'], 'L0_attn_dt_b': _L0_attn_in['dt_b'], 'L0_attn_A_log': _L0_attn_in['A_log'], 'L0_attn_D_skip': _L0_attn_in['D_skip'], 'L0_attn_out_proj_w': _L0_attn_in['out_proj_w'], 'L0_attn_norm_attn_w': _L0_attn_in['norm_attn_w'], 'L0_attn_q_w': _L0_attn_in['q_w'], 'L0_attn_k_w': _L0_attn_in['k_w'], 'L0_attn_v_w': _L0_attn_in['v_w'], 'L0_attn_o_w': _L0_attn_in['o_w'], 'L0_attn_norm_ffn_w': _L0_attn_in['norm_ffn_w'], 'L0_attn_gate_w': _L0_attn_in['gate_w'], 'L0_attn_up_w': _L0_attn_in['up_w'], 'L0_attn_down_w': _L0_attn_in['down_w'], 'L0_ffn_w1': _L0_ffn_in['w1'], 'L0_ffn_b1': _L0_ffn_in['b1'], 'L0_ffn_w2': _L0_ffn_in['w2'], 'L0_ffn_b2': _L0_ffn_in['b2']}
    _x0 = _d['L0_attn_x']
    _d['L0_attn_x'] = jax.random.normal(jax.random.fold_in(jax.random.key(seed), 1), (2, 1024, 128), dtype=_x0.dtype)
    del _x0
    return _d

def reference(L0_attn_x, L0_attn_norm_m_w, L0_attn_in_proj_w, L0_attn_conv_w, L0_attn_conv_b, L0_attn_x_proj_w, L0_attn_dt_w, L0_attn_dt_b, L0_attn_A_log, L0_attn_D_skip, L0_attn_out_proj_w, L0_attn_norm_attn_w, L0_attn_q_w, L0_attn_k_w, L0_attn_v_w, L0_attn_o_w, L0_attn_norm_ffn_w, L0_attn_gate_w, L0_attn_up_w, L0_attn_down_w, L0_ffn_w1, L0_ffn_b1, L0_ffn_w2, L0_ffn_b2):

    def _L0_attn_ref(x, norm_m_w, in_proj_w, conv_w, conv_b, x_proj_w, dt_w, dt_b, A_log, D_skip, out_proj_w, norm_attn_w, q_w, k_w, v_w, o_w, norm_ffn_w, gate_w, up_w, down_w):
        import jax, jax.numpy as jnp
        import numpy as np
        EPS = 1e-06
        N_HEADS = 4
        N_KV = 2

        def rmsnorm(x, w):
            xf = x.astype(jnp.float32)
            n = jax.lax.rsqrt(jnp.mean(jnp.square(xf), axis=-1, keepdims=True) + EPS)
            return (xf * n).astype(x.dtype) * w

        def selective_scan(x, delta, A, Bp, Cp, D_skip):
            Bb, L, D = x.shape
            N = A.shape[1]

            def step(h, inp):
                x_t, d_t, B_t, C_t = inp
                dA = jnp.exp(d_t[:, :, None] * A)
                h = dA * h + d_t[:, :, None] * B_t[:, None, :] * x_t[:, :, None]
                y_t = jnp.sum(h * C_t[:, None, :], axis=-1)
                return (h, y_t)
            h0 = jnp.zeros((Bb, D, N), x.dtype)
            xs = (x.transpose(1, 0, 2), delta.transpose(1, 0, 2), Bp.transpose(1, 0, 2), Cp.transpose(1, 0, 2))
            _, ys = jax.lax.scan(step, h0, xs)
            return ys.transpose(1, 0, 2) + x * D_skip

        def mamba_block(x, norm_m_w, in_proj_w, conv_w, conv_b, x_proj_w, dt_w, dt_b, A_log, D_skip, out_proj_w):
            d_inner = conv_w.shape[0]
            d_conv = conv_w.shape[-1]
            d_state = (x_proj_w.shape[0] - 1) // 2
            residual = x
            xn = rmsnorm(x, norm_m_w)
            xz = xn @ in_proj_w.T
            x_ssm, z = jnp.split(xz, 2, axis=-1)
            xc = x_ssm.transpose(0, 2, 1)
            xc = jax.lax.conv_general_dilated(xc, conv_w, window_strides=(1,), padding=[(d_conv - 1, 0)], feature_group_count=d_inner, dimension_numbers=('NCH', 'OIH', 'NCH')) + conv_b[None, :, None]
            x_ssm = jax.nn.silu(xc.transpose(0, 2, 1))
            ssm_p = x_ssm @ x_proj_w.T
            Bp = ssm_p[..., :d_state]
            Cp = ssm_p[..., d_state:2 * d_state]
            dt_raw = ssm_p[..., -1:]
            delta = jax.nn.softplus(dt_raw @ dt_w.T + dt_b)
            A = -jnp.exp(A_log)
            y = selective_scan(x_ssm, delta, A, Bp, Cp, D_skip)
            y = y * jax.nn.silu(z)
            return residual + y @ out_proj_w.T

        def attention_block(x, norm_attn_w, q_w, k_w, v_w, o_w, norm_ffn_w, gate_w, up_w, down_w):
            B, L, D = x.shape
            head_dim = D // N_HEADS
            scale = head_dim ** (-0.5)
            residual = x
            xn = rmsnorm(x, norm_attn_w)
            q = (xn @ q_w.T).reshape(B, L, N_HEADS, head_dim).transpose(0, 2, 1, 3)
            k = (xn @ k_w.T).reshape(B, L, N_KV, head_dim).transpose(0, 2, 1, 3)
            v = (xn @ v_w.T).reshape(B, L, N_KV, head_dim).transpose(0, 2, 1, 3)
            hpg = N_HEADS // N_KV
            k = jnp.repeat(k, hpg, axis=1)
            v = jnp.repeat(v, hpg, axis=1)
            attn = jnp.einsum('bhqd,bhkd->bhqk', q, k) * scale
            causal = jnp.triu(jnp.ones((L, L), dtype=bool), k=1)
            attn = jnp.where(causal[None, None], -jnp.inf, attn)
            attn = jax.nn.softmax(attn, axis=-1)
            out = jnp.einsum('bhqk,bhkd->bhqd', attn, v)
            out = out.transpose(0, 2, 1, 3).reshape(B, L, D) @ o_w.T
            x = residual + out
            residual = x
            xn = rmsnorm(x, norm_ffn_w)
            x_ffn = jax.nn.silu(xn @ gate_w.T) * (xn @ up_w.T) @ down_w.T
            return residual + x_ffn
        h = mamba_block(x, norm_m_w, in_proj_w, conv_w, conv_b, x_proj_w, dt_w, dt_b, A_log, D_skip, out_proj_w)
        return attention_block(h, norm_attn_w, q_w, k_w, v_w, o_w, norm_ffn_w, gate_w, up_w, down_w)

    def _L0_ffn_ref(x, w1, b1, w2, b2):
        import jax, jax.numpy as jnp
        import numpy as np
        N_EMBD = 128
        N_STATE = 512
        h = jax.nn.gelu(jnp.einsum('bse,eh->bsh', x, w1) + b1, approximate=False)
        return jnp.einsum('bsh,he->bse', h, w2) + b2
    x = L0_attn_x
    x = _layernorm(x + _L0_attn_ref(x, L0_attn_norm_m_w, L0_attn_in_proj_w, L0_attn_conv_w, L0_attn_conv_b, L0_attn_x_proj_w, L0_attn_dt_w, L0_attn_dt_b, L0_attn_A_log, L0_attn_D_skip, L0_attn_out_proj_w, L0_attn_norm_attn_w, L0_attn_q_w, L0_attn_k_w, L0_attn_v_w, L0_attn_o_w, L0_attn_norm_ffn_w, L0_attn_gate_w, L0_attn_up_w, L0_attn_down_w), axis=-1)
    x = _layernorm(x + _L0_ffn_ref(x, L0_ffn_w1, L0_ffn_b1, L0_ffn_w2, L0_ffn_b2), axis=-1)
    return x

_drawn_inputs = setup_inputs


def setup_inputs(seed=0):
    import zlib

    import numpy as np

    out = dict(_drawn_inputs(seed))
    spreads = {'L0_attn_norm_m_w': (1.0, 0.6),
     'L0_attn_conv_b': (0.0, 0.8),
     'L0_attn_dt_b': (0.0, 0.8),
     'L0_attn_D_skip': (1.0, 0.6),
     'L0_attn_norm_attn_w': (1.0, 0.6),
     'L0_attn_norm_ffn_w': (1.0, 0.6)}
    factors = {'L0_attn_in_proj_w': 8.0,
     'L0_attn_conv_w': 8.0,
     'L0_attn_x_proj_w': 8.0,
     'L0_attn_dt_w': 8.0,
     'L0_attn_A_log': 8.0,
     'L0_attn_out_proj_w': 8.0,
     'L0_attn_q_w': 8.0,
     'L0_attn_k_w': 8.0,
     'L0_attn_v_w': 8.0,
     'L0_attn_o_w': 8.0,
     'L0_attn_gate_w': 8.0,
     'L0_attn_up_w': 8.0,
     'L0_attn_down_w': 8.0,
     'L0_ffn_b1': 5.123,
     'L0_ffn_b2': 3.319}
    for name, (base, spread) in spreads.items():
        noise = np.random.default_rng([zlib.crc32(name.encode()), seed]).standard_normal(out[name].shape)
        drawn = base * np.exp(spread * noise) if base else spread * noise
        out[name] = jnp.asarray(drawn.astype(out[name].dtype))
    for name, factor in factors.items():
        out[name] = (out[name] * factor).astype(out[name].dtype)
    return out
```

```python
import concourse.bass as bass
from concourse import mybir
from contextlib import ExitStack

BATCH, SEQ, D = 2, 1024, 128
DI, NSTATE, DCONV = 256, 16, 4
HEADS, KV, HD = 4, 2, 32
FFN, MLP = 341, 512
CT = 512
NC = SEQ // CT
NH = DI // 128
NS, DS = 4, 32
NG, DG = NSTATE // NS, DI // DS
QT = SEQ // 128
FM = [128, 128, FFN - 256]
MM = MLP // 128
EPS_RMS, EPS_LN = 1e-6, 1e-5

W_COLS = {"in": 512, "xp": 2 * 33, "nm": 1, "na": 1, "nf": 1, "cb": 2, "dtw": 2, "dtb": 2, "dsk": 2,
          "b1": 4, "alog": 32, "out": 256, "q": 128, "k": 64, "v": 64, "o": 128, "gate": FFN,
          "up": FFN, "down": 384, "w1": 512, "w2": 512}
C_COLS = {"ident": 128, "center": 128, "mean": 128, "selD": 128, "selB": 128, "selC": 128, "sum": 32,
          "mask": 128, "ones": 128}


def offsets(cols):
    at, out = 0, {}
    for name, n in cols.items():
        out[name] = (at, n)
        at += n
    return out, at


W_AT, W_ALL = offsets(W_COLS)
C_AT, C_ALL = offsets(C_COLS)
W_FIRST = W_AT["out"][0]

SIGNALS = {
    "a_ready": 1, "nega_ready": 1, "square_ready": 8, "meansq_ready": 8, "log_ready": 8, "rstd_ready": 8, "xn_ready": 2,
    "inproj_ready": 8, "tanh_ready": 8, "gated_ready": 8,
    "xproj_ready": 2, "bc_ready": 2, "dtpre_ready": 4, "abs_ready": 2, "expabs_ready": 2, "log1p_ready": 2,
    "u_ready": 2, "resid_ready": 2, "relulog_ready": 2, "delta_ready": 2, "du_ready": 2,
    "brep_ready": 8, "crep_ready": 8, "b_stored": 8, "c_stored": 8,
    "drep_ready": 8, "durep_ready": 8, "decay_ready": 64, "drive_ready": 64, "state_ready": 64,
    "hc_ready": 64, "hc_summed": 64, "yskip_ready": 4, "y_ready": 4,
    "outproj_ready": 2, "h1_ready": 2, "xn2_ready": 2, "qk_ready": 2, "v_ready": 2, "v_stored": 2,
    "part1_ready": 2, "rest1_ready": 2, "part2_ready": 2, "part3_ready": 2,
    "stack_ready": 12, "stack_a_stored": 11, "stack_b_stored": 1,
    "scores_ready": 32, "max_ready": 32, "maxpart_ready": 4, "maxrow_ready": 2, "maxrow_a_stored": 2,
    "maxrow_b_stored": 2, "scorest_ready": 48, "probs_ready": 48, "pv_ready": 12, "logden_ready": 2,
    "rden_ready": 2, "attn_stored": 2,
    "oproj_ready": 2, "h2_ready": 2, "xn3_ready": 2,
    "gateup_ready": 6, "gtanh_ready": 6, "gsilu_ready": 6, "swiglu_ready": 6,
    "down_ready": 2, "h3_ready": 2, "sum_ready": 2, "centered_ready": 2, "ln1_ready": 2,
    "mlp_ready": 8, "gelu_ready": 8, "mlpout_ready": 2, "stats_ready": 8, "meanvar_ready": 8,
    "logvar_ready": 1, "rstd2_ready": 1, "out_ready": 1,
}


def build(nc, x, wts, cst, convw, b2, out):
    fp32, bf16 = mybir.dt.float32, mybir.dt.bfloat16
    ALU, ACT, AX = mybir.AluOpType, mybir.ActivationFunctionType, mybir.AxisListType
    LN_EXP = "natural_log_exp_and_others"

    ctx = ExitStack()
    with ctx:
        def sb(name, shape, dt=fp32):
            return ctx.enter_context(nc.sbuf_tensor(name, shape, dt))

        def sem(name):
            return ctx.enter_context(nc.semaphore(name))

        w_sb = sb("w_sb", [128, W_ALL])
        c_sb = sb("c_sb", [128, C_ALL])

        def W(name, a=0, b=None):
            at, n = W_AT[name]
            return w_sb[:, at + a:at + (n if b is None else b)]

        def C(name):
            at, n = C_AT[name]
            return c_sb[:, at:at + n]

        b2_sb = sb("b2_sb", [1, D])
        win_sb = sb("win_sb", [128, 2 * DI])
        wconv_sb = sb("wconv_sb", [128, DCONV, DI])
        wbc_sb = sb("wbc_sb", [128, NH, 4, 32])
        wdt_sb = sb("wdt_sb", [128, NH, 128])
        wout_sb = sb("wout_sb", [128, NH, D])
        wq_sb = sb("wq_sb", [128, D])
        wk_sb = sb("wk_sb", [128, HEADS, HD])
        wv_sb = sb("wv_sb", [128, KV * HD])
        wgate_sb = sb("wgate_sb", [128, FFN])
        wup_sb = sb("wup_sb", [128, FFN])
        wdown_sb = sb("wdown_sb", [128, 3, D])
        a_sb = sb("a_sb", [128, DG * NG])
        nega_sb = sb("nega_sb", [128, DG * NG])
        cbh_sb = sb("cbh_sb", [128, NH])
        dskh_sb = sb("dskh_sb", [128, NH])
        identb = sb("identb", [128, 128], bf16)
        maskb = sb("maskb", [128, 128], bf16)
        eps_sb = sb("eps_sb", [128, 2])

        x_sb = sb("x_sb", [128, SEQ])
        rstd_sb = sb("rstd_sb", [128, NC, CT])
        xn_sb = sb("xn_sb", [128, DCONV - 1 + SEQ])
        xs_sb = sb("xs_sb", [128, NC, NH, CT])
        zs_sb = sb("zs_sb", [128, NC, NH, CT])
        bc_sb = sb("bc_sb", [128, NC, CT])
        dt_sb = sb("dt_sb", [128, NC, NH, CT])
        e_sb = sb("e_sb", [128, NC, NH, CT])
        l_sb = sb("l_sb", [128, NC, NH, CT])
        delta_sb = sb("delta_sb", [128, NC, NH, CT])
        du_sb = sb("du_sb", [128, NC, NH, CT])
        brep_sb = sb("brep_sb", [128, NC, NG, CT])
        crep_sb = sb("crep_sb", [128, NC, NG, CT])
        NDEC, NDRV, NST, NHC = 6, 4, 12, 4
        decay_sb = sb("decay_sb", [128, NDEC, CT])
        drive_sb = sb("drive_sb", [128, NDRV, CT])
        state_sb = sb("state_sb", [128, NST, CT])
        hc_sb = sb("hc_sb", [128, NHC, CT])
        y_sb = dt_sb
        convw_sb = decay_sb[:, 0:2, :].rearrange("p a t -> p (a t)").rearrange("p (j d) -> p j d", j=DCONV)
        v_sb, th_sb = drive_sb, state_sb[:, 0:4, :]
        u_sb, r_sb = hc_sb[:, 0:2, :], hc_sb[:, 2:4, :]
        out_sb = decay_sb[:, 2:4, :].rearrange("p a t -> p (a t)").rearrange("p (t d) -> p t d", t=QT)
        h1_sb = zs_sb[:, 0, :, :].rearrange("p a t -> p (a t)")
        xn2_sb = e_sb[:, 0, :, :].rearrange("p a t -> p (a t)")
        attn_sb = l_sb[:, 1, :, :].rearrange("p a t -> p (a t)")
        vt_sb = sb("vt_sb", [128, QT, KV * HD])
        crep_b = crep_sb[:, :, :, :].rearrange("p c g t -> p (c g t)").bitcast(bf16)
        part_sb = [crep_b[:, 2 * SEQ * n:2 * SEQ * (n + 1)].rearrange("p (w t) -> p w t", w=2) for n in range(3)]
        rest_sb = drive_sb[:, :, :].rearrange("p (c w) t -> p c w t", c=NC)
        state_b = state_sb[:, :, :].rearrange("p a t -> p (a t)").bitcast(bf16)
        qstack = state_b[:, 0:2 * HEADS * SEQ].rearrange("p (m h t) -> p m h t", m=2, h=HEADS)
        kstack = sb("kstack", [128, 2, KV, SEQ], bf16)
        Q_PARTS = [(0, 0, 1), (1, 0, 2)]
        K_PARTS = [(0, 1, 0), (1, 2, 0)]
        sq_sb, log_sb = decay_sb[:, 4:6, :], hc_sb[:, 0:2, :]
        pt_sb = brep_sb[:, :, :, :]
        negmax_sb = sb("negmax_sb", [128, QT * HEADS])
        maxpart_sb = sb("maxpart_sb", [128, NC, 16, 2], bf16)
        rden_sb = rstd_sb
        h2_sb = du_sb[:, 0, :, :].rearrange("p a t -> p (a t)")
        swi_sb = brep_sb[:, :, 0:3, :]
        s_sb = delta_sb[:, 0, :, :]
        ln1_sb = delta_sb[:, 1, :, :]
        gelu_sb = crep_sb
        stats_sb = sb("stats_sb", [128, QT, 6])
        mv_sb = sb("mv_sb", [128, QT, 2])
        lv_sb = sb("lv_sb", [128, QT])
        spare_sb = sb("spare_sb", [128, 1])
        rs2_sb = sb("rs2_sb", [128, QT])

        ps = ctx.enter_context(nc.psum_tensor("ps", [128, 8 * CT], fp32))

        def bank(k, a=0, b=CT, rows=slice(0, 128)):
            return ps[rows, k * CT + a:k * CT + b]

        DU_BANK = [2, 6]
        BC_BANK = [6, 4]
        def banks(k, n, rows=slice(0, 128)):
            return ps[rows, k * CT:(k + n) * CT].rearrange("p (w t) -> p w t", w=n)

        MEANSQ = [4, 5, 6, 7, 6, 7, 6, 7]

        loaded = sem("loaded")
        rest_loaded = sem("rest_loaded")
        consts_loaded = sem("consts_loaded")
        x_loaded = sem("x_loaded")
        out_free = sem("out_free")
        setup_dve = sem("setup_dve")
        setup_pool = sem("setup_pool")
        S = {name: sem(name) for name in SIGNALS}

        def turns(b):
            def wait(eng, name, k):
                eng.wait_ge(S[name], b * SIGNALS[name] + k)
            return wait

        def stack_target(u):
            c, m, pair = stack_unit(u)
            at = slice(c * CT, (c + 1) * CT)
            return kstack[0:96, m, :, at] if pair == 0 else qstack[0:96, m, 2 * pair - 2:2 * pair, at]

        block = ctx.enter_context(nc.Block())
        N_SETUP_DVE = 3

        @block.sync
        def _(sp):
            sp.dma_start(x_sb[:, :], x[:, 0:SEQ]).then_inc(x_loaded, 16)
            sp.dma_start(c_sb[:, :], cst).then_inc(consts_loaded, 16)
            sp.dma_start(w_sb[:, 0:W_FIRST], wts[:, 0:W_FIRST]).then_inc(loaded, 16)
            sp.dma_start(convw_sb[:, :, :].rearrange("p j d -> p (j d)"),
                         convw.to_broadcast([128, DCONV * DI])).then_inc(loaded, 16)
            sp.dma_start(w_sb[:, W_FIRST:], wts[:, W_FIRST:]).then_inc(rest_loaded, 16)
            sp.dma_start(b2_sb[:, :], b2).then_inc(out_free, 16)
            for b in range(BATCH):
                if b + 1 < BATCH:
                    sp.wait_ge(S["sum_ready"], NC * (b + 1))
                    sp.dma_start(x_sb[:, :], x[:, (b + 1) * SEQ:(b + 2) * SEQ]).then_inc(x_loaded, 16)
                sp.wait_ge(S["out_ready"], b + 1)
                sp.dma_start(out[:, b * QT:(b + 1) * QT, :], out_sb[:, :, :]).then_inc(out_free, 16)
            sp.wait_ge(out_free, 16 + 16 * BATCH)

        @block.gpsimd
        def _(pool):
            nc.gpsimd.memset(xn_sb[:, 0:DCONV - 1], 0.0)
            nc.gpsimd.memset(eps_sb[:, 0:1], EPS_RMS)
            nc.gpsimd.memset(eps_sb[:, 1:2], EPS_LN).then_inc(setup_pool, 1)
            pool.wait_ge(loaded, 32)
            nc.gpsimd.tensor_scalar(wbc_sb[:, :, :, :],
                                    W("xp").rearrange("p (h n) -> p h n", h=NH)[:, :, 0:32]
                                    .rearrange("p h (a n) -> p h a n", a=1).to_broadcast([128, NH, 4, 32]),
                                    0.5, 1.0, ALU.mult, ALU.mult)
            for h in range(NH):
                nc.gpsimd.tensor_scalar(wdt_sb[:, h, :], W("xp", 33 * h + 32, 33 * h + 33).to_broadcast([128, 128]),
                                        0.5, 1.0, ALU.mult, ALU.mult)
            nc.gpsimd.tensor_scalar(dskh_sb[:, :], W("dsk"), 0.5, 1.0, ALU.mult, ALU.mult).then_inc(setup_pool, 1)
            pool.wait_ge(rest_loaded, 16)
            pool.wait_ge(consts_loaded, 16)
            nc.gpsimd.tensor_scalar(wout_sb[:, :, :].rearrange("p h n -> p (h n)"), W("out"), 0.5, 1.0, ALU.mult,
                                    ALU.mult)
            nc.gpsimd.tensor_scalar(wq_sb[:, :], W("q"), W("na"), float(HD) ** -0.5, ALU.mult, ALU.mult)
            nc.gpsimd.tensor_scalar(wk_sb[:, :, :].rearrange("p (k r) d -> p k r d", k=KV),
                                    W("k").rearrange("p (k a d) -> p k a d", k=KV, a=1)
                                    .to_broadcast([128, KV, HEADS // KV, HD]), W("na"), 1.0, ALU.mult, ALU.mult)
            nc.gpsimd.tensor_scalar(wv_sb[:, :], W("v"), W("na"), 1.0, ALU.mult, ALU.mult)
            nc.gpsimd.tensor_scalar(wgate_sb[:, :], W("gate"), W("nf"), 1.0, ALU.mult, ALU.mult)
            nc.gpsimd.tensor_scalar(wup_sb[:, :], W("up"), W("nf"), 1.0, ALU.mult, ALU.mult)
            nc.gpsimd.tensor_scalar(wdown_sb[:, :, :].rearrange("p h n -> p (h n)"), W("down"), 0.5, 1.0, ALU.mult,
                                    ALU.mult)
            nc.gpsimd.tensor_copy(identb[:, :], C("ident"))
            nc.gpsimd.tensor_copy(maskb[:, :], C("mask")).then_inc(setup_pool, 1)
            with pool.Fori(0, BATCH) as b:
                wait = turns(b)
                for c in range(NC):
                    wait(pool, "delta_ready", c + 1)
                    nc.gpsimd.tensor_tensor(du_sb[:, c, :, :], delta_sb[:, c, :, :], xs_sb[:, c, :, :],
                                            ALU.mult).then_inc(S["du_ready"], 1)
                for i in range(64):
                    _, c, ng, _ = scan_tile(i)
                    wait(pool, "state_ready", i + 1)
                    if i == 0:
                        wait(pool, "c_stored", NG * NC)
                    if i >= NHC:
                        wait(pool, "hc_summed", i - NHC + 1)
                    nc.gpsimd.tensor_tensor(hc_sb[:, i % NHC, :], state_sb[:, i % NST, :], crep_sb[:, c, ng, :],
                                            ALU.mult).then_inc(S["hc_ready"], 1)
                for c in range(NC):
                    at = slice(c * CT, (c + 1) * CT)
                    wait(pool, "part2_ready", c + 1)
                    nc.gpsimd.tensor_tensor(part_sb[2][:, :, at], rest_sb[:, c, :, :], part_sb[1][:, :, at],
                                            ALU.subtract).then_inc(S["part3_ready"], 1)

        @block.scalar
        def _(act):
            act.wait_ge(setup_pool, 1)

            def squares(src, k):
                nc.scalar.activation(sq_sb[:, k % 2, :], src, ACT.Square).then_inc(S["square_ready"], 1)

            def rstd(wait, k, eps):
                wait(act, "meansq_ready", k + 1)
                nc.scalar.activation(log_sb[:, k % 2, :], bank(MEANSQ[k]), ACT.Ln,
                                     bias=eps_sb[:, eps:eps + 1]).then_inc(S["log_ready"], 1)
                wait(act, "log_ready", k + 1)
                nc.scalar.activation(rstd_sb[:, k % 2, :], log_sb[:, k % 2, :], ACT.Exp,
                                     scale=-0.5).then_inc(S["rstd_ready"], 1)

            with act.Fori(0, BATCH) as b:
                wait = turns(b)
                act.preload_act_table_set(LN_EXP)
                act.wait_ge(x_loaded, 16 * b + 16)
                for c in range(NC):
                    squares(x_sb[:, c * CT:(c + 1) * CT], c)
                for c in range(NC):
                    rstd(wait, c, 0)
                act.wait_ge(loaded, 32)
                nc.scalar.activation(a_sb[:, :], W("alog"), ACT.Exp).then_inc(S["a_ready"], 1)
                act.preload_act_table_set("exp_and_others")
                act.wait_ge(setup_dve, N_SETUP_DVE)
                for u in range(8):
                    half = u % 2
                    wait(act, "inproj_ready", u + 1)
                    if u >= 4:
                        wait(act, "gated_ready", u - 3)
                    if u % 4 < 2:
                        nc.scalar.activation(v_sb[:, u % 4, :], bank(u % 4), ACT.Identity,
                                             bias=W("cb", half, half + 1))
                        nc.scalar.activation(th_sb[:, u % 4, :], bank(u % 4), ACT.Tanh, scale=0.5,
                                             bias=cbh_sb[:, half:half + 1]).then_inc(S["tanh_ready"], 1)
                    else:
                        nc.scalar.activation(th_sb[:, u % 4, :], bank(u % 4), ACT.Tanh,
                                             scale=0.5).then_inc(S["tanh_ready"], 1)
                act.wait_ge(consts_loaded, 16)
                act.preload_act_table_set(LN_EXP)
                for c in range(NC):
                    wait(act, "xproj_ready", c + 1)
                    nc.scalar.activation(bc_sb[:, c, :], bank(BC_BANK[c]), ACT.Copy).then_inc(S["bc_ready"], 1)
                    wait(act, "dtpre_ready", 2 * c + 2)
                    nc.scalar.activation(l_sb[:, c, :, :], dt_sb[:, c, :, :], ACT.Abs).then_inc(S["abs_ready"], 1)
                    wait(act, "abs_ready", c + 1)
                    nc.scalar.activation(e_sb[:, c, :, :], l_sb[:, c, :, :], ACT.Exp,
                                         scale=-1.0).then_inc(S["expabs_ready"], 1)
                    wait(act, "expabs_ready", c + 1)
                    nc.scalar.activation(l_sb[:, c, :, :], e_sb[:, c, :, :], ACT.Ln,
                                         bias=C("ones")[:, 0:1]).then_inc(S["log1p_ready"], 1)
                for k in range(NC * NG):
                    wait(act, "brep_ready", k + 1)
                    nc.scalar.activation(brep_sb[:, k // NG, k % NG, :], bank(2 * (k % 2)),
                                         ACT.Copy).then_inc(S["b_stored"], 1)
                act.wait_ge(out_free, 16 * b + 16)
                wait(act, "nega_ready", 1)
                for i in range(64):
                    pr, c, ng, s = scan_tile(i)
                    if ng == 0:
                        wait(act, "drep_ready", i // 8 + 1)
                    if i >= NDEC:
                        wait(act, "state_ready", i - NDEC + 1)
                    col = (2 * pr + s) * NG + ng
                    nc.scalar.activation(decay_sb[:, i % NDEC, :], bank(s), ACT.Exp,
                                         scale=nega_sb[:, col:col + 1]).then_inc(S["decay_ready"], 1)
                for c in range(NC):
                    wait(act, "h1_ready", c + 1)
                    squares(h1_sb[:, c * CT:(c + 1) * CT], 2 + c)
                    rstd(wait, 2 + c, 0)
                for c in range(NC):
                    at = slice(c * CT, (c + 1) * CT)
                    wait(act, "qk_ready", c + 1)
                    nc.scalar.activation(part_sb[0][:, :, at], banks(2 * c, 2),
                                         ACT.Copy).then_inc(S["part1_ready"], 1)
                for c in range(NC):
                    at = slice(c * CT, (c + 1) * CT)
                    wait(act, "rest1_ready", c + 1)
                    nc.scalar.activation(part_sb[1][:, :, at], rest_sb[:, c, :, :],
                                         ACT.Copy).then_inc(S["part2_ready"], 1)

                for u in range(12):
                    if stack_reader(u) == "stack_a_stored":
                        wait(act, "stack_ready", u + 1)
                        nc.scalar.activation(stack_target(u), banks(4 + 2 * (u % 2), 2, rows=slice(0, 96)),
                                             ACT.Copy).then_inc(S["stack_a_stored"], 1)

                def max_rows(c):
                    wait(act, "maxrow_ready", c + 1)
                    nc.scalar.activation(qstack[96:98, 0, 0:2, c * CT:(c + 1) * CT],
                                         banks(0, 2, rows=slice(96, 98)), ACT.Copy).then_inc(S["maxrow_a_stored"], 1)

                def exponential(v):
                    c, j, h, q0 = st_unit(v)
                    wait(act, "scorest_ready", v + 1)
                    if v >= 8:
                        wait(act, "pv_ready", v // 4 - 1)
                    nc.scalar.activation(pt_sb[:, v // 4 % 2, h, q0:CT], bank(st_bank(v), q0, CT),
                                         ACT.Exp).then_inc(S["probs_ready"], 1)

                def inverse_sum(c):
                    wait(act, "pv_ready", 4 if c == 0 else 12)
                    nc.scalar.activation(log_sb[:, c, :], bank(7), ACT.Ln).then_inc(S["logden_ready"], 1)
                    wait(act, "logden_ready", c + 1)
                    nc.scalar.activation(rden_sb[:, c, :], log_sb[:, c, :], ACT.Exp,
                                         scale=-1.0).then_inc(S["rden_ready"], 1)

                max_rows(0)
                for v in range(16):
                    exponential(v)
                max_rows(1)
                inverse_sum(0)
                for v in range(16, 48):
                    exponential(v)
                inverse_sum(1)
                for c in range(NC):
                    wait(act, "h2_ready", c + 1)
                    squares(h2_sb[:, c * CT:(c + 1) * CT], 4 + c)
                    rstd(wait, 4 + c, 0)
                act.preload_act_table_set("exp_and_others")
                for u in range(6):
                    rows = slice(0, FM[u % 3])
                    wait(act, "gateup_ready", u + 1)
                    if u >= 4:
                        wait(act, "gsilu_ready", u - 3)
                    nc.scalar.activation(th_sb[rows, u % 4, :], bank(2 * (u % 2), rows=rows), ACT.Tanh,
                                         scale=0.5).then_inc(S["gtanh_ready"], 1)
                act.preload_act_table_set(LN_EXP)
                for c in range(NC):
                    wait(act, "centered_ready", c + 1)
                    squares(bank(4 + c), 6 + c)
                for c in range(NC):
                    rstd(wait, 6 + c, 1)
                for u in range(8):
                    m = u % MM
                    wait(act, "mlp_ready", u + 1)
                    nc.scalar.activation(gelu_sb[:, u // MM, m, :], bank(u % 4), ACT.Gelu,
                                         bias=W("b1", m, m + 1)).then_inc(S["gelu_ready"], 1)
                act.preload_act_table_set(LN_EXP)
                wait(act, "meanvar_ready", 8)
                nc.scalar.activation(lv_sb[:, :], mv_sb[:, :, 1], ACT.Ln,
                                     bias=eps_sb[:, 1:2]).then_inc(S["logvar_ready"], 1)
                wait(act, "logvar_ready", 1)
                nc.scalar.activation(rs2_sb[:, :], lv_sb[:, :], ACT.Exp,
                                     scale=-0.5).then_inc(S["rstd2_ready"], 1)

        @block.vector
        def _(dve):
            nc.vector.memset(kstack[96:98, 0, :, :], 1.0)
            dve.wait_ge(loaded, 32)
            nc.vector.tensor_scalar(win_sb[:, :], W("in"), W("nm"), None, ALU.mult).then_inc(setup_dve, 1)
            nc.vector.tensor_scalar(cbh_sb[:, :], W("cb"), 0.5, None, ALU.mult).then_inc(setup_dve, 1)
            dve.wait_ge(setup_dve, 2)
            for j in range(DCONV):
                last = nc.vector.tensor_tensor(wconv_sb[:, j, :], win_sb[:, 0:DI], convw_sb[:, j, :], ALU.mult)
            last.then_inc(setup_dve, 1)
            assert N_SETUP_DVE == 3

            def c_spread(wait, k):
                wait(dve, "crep_ready", k + 1)
                nc.vector.tensor_copy(crep_sb[:, k // NG, k % NG, :], bank(2 * (k % 2) + 1)).then_inc(S["c_stored"], 1)

            with dve.Fori(0, BATCH) as b:
                wait = turns(b)
                dve.wait_ge(x_loaded, 16 * b + 16)
                for c in range(NC):
                    wait(dve, "rstd_ready", c + 1)
                    nc.vector.tensor_tensor(xn_sb[:, DCONV - 1 + c * CT:DCONV - 1 + (c + 1) * CT],
                                            x_sb[:, c * CT:(c + 1) * CT], rstd_sb[:, c, :],
                                            ALU.mult).then_inc(S["xn_ready"], 1)
                dve.wait_ge(setup_pool, 2)
                for u in range(8):
                    c, half = u // 4, u % 2
                    wait(dve, "tanh_ready", u + 1)
                    src = v_sb[:, u % 4, :] if u % 4 < 2 else bank(u % 4)
                    dst = xs_sb if u % 4 < 2 else zs_sb
                    nc.vector.scalar_tensor_tensor(out=dst[:, c, half, :], in0=th_sb[:, u % 4, :], scalar=1.0, in1=src,
                                                   op0=ALU.add, op1=ALU.mult).then_inc(S["gated_ready"], 1)
                wait(dve, "a_ready", 1)
                nc.vector.tensor_scalar(nega_sb[:, :], a_sb[:, :], -1.0, None, ALU.mult).then_inc(S["nega_ready"], 1)
                for c in range(NC):
                    wait(dve, "xproj_ready", c + 1)
                    for h in range(NH):
                        nc.vector.tensor_scalar(dt_sb[:, c, h, :], bank(BC_BANK[c] + 1), W("dtw", h, h + 1),
                                                W("dtb", h, h + 1), ALU.mult, ALU.add).then_inc(S["dtpre_ready"], 1)
                for c in range(NC):
                    wait(dve, "expabs_ready", c + 1)
                    if c:
                        wait(dve, "delta_ready", c)
                    nc.vector.tensor_scalar(u_sb[:, :, :], e_sb[:, c, :, :], 1.0, None,
                                            ALU.add).then_inc(S["u_ready"], 1)
                    c_spread(wait, 4 * c)
                    wait(dve, "u_ready", c + 1)
                    nc.vector.scalar_tensor_tensor(out=r_sb[:, :, :], in0=u_sb[:, :, :], scalar=-1.0,
                                                   in1=e_sb[:, c, :, :], op0=ALU.add,
                                                   op1=ALU.subtract).then_inc(S["resid_ready"], 1)
                    wait(dve, "log1p_ready", c + 1)
                    nc.vector.scalar_tensor_tensor(out=delta_sb[:, c, :, :], in0=dt_sb[:, c, :, :], scalar=0.0,
                                                   in1=l_sb[:, c, :, :], op0=ALU.max,
                                                   op1=ALU.add).then_inc(S["relulog_ready"], 1)
                    c_spread(wait, 4 * c + 1)
                    wait(dve, "relulog_ready", c + 1)
                    nc.vector.tensor_tensor(delta_sb[:, c, :, :], delta_sb[:, c, :, :], r_sb[:, :, :],
                                            ALU.subtract).then_inc(S["delta_ready"], 1)
                    c_spread(wait, 4 * c + 2)
                    c_spread(wait, 4 * c + 3)

                def drive(i):
                    _, c, ng, s = scan_tile(i)
                    if ng == 0:
                        wait(dve, "durep_ready", i // 8 + 1)
                    if i == 0:
                        wait(dve, "b_stored", NG * NC)
                    if i >= NDRV:
                        wait(dve, "state_ready", i - NDRV + 1)
                    nc.vector.tensor_tensor(drive_sb[:, i % NDRV, :], bank(DU_BANK[i // 8 % 2] + s), brep_sb[:, c, ng, :],
                                            ALU.mult).then_inc(S["drive_ready"], 1)

                def finish_y(k):
                    h, c = k // NC, k % NC
                    wait(dve, "hc_summed", 32 * h + 8 * c + 24)
                    nc.vector.scalar_tensor_tensor(out=y_sb[:, c, h, :], in0=xs_sb[:, c, h, :],
                                                   scalar=dskh_sb[:, h:h + 1], in1=bank(4 + c), op0=ALU.mult,
                                                   op1=ALU.add).then_inc(S["yskip_ready"], 1)
                    wait(dve, "yskip_ready", k + 1)
                    nc.vector.tensor_tensor(y_sb[:, c, h, :], y_sb[:, c, h, :], zs_sb[:, c, h, :],
                                            ALU.mult).then_inc(S["y_ready"], 1)

                drive(0)
                drive(1)
                for i in range(64):
                    _, c, _, _ = scan_tile(i)
                    if i + 2 < 64:
                        drive(i + 2)
                    wait(dve, "decay_ready", i + 1)
                    wait(dve, "drive_ready", i + 1)
                    if i >= NST:
                        wait(dve, "hc_ready", i - NST + 1)
                    first = 0.0
                    if c:
                        wait(dve, "state_ready", i - 7)
                        first = state_sb[:, (i - 8) % NST, CT - 1:CT]
                    nc.vector.tensor_tensor_scan(state_sb[:, i % NST, :], decay_sb[:, i % NDEC, :],
                                                 drive_sb[:, i % NDRV, :], first,
                                                 ALU.mult, ALU.add).then_inc(S["state_ready"], 1)
                    if i in (29, 37, 61):
                        finish_y((29, 37, 61).index(i))
                finish_y(3)
                for c in range(NC):
                    wait(dve, "outproj_ready", c + 1)
                    nc.vector.tensor_tensor(h1_sb[:, c * CT:(c + 1) * CT], x_sb[:, c * CT:(c + 1) * CT], bank(c),
                                            ALU.add).then_inc(S["h1_ready"], 1)
                for c in range(NC):
                    wait(dve, "rstd_ready", 2 + c + 1)
                    nc.vector.tensor_tensor(xn2_sb[:, c * CT:(c + 1) * CT], h1_sb[:, c * CT:(c + 1) * CT],
                                            rstd_sb[:, c, :], ALU.mult).then_inc(S["xn2_ready"], 1)
                for c in range(NC):
                    wait(dve, "v_ready", c + 1)
                    nc.vector.tensor_copy(vt_sb[:, 4 * c:4 * c + 4, :].rearrange("p a n -> p (a n)"),
                                          bank(4 + c, 0, 256)).then_inc(S["v_stored"], 1)

                for c in range(NC):
                    at = slice(c * CT, (c + 1) * CT)
                    wait(dve, "part1_ready", c + 1)
                    nc.vector.tensor_tensor(rest_sb[:, c, :, :], banks(2 * c, 2), part_sb[0][:, :, at],
                                            ALU.subtract).then_inc(S["rest1_ready"], 1)
                for u in range(12):
                    if stack_reader(u) == "stack_b_stored":
                        wait(dve, "stack_ready", u + 1)
                        nc.vector.tensor_copy(stack_target(u), banks(4 + 2 * (u % 2), 2, rows=slice(0, 96))
                                              ).then_inc(S["stack_b_stored"], 1)

                def max_parts(c):
                    m = negmax_sb[:, 16 * c:16 * c + 16]
                    wait(dve, "max_ready", 16 * c + 16)
                    nc.vector.tensor_copy(maxpart_sb[:, c, :, 0], m).then_inc(S["maxpart_ready"], 1)
                    wait(dve, "maxpart_ready", 2 * c + 1)
                    nc.vector.tensor_tensor(maxpart_sb[:, c, :, 1], m, maxpart_sb[:, c, :, 0],
                                            ALU.subtract).then_inc(S["maxpart_ready"], 1)
                    wait(dve, "maxrow_ready", c + 1)
                    nc.vector.tensor_copy(qstack[96:98, 0, 2:4, c * CT:(c + 1) * CT],
                                          banks(2, 2, rows=slice(96, 98))).then_inc(S["maxrow_b_stored"], 1)

                def weighted_values(c):
                    wait(dve, "rden_ready", c + 1)
                    nc.vector.tensor_tensor(attn_sb[:, c * CT:(c + 1) * CT], rden_sb[:, c, :], bank(6),
                                            ALU.mult).then_inc(S["attn_stored"], 1)

                for n in range(QT * HEADS):
                    K = (n // HEADS + 1) * 128
                    wait(dve, "scores_ready", n + 1)
                    nc.vector.tensor_reduce(negmax_sb[:, n:n + 1], ps[:, scores_bank(n) * CT:scores_bank(n) * CT + K], AX.X,
                                            ALU.max, negate=True).then_inc(S["max_ready"], 1)
                    if n % 16 == 15:
                        max_parts(n // 16)
                weighted_values(0)
                weighted_values(1)
                for c in range(NC):
                    wait(dve, "oproj_ready", c + 1)
                    nc.vector.tensor_tensor(h2_sb[:, c * CT:(c + 1) * CT], h1_sb[:, c * CT:(c + 1) * CT], bank(c),
                                            ALU.add).then_inc(S["h2_ready"], 1)
                for c in range(NC):
                    wait(dve, "rstd_ready", 4 + c + 1)
                    nc.vector.tensor_tensor(xn2_sb[:, c * CT:(c + 1) * CT], h2_sb[:, c * CT:(c + 1) * CT],
                                            rstd_sb[:, c, :], ALU.mult).then_inc(S["xn3_ready"], 1)
                for u in range(6):
                    c, m = u // 3, u % 3
                    rows = slice(0, FM[m])
                    wait(dve, "gtanh_ready", u + 1)
                    nc.vector.scalar_tensor_tensor(out=v_sb[rows, u % 4, :], in0=th_sb[rows, u % 4, :], scalar=1.0,
                                                   in1=bank(2 * (u % 2), rows=rows), op0=ALU.add,
                                                   op1=ALU.mult).then_inc(S["gsilu_ready"], 1)
                    wait(dve, "gsilu_ready", u + 1)
                    nc.vector.tensor_tensor(swi_sb[rows, c, m, :], v_sb[rows, u % 4, :],
                                            bank(2 * (u % 2) + 1, rows=rows), ALU.mult).then_inc(S["swiglu_ready"], 1)
                for c in range(NC):
                    wait(dve, "down_ready", c + 1)
                    nc.vector.tensor_tensor(s_sb[:, c, :], h2_sb[:, c * CT:(c + 1) * CT], bank(6 + c),
                                            ALU.add).then_inc(S["h3_ready"], 1)
                    wait(dve, "h3_ready", c + 1)
                    nc.vector.tensor_tensor(s_sb[:, c, :], s_sb[:, c, :], x_sb[:, c * CT:(c + 1) * CT],
                                            ALU.add).then_inc(S["sum_ready"], 1)
                for c in range(NC):
                    wait(dve, "rstd_ready", 6 + c + 1)
                    nc.vector.tensor_tensor(ln1_sb[:, c, :], rstd_sb[:, c, :], bank(4 + c),
                                            ALU.mult).then_inc(S["ln1_ready"], 1)
                for t in range(QT):
                    wait(dve, "mlpout_ready", t // 4 + 1)
                    nc.vector.bn_stats(stats_sb[:, t, :], bank(6 + t // 4, (t % 4) * 128, (t % 4) * 128 + 128)
                                       ).then_inc(S["stats_ready"], 1)
                wait(dve, "stats_ready", QT)
                nc.vector.memset(spare_sb[:, :], 0.0)
                for t in range(QT):
                    nc.vector.bn_aggr(mv_sb[:, t, :], stats_sb[:, t, :]).then_inc(S["meanvar_ready"], 1)
                wait(dve, "rstd2_ready", 1)
                wait(dve, "meanvar_ready", 8)
                dve.wait_ge(out_free, 16 * b + 16)
                for t in range(QT):
                    last = nc.vector.tensor_scalar(out_sb[:, t, :],
                                                   bank(6 + t // 4, (t % 4) * 128, (t % 4) * 128 + 128),
                                                   mv_sb[:, t, 0:1], rs2_sb[:, t:t + 1], ALU.subtract, ALU.mult)
                last.then_inc(S["out_ready"], 1)

        @block.tensor
        def _(pe):
            mm = nc.tensor.matmul

            def meansq(wait, k):
                wait(pe, "square_ready", k + 1)
                mm(bank(MEANSQ[k]), C("mean"), sq_sb[:, k % 2, :], start=True,
                   stop=True).then_inc(S["meansq_ready"], 1)

            pe.wait_ge(consts_loaded, 16)
            pe.wait_ge(out_free, 16)
            with pe.Fori(0, BATCH) as b:
                wait = turns(b)
                for c in range(NC):
                    meansq(wait, c)
                pe.wait_ge(setup_dve, N_SETUP_DVE)
                def in_proj(u):
                    c, half = u // 4, u % 2
                    wait(pe, "xn_ready", c + 1)
                    if u >= 4:
                        wait(pe, "gated_ready", u - 3)
                    if u % 4 < 2:
                        for j in range(DCONV):
                            last = mm(bank(u % 4), wconv_sb[:, j, half * 128:(half + 1) * 128],
                                      xn_sb[:, c * CT + j:c * CT + j + CT], start=(j == 0), stop=(j == DCONV - 1))
                    else:
                        last = mm(bank(u % 4), win_sb[:, DI + half * 128:DI + (half + 1) * 128],
                                  xn_sb[:, DCONV - 1 + c * CT:DCONV - 1 + (c + 1) * CT], start=True, stop=True)
                    last.then_inc(S["inproj_ready"], 1)

                def x_proj(c):
                    wait(pe, "gated_ready", 4 * c + 2)
                    for h in range(NH):
                        mm(bank(BC_BANK[c]), wbc_sb[:, h, :, :].rearrange("p a n -> p (a n)"), xs_sb[:, c, h, :],
                           start=(h == 0), stop=(h == NH - 1))
                    for h in range(NH):
                        last = mm(bank(BC_BANK[c] + 1), wdt_sb[:, h, :], xs_sb[:, c, h, :], start=(h == 0),
                                  stop=(h == NH - 1))
                    last.then_inc(S["xproj_ready"], 1)

                for u in range(6):
                    in_proj(u)
                pe.wait_ge(setup_pool, 2)
                x_proj(0)
                in_proj(6)
                in_proj(7)
                x_proj(1)
                wait(pe, "gated_ready", 8)
                for k in range(NC * NG):
                    c, g = k // NG, k % NG
                    rows = slice(32 * g, 32 * g + 32)
                    if g == 0:
                        wait(pe, "bc_ready", c + 1)
                    if k >= 2:
                        wait(pe, "b_stored", k - 1)
                    mm(bank(2 * (k % 2)), C("selB")[rows, :], bc_sb[rows, c, :], start=True,
                       stop=True).then_inc(S["brep_ready"], 1)
                    if k >= 2:
                        wait(pe, "c_stored", k - 1)
                    mm(bank(2 * (k % 2) + 1), C("selC")[rows, :], bc_sb[rows, c, :], start=True,
                       stop=True).then_inc(S["crep_ready"], 1)

                def spread(q, k, src, ready):
                    pr, c, _, _ = scan_tile(8 * q)
                    for s in range(2):
                        h, j = (2 * pr + s) // 4, (2 * pr + s) % 4
                        rows = slice(32 * j, 32 * j + 32)
                        last = mm(bank(k + s), C("selD")[rows, :], src[rows, c, h, :], start=True, stop=True)
                    last.then_inc(S[ready], 1)

                wait(pe, "b_stored", NG * NC)
                wait(pe, "c_stored", NG * NC)
                wait(pe, "delta_ready", NC)
                spread(0, 0, delta_sb, "drep_ready")
                wait(pe, "du_ready", NC)
                spread(0, DU_BANK[0], du_sb, "durep_ready")
                for i in range(64):
                    pr, c, ng, s = scan_tile(i)
                    dg = 2 * pr + s
                    h, j = dg // 4, dg % 4
                    q = i // 8 + 1
                    if i % 8 == 1 and q < 8:
                        if q > 1:
                            wait(pe, "drive_ready", 8 * (q - 1))
                        spread(q, DU_BANK[q % 2], du_sb, "durep_ready")
                    if i % 8 == 3 and q < 8:
                        wait(pe, "decay_ready", 8 * q)
                        spread(q, 0, delta_sb, "drep_ready")
                    if pr == 2 and ng == 0 and s == 0:
                        wait(pe, "yskip_ready", c + 1)
                    wait(pe, "hc_ready", i + 1)
                    mm(bank(4 + c, rows=slice(32 * j, 32 * j + 32)), C("sum"), hc_sb[:, i % NHC, :],
                       start=(ng == 0), stop=(ng == NG - 1)).then_inc(S["hc_summed"], 1)
                pe.wait_ge(setup_pool, 3)
                for c in range(NC):
                    wait(pe, "y_ready", NC + c + 1)
                    for h in range(NH):
                        last = mm(bank(c), wout_sb[:, h, :], y_sb[:, c, h, :], start=(h == 0), stop=(h == NH - 1))
                    last.then_inc(S["outproj_ready"], 1)
                for c in range(NC):
                    meansq(wait, 2 + c)
                for c in range(NC):
                    wait(pe, "xn2_ready", c + 1)
                    xn2 = xn2_sb[:, c * CT:(c + 1) * CT]
                    wait(pe, "h1_ready", 2)
                    mm(bank(2 * c), wq_sb[:, :], xn2, start=True, stop=True)
                    mm(bank(2 * c + 1), wk_sb[:, :, :].rearrange("p a n -> p (a n)"), xn2, start=True,
                       stop=True).then_inc(S["qk_ready"], 1)
                    for t in range(4):
                        last = mm(bank(4 + c, 64 * t, 64 * t + 64), xn2[:, t * 128:(t + 1) * 128], wv_sb[:, :],
                                  start=True, stop=True)
                    last.then_inc(S["v_ready"], 1)

                def scores(n):
                    i, h = n // HEADS, n % HEADS
                    K = (i + 1) * 128
                    if n == 0:
                        wait(pe, "stack_a_stored", stack_reads(2))
                        wait(pe, "stack_b_stored", 1)
                    if n == 2:
                        wait(pe, "rest1_ready", NC)
                    if n == 16:
                        wait(pe, "stack_a_stored", stack_reads(8))
                        wait(pe, "maxrow_a_stored", 1)
                        wait(pe, "maxrow_b_stored", 1)
                    elif 4 <= n < 16:
                        wait(pe, "max_ready", n - 3)
                    elif n >= 18:
                        wait(pe, "max_ready", n - 1)
                    for k0 in range(0, K, CT):
                        k1 = min(k0 + CT, K)
                        mm(bank(scores_bank(n) + k0 // CT, 0, k1 - k0), qstack[0:96, 0, h, i * 128:(i + 1) * 128],
                           kstack[0:96, 0, h // 2, k0:k1], start=True, stop=(k1 < K))
                    mm(bank(scores_bank(n) + k0 // CT, k1 - k0 - 128, k1 - k0), identb[:, :], maskb[:, :],
                       start=False, stop=True).then_inc(S["scores_ready"], 1)

                def max_rows(c):
                    wait(pe, "maxpart_ready", 2 * c + 2)
                    for h in range(HEADS):
                        for i in range(4):
                            last = mm(bank(h, i * 128, (i + 1) * 128, rows=slice(96, 98)),
                                      maxpart_sb[:, c, i * HEADS + h, :], identb[:, :], start=True, stop=True)
                    last.then_inc(S["maxrow_ready"], 1)

                def scores_t(v):
                    c, j, h, q0 = st_unit(v)
                    if v in (0, 16):
                        wait(pe, "maxrow_a_stored", c + 1)
                        wait(pe, "maxrow_b_stored", c + 1)
                        wait(pe, "stack_a_stored", stack_reads(6 * c + 5))
                    if 2 <= v < 16:
                        wait(pe, "probs_ready", v - 1)
                    elif v >= 22:
                        wait(pe, "probs_ready", v - 5)
                    elif v >= 20:
                        wait(pe, "probs_ready", 16)
                    o = bank(st_bank(v), q0, CT)
                    at = slice(c * CT + q0, (c + 1) * CT)
                    mm(o, kstack[0:98, 0, h // 2, j * 128:(j + 1) * 128], qstack[0:98, 0, h, at], start=True,
                       stop=False)
                    last = mm(o, kstack[0:96, 1, h // 2, j * 128:(j + 1) * 128], qstack[0:96, 1, h, at], start=False,
                              stop=(j < 4 * c))
                    if j >= 4 * c:
                        last = mm(bank(st_bank(v), q0, q0 + 128), maskb[:, :], identb[:, :], start=False, stop=True)
                    last.then_inc(S["scorest_ready"], 1)

                def weighted(g):
                    c, j, _, q0 = st_unit(4 * g)
                    wait(pe, "probs_ready", 4 * g + 4)
                    if g == 4:
                        wait(pe, "attn_stored", 1)
                    for k in (6, 7):
                        for h in range(HEADS):
                            kv = h // (HEADS // KV)
                            last = mm(bank(k, q0, CT, rows=slice(32 * h, 32 * h + 32)),
                                      vt_sb[:, j, kv * HD:(kv + 1) * HD] if k == 6 else C("ones")[:, 0:32],
                                      pt_sb[:, g % 2, h, q0:CT], start=(j == 0), stop=(j == 4 * c + 3))
                    last.then_inc(S["pv_ready"], 1)

                def stack(u):
                    c, m, pair = stack_unit(u)
                    which, parts = (1, K_PARTS) if pair == 0 else (0, Q_PARTS)
                    wait(pe, "part3_ready" if m else "part2_ready", c + 1)
                    if u == 0:
                        wait(pe, "v_stored", NC)
                    if u >= 2:
                        wait(pe, stack_reader(u - 2), stack_reads(u - 2))
                    for e in range(2):
                        row = 64 * e if pair == 0 else 64 * (pair - 1) + 32 * e
                        rows = slice(row, row + 32)
                        for g, n in enumerate(parts[m]):
                            last = mm(bank(4 + 2 * (u % 2) + e, rows=slice(32 * g, 32 * g + 32)), identb[:, rows],
                                      part_sb[n][:, which, c * CT:(c + 1) * CT], start=True, stop=True)
                    last.then_inc(S["stack_ready"], 1)

                for u in range(3):
                    stack(u)
                for n in range(16):
                    scores(n)
                    if 3 <= n < 12:
                        stack(n)
                max_rows(0)
                for v in range(16):
                    scores(16 + v)
                    scores_t(v)
                    if v % 4 == 3 and v > 3:
                        weighted(v // 4 - 1)
                max_rows(1)
                weighted(3)
                for g in range(4, 12):
                    for v in range(4 * g, 4 * g + 4):
                        scores_t(v)
                    if g > 4:
                        weighted(g - 1)
                weighted(11)
                for c in range(NC):
                    wait(pe, "attn_stored", c + 1)
                    mm(bank(c), W("o"), attn_sb[:, c * CT:(c + 1) * CT], start=True,
                       stop=True).then_inc(S["oproj_ready"], 1)
                for c in range(NC):
                    meansq(wait, 4 + c)
                for u in range(6):
                    c, m = u // 3, u % 3
                    rows = slice(0, FM[m])
                    wait(pe, "xn3_ready", c + 1)
                    wait(pe, "h2_ready", 2)
                    if u >= 2:
                        wait(pe, "swiglu_ready", u - 1)
                    xn3 = xn2_sb[:, c * CT:(c + 1) * CT]
                    mm(bank(2 * (u % 2), rows=rows), wgate_sb[:, m * 128:m * 128 + FM[m]], xn3, start=True, stop=True)
                    mm(bank(2 * (u % 2) + 1, rows=rows), wup_sb[:, m * 128:m * 128 + FM[m]], xn3, start=True,
                       stop=True).then_inc(S["gateup_ready"], 1)
                for c in range(NC):
                    for m in range(3):
                        wait(pe, "swiglu_ready", 3 * c + m + 1)
                        last = mm(bank(6 + c), wdown_sb[0:FM[m], m, :], swi_sb[0:FM[m], c, m, :], start=(m == 0),
                                  stop=(m == 2))
                    last.then_inc(S["down_ready"], 1)
                for c in range(NC):
                    wait(pe, "sum_ready", c + 1)
                    mm(bank(4 + c), C("center"), s_sb[:, c, :], start=True,
                       stop=True).then_inc(S["centered_ready"], 1)
                for c in range(NC):
                    meansq(wait, 6 + c)
                for u in range(8):
                    c, m = u // MM, u % MM
                    wait(pe, "ln1_ready", c + 1)
                    if u >= 4:
                        wait(pe, "gelu_ready", u - 3)
                    mm(bank(u % 4), W("w1", m * 128, (m + 1) * 128), ln1_sb[:, c, :], start=True,
                       stop=True).then_inc(S["mlp_ready"], 1)
                for c in range(NC):
                    wait(pe, "gelu_ready", MM * (c + 1))
                    for t in range(4):
                        o = bank(6 + c, t * 128, (t + 1) * 128)
                        mm(o, ln1_sb[:, c, t * 128:(t + 1) * 128], C("ident"), start=True, stop=False)
                        mm(o, C("ones")[0:1, :], b2_sb[:, :], start=False, stop=False)
                        for m in range(MM):
                            last = mm(o, gelu_sb[:, c, m, t * 128:(t + 1) * 128], W("w2", m * 128, (m + 1) * 128),
                                      start=False, stop=(m == MM - 1))
                    last.then_inc(S["mlpout_ready"], 1)


def scan_tile(i):
    return i // 16, (i // 8) % 2, (i // 2) % 4, i % 2


def stack_unit(u):
    return u // 6, u // 3 % 2, u % 3


def stack_reader(u):
    return "stack_b_stored" if u == 1 else "stack_a_stored"


def stack_reads(u):
    return sum(stack_reader(v) == stack_reader(u) for v in range(u + 1))


def scores_bank(n):
    return n % 4 if n < 16 else 2 * (n % 2)


def st_bank(v):
    return 4 + v % 2 if v < 16 else (v - 16) % 6


def st_unit(v):
    c, g = (0, v // 4) if v < 16 else (1, v // 4 - 4)
    return c, g, v % 4, max(0, (g - 4 * c) * 128)


def kernel(**inputs):
    import numpy as np
    import concourse.bacc as bacc
    from concourse.bass_utils import run_bass_kernel_spmd

    f = {k.replace("L0_", ""): np.asarray(v) for k, v in inputs.items()}

    def halves(a, n):
        return a.reshape(n, 128, -1).transpose(1, 0, 2).reshape(128, -1)

    down = np.zeros((384, D), np.float32)
    down[:FFN] = f["attn_down_w"].T
    alog = f["attn_A_log"].reshape(DG, DS, NG, NS).transpose(3, 1, 0, 2).reshape(128, DG * NG)
    parts = {
        "in": f["attn_in_proj_w"].T, "xp": halves(f["attn_x_proj_w"].T, 2), "out": halves(f["attn_out_proj_w"].T, 2),
        "q": f["attn_q_w"].T, "k": f["attn_k_w"].T, "v": f["attn_v_w"].T, "o": f["attn_o_w"].T,
        "gate": f["attn_gate_w"].T, "up": f["attn_up_w"].T, "down": halves(down, 3),
        "w1": f["ffn_w1"], "w2": halves(f["ffn_w2"], 4),
        "nm": f["attn_norm_m_w"][:, None], "na": f["attn_norm_attn_w"][:, None], "nf": f["attn_norm_ffn_w"][:, None],
        "cb": f["attn_conv_b"].reshape(2, 128).T, "dtw": f["attn_dt_w"].reshape(2, 128).T,
        "dtb": f["attn_dt_b"].reshape(2, 128).T, "dsk": f["attn_D_skip"].reshape(2, 128).T,
        "b1": f["ffn_b1"].reshape(4, 128).T, "alog": alog,
    }
    wts = np.ascontiguousarray(np.concatenate([parts[k] for k in W_COLS], axis=1))
    p, q = np.arange(128)[:, None], np.arange(128)[None, :]
    eye = (p == q).astype(np.float32)
    consts = {
        "ident": eye, "center": eye - np.float32(1 / 128), "mean": np.full((128, 128), 1 / 128, np.float32),
        "selD": (p % 32 == q % 32).astype(np.float32),
        "selB": (p % 32 == 4 * (p // 32) + q // 32) * np.float32(0.5),
        "selC": (p % 32 == 16 + 4 * (p // 32) + q // 32).astype(np.float32),
        "sum": (p % 32 == np.arange(32)[None, :]).astype(np.float32),
        "mask": np.where(q > p, np.float32(-1e30), np.float32(0)),
        "ones": np.ones((128, 128), np.float32),
    }
    cst = np.ascontiguousarray(np.concatenate([consts[k] for k in C_COLS], axis=1).astype(np.float32))
    arrays = {
        "x": np.ascontiguousarray(f["attn_x"].reshape(BATCH * SEQ, D).T), "wts": wts, "cst": cst,
        "convw": np.ascontiguousarray(f["attn_conv_w"][:, 0, :].T.reshape(1, -1)), "b2": f["ffn_b2"].reshape(1, D),
    }
    nc = bacc.Bacc("TRN2", target_bir_lowering=False, num_devices=1)
    args = [nc.dram_tensor(n, a.shape, mybir.dt.float32, kind="ExternalInput").ap() for n, a in arrays.items()]
    out = nc.dram_tensor("out", (128, BATCH * QT, D), mybir.dt.float32, kind="ExternalOutput").ap()
    build(nc, *args, out)
    r = run_bass_kernel_spmd(nc, [arrays], core_ids=[0])
    return np.ascontiguousarray(r.results[0]["out"].transpose(1, 0, 2)).reshape(BATCH, SEQ, D)
```

```python
import concourse.bass as bass
from concourse import mybir
from contextlib import ExitStack

BATCH, SEQ, D = 2, 1024, 128
DI, NSTATE, DCONV = 256, 16, 4
HEADS, KV, HD = 4, 2, 32
FFN, MLP = 341, 512
CT = 512
NC = SEQ // CT
NH = DI // 128
NS, DS = 4, 32
NG, DG = NSTATE // NS, DI // DS
QT = SEQ // 128
FM = [128, 128, FFN - 256]
MM = MLP // 128
EPS_RMS, EPS_LN = 1e-6, 1e-5

W_COLS = {"in": 512, "xp": 2 * 33, "nm": 1, "na": 1, "nf": 1, "cb": 2, "dtw": 2, "dtb": 2, "dsk": 2,
          "b1": 4, "alog": 32, "out": 256, "q": 128, "k": 64, "v": 64, "o": 128, "gate": FFN,
          "up": FFN, "down": 384, "w1": 512, "w2": 512}
C_COLS = {"ident": 128, "center": 128, "mean": 128, "selD": 4 * 128, "sum": 32, "mask": 128, "ones": 128,
          "less1": 1, "less2": 1}


def offsets(cols):
    at, out = 0, {}
    for name, n in cols.items():
        out[name] = (at, n)
        at += n
    return out, at


W_AT, W_ALL = offsets(W_COLS)
C_AT, C_ALL = offsets(C_COLS)
W_FIRST = W_AT["out"][0]

SIGNALS = {
    "a_ready": 1, "nega_ready": 1, "square_ready": 8, "meansq_ready": 8, "log_ready": 8, "rstd_ready": 8, "xn_ready": 2,
    "inproj_ready": 8, "tanh_ready": 8, "gated_ready": 8,
    "dtraw_ready": 2, "bcraw_ready": 2, "bc1_ready": 2, "bcrest_ready": 2, "bc2_ready": 2, "bcparts_ready": 2,
    "dtpre_ready": 4, "abs_ready": 2, "expabs_ready": 2, "log1p_ready": 2,
    "u_ready": 2, "resid_ready": 2, "relulog_ready": 2, "delta_ready": 2, "du0_ready": 1, "du1_ready": 1,
    "brep_ready": 4, "crep_ready": 4, "brep_stored": 4, "crep0_stored": 2, "crep1_stored": 2,
    "drep_ready": 8, "durep_ready": 8, "decay_ready": 64, "drive_ready": 32, "state_ready": 64,
    "hc_ready": 32, "hc_summed": 64, "yskip_ready": 4, "y_ready": 4,
    "outproj_ready": 2, "h1_ready": 2, "xn2_ready": 2, "qk_ready": 2, "v_ready": 1, "v_stored": 1,
    "part1_ready": 2, "rest1_ready": 2, "part2_ready": 2, "part3_ready": 2,
    "stack_ready": 12, "stack_a_stored": 9, "stack_b_stored": 3,
    "scores_ready": 34,
    "max_ready": 32, "maxpart_ready": 4, "maxrow_a_stored": 2,
    "maxrow_b_stored": 2, "scorest_ready": 48, "probs_ready": 48, "pv_ready": 12, "probsum_ready": 8, "den_ready": 1, "logden_ready": 2,
    "rden_ready": 2, "attn_stored": 2,
    "oproj_ready": 2, "h2_ready": 2, "xn3_ready": 2,
    "gateup_ready": 6, "gtanh_ready": 6, "gsilu_ready": 6, "swiglu_ready": 6,
    "down_ready": 2, "h3_ready": 2, "sum_ready": 2, "centered_ready": 2, "ln1_ready": 2, "ln1bias_ready": 2,
    "mlp_ready": 8, "gelu_ready": 8, "mlpout_ready": 2, "stats_ready": 8, "meanvar_ready": 8,
    "logvar_ready": 1, "rstd2_ready": 1, "out_ready": 1,
}


def build(nc, x, wts, cst, convw, b2, out):
    fp32, bf16 = mybir.dt.float32, mybir.dt.bfloat16
    ALU, ACT, AX = mybir.AluOpType, mybir.ActivationFunctionType, mybir.AxisListType
    LN_EXP = "natural_log_exp_and_others"

    ctx = ExitStack()
    with ctx:
        def sb(name, shape, dt=fp32):
            return ctx.enter_context(nc.sbuf_tensor(name, shape, dt))

        def sem(name):
            return ctx.enter_context(nc.semaphore(name))

        w_sb = sb("w_sb", [128, W_ALL])
        c_sb = sb("c_sb", [128, C_ALL])

        def W(name, a=0, b=None):
            at, n = W_AT[name]
            return w_sb[:, at + a:at + (n if b is None else b)]

        def C(name):
            at, n = C_AT[name]
            return c_sb[:, at:at + n]

        b2_sb = sb("b2_sb", [D, 1])
        win_sb = sb("win_sb", [128, 2 * DI])
        wconv_sb = sb("wconv_sb", [128, DCONV, DI])
        wbc_sb = sb("wbc_sb", [128, NH, 3, 32])
        wdt_sb = sb("wdt_sb", [128, NH, 128])
        wout_sb = sb("wout_sb", [128, NH, D])
        wq_sb = sb("wq_sb", [128, D])
        wk_sb = sb("wk_sb", [128, HEADS, HD])
        wv_sb = sb("wv_sb", [128, KV * HD])
        wgate_sb = sb("wgate_sb", [128, FFN])
        wup_sb = sb("wup_sb", [128, FFN])
        wdown_sb = sb("wdown_sb", [128, 3, D])
        a_sb = sb("a_sb", [128, DG * NG])
        nega_sb = sb("nega_sb", [128, DG * NG])
        cbh_sb = sb("cbh_sb", [128, NH])
        dskh_sb = sb("dskh_sb", [128, NH])
        identb = sb("identb", [128, 128], bf16)
        maskb = sb("maskb", [128, 128], bf16)
        eps_sb = sb("eps_sb", [128, 2])

        x_sb = sb("x_sb", [128, SEQ])
        rstd_sb = sb("rstd_sb", [128, NC, CT])
        xn_sb = sb("xn_sb", [128, DCONV - 1 + SEQ])
        xs_sb = sb("xs_sb", [128, NC, NH, CT])
        zs_sb = sb("zs_sb", [128, NC, NH, CT])
        bc_sb = sb("bc_sb", [128, NC, CT], bf16)
        selbc_sb = sb("selbc_sb", [128, 32, 32], bf16)
        dt_sb = sb("dt_sb", [128, NC, NH, CT])
        e_sb = sb("e_sb", [128, NC, NH, CT])
        l_sb = sb("l_sb", [128, NC, NH, CT])
        delta_sb = sb("delta_sb", [128, NC, NH, CT])
        du_sb = sb("du_sb", [128, NC, NH, CT])
        brep_sb = sb("brep_sb", [128, NC, NG, CT])
        crep_sb = sb("crep_sb", [128, NC, NG, CT])
        NDEC, NDRV, NST, NHC = 6, 4, 12, 4
        decay_sb = sb("decay_sb", [128, NDEC, CT])
        drive_sb = sb("drive_sb", [128, NDRV, CT])
        state_sb = sb("state_sb", [128, NST, CT])
        hc_sb = sb("hc_sb", [128, NHC, CT])
        y_sb = dt_sb
        convw_sb = decay_sb[:, 0:2, :].rearrange("p a t -> p (a t)").rearrange("p (j d) -> p j d", j=DCONV)
        v_sb, th_sb = drive_sb, state_sb[:, 0:4, :]
        u_sb = du_sb
        hc_b = hc_sb[:, :, :].rearrange("p a t -> p (a t)").bitcast(bf16).rearrange("p (a t) -> p a t", t=CT)
        bc1_sb, bc2_sb = hc_b[:, 0:2, :], hc_b[:, 2:4, :]
        bcrest_sb = hc_sb[:, 2:4, :]
        out_sb = decay_sb[:, 2:4, :].rearrange("p a t -> p (a t)").rearrange("p (t d) -> p t d", t=QT)
        h1_sb = zs_sb[:, 0, :, :].rearrange("p a t -> p (a t)")
        xn2_sb = e_sb[:, 0, :, :].rearrange("p a t -> p (a t)")
        attn_sb = l_sb[:, 1, :, :].rearrange("p a t -> p (a t)")
        vt_sb = sb("vt_sb", [128, QT, KV * HD])
        crep_b = crep_sb[:, :, :, :].rearrange("p c g t -> p (c g t)").bitcast(bf16)
        part_sb = [crep_b[:, 2 * SEQ * n:2 * SEQ * (n + 1)].rearrange("p (w t) -> p w t", w=2) for n in range(3)]
        rest_sb = drive_sb[:, :, :].rearrange("p (c w) t -> p c w t", c=NC)
        state_b = state_sb[:, :, :].rearrange("p a t -> p (a t)").bitcast(bf16)
        qstack = state_b[:, 0:2 * HEADS * SEQ].rearrange("p (m h t) -> p m h t", m=2, h=HEADS)
        kstack = sb("kstack", [128, 2, KV, SEQ], bf16)
        Q_PARTS = [(0, 0, 1), (1, 0, 2)]
        K_PARTS = [(0, 1, 0), (1, 2, 0)]
        sq_sb = sb("sq_sb", [128, 2, CT])
        log_sb = sb("log_sb", [128, 2, CT])
        pt_sb = brep_sb[:, :, :, :]
        probsum_sb = decay_sb[:, 0:4, :]
        negmax_sb = sb("negmax_sb", [128, QT * HEADS])
        maxpart_sb = sb("maxpart_sb", [128, NC, 16, 2], bf16)
        rden_sb = rstd_sb
        h2_sb = du_sb[:, 0, :, :].rearrange("p a t -> p (a t)")
        swi_sb = brep_sb[:, :, 0:3, :]
        s_sb = delta_sb[:, 0, :, :]
        ln1_sb = delta_sb[:, 1, :, :]
        gelu_sb = crep_sb
        stats_sb = sb("stats_sb", [128, QT, 6])
        mv_sb = sb("mv_sb", [128, QT, 2])
        lv_sb = sb("lv_sb", [128, QT])
        spare_sb = sb("spare_sb", [128, 1])
        rs2_sb = sb("rs2_sb", [128, QT])

        ps = ctx.enter_context(nc.psum_tensor("ps", [128, 8 * CT], fp32))

        def bank(k, a=0, b=CT, rows=slice(0, 128)):
            return ps[rows, k * CT + a:k * CT + b]

        DU_BANK = [2, 6]
        XPROJ_BANK = [4, 6]
        B_BANK, C_BANK = [2, 0, 6, 6], [4, 4, 6, 6]
        IN_BANK = [0, 1, 2, 3, 2, 5, 5, 5]
        def banks(k, n, rows=slice(0, 128)):
            return ps[rows, k * CT:(k + n) * CT].rearrange("p (w t) -> p w t", w=n)

        ROW_BANK = [4, 0]
        MEANSQ = [4, 5, 4, 2, 6, 7, 6, 7, 4, 5]

        loaded = sem("loaded")
        rest_loaded = sem("rest_loaded")
        consts_loaded = sem("consts_loaded")
        x_loaded = sem("x_loaded")
        out_free = sem("out_free")
        setup_dve = sem("setup_dve")
        setup_pool = sem("setup_pool")
        S = {name: sem(name) for name in SIGNALS}

        def twice(tile):
            return tile.rearrange("p (w t) -> p w t", w=1).to_broadcast([128, 2, CT])

        def turns(b):
            return lambda name, k: b * SIGNALS[name] + k

        def stack_target(u):
            c, m, pair = stack_unit(u)
            at = slice(c * CT, (c + 1) * CT)
            return kstack[0:96, m, :, at] if pair == 0 else qstack[0:96, m, 2 * pair - 2:2 * pair, at]

        block = ctx.enter_context(nc.Block())
        N_SETUP_DVE = 3

        @block.sync
        def _(sp):
            sp.dma_start(x_sb[:, :], x[:, 0:SEQ]).then_inc(x_loaded, 16)
            sp.dma_start(c_sb[:, :], cst).then_inc(consts_loaded, 16)
            sp.dma_start(w_sb[:, 0:W_FIRST], wts[:, 0:W_FIRST]).then_inc(loaded, 16)
            sp.dma_start(convw_sb[:, :, :].rearrange("p j d -> p (j d)"),
                         convw.to_broadcast([128, DCONV * DI])).then_inc(loaded, 16)
            sp.dma_start(b2_sb[:, :], b2).then_inc(out_free, 16)
            sp.dma_start(w_sb[:, W_FIRST:], wts[:, W_FIRST:]).then_inc(rest_loaded, 16)
            for b in range(BATCH):
                n = (b + 1) % BATCH
                sp.wait_ge(S["sum_ready"], NC * (b + 1))
                sp.dma_start(x_sb[:, :], x[:, n * SEQ:(n + 1) * SEQ]).then_inc(x_loaded, 16)
                sp.wait_ge(S["out_ready"], b + 1)
                sp.dma_start(out[:, b * QT:(b + 1) * QT, :], out_sb[:, :, :]).then_inc(out_free, 16)
            sp.wait_ge(out_free, 16 + 16 * BATCH)

        @block.gpsimd
        def _(pool):
            nc.gpsimd.memset(xn_sb[:, 0:DCONV - 1], 0.0)
            nc.gpsimd.memset(eps_sb[:, 0:1], EPS_RMS)
            nc.gpsimd.memset(eps_sb[:, 1:2], EPS_LN).then_inc(setup_pool, 1)
            pool.wait_ge(loaded, 32)
            nc.gpsimd.tensor_scalar(wbc_sb[:, :, :, :],
                                    W("xp").rearrange("p (h n) -> p h n", h=NH)[:, :, 0:32]
                                    .rearrange("p h (a n) -> p h a n", a=1).to_broadcast([128, NH, 3, 32]),
                                    0.5, 1.0, ALU.mult, ALU.mult)
            for h in range(NH):
                nc.gpsimd.tensor_scalar(wdt_sb[:, h, :], W("xp", 33 * h + 32, 33 * h + 33).to_broadcast([128, 128]),
                                        0.5, 1.0, ALU.mult, ALU.mult)
            nc.gpsimd.tensor_scalar(dskh_sb[:, :], W("dsk"), 0.5, 1.0, ALU.mult, ALU.mult)
            pool.wait_ge(consts_loaded, 16)
            for n, scale in ((0, 0.5), (1, 1.0)):
                last = nc.gpsimd.tensor_scalar(selbc_sb[:, 16 * n:16 * n + 16, :],
                                               C("sum")[:, 16 * n:16 * n + 16].rearrange("p (n a) -> p n a", a=1)
                                               .to_broadcast([128, 16, 32]), scale, 1.0, ALU.mult, ALU.mult)
            last.then_inc(setup_pool, 1)
            pool.wait_ge(rest_loaded, 16)
            pool.wait_ge(consts_loaded, 16)
            nc.gpsimd.tensor_scalar(wout_sb[:, :, :].rearrange("p h n -> p (h n)"), W("out"), 0.5, 1.0, ALU.mult,
                                    ALU.mult)
            nc.gpsimd.tensor_scalar(wq_sb[:, :], W("q"), W("na"), float(HD) ** -0.5, ALU.mult, ALU.mult)
            nc.gpsimd.tensor_scalar(wk_sb[:, :, :].rearrange("p (k r) d -> p k r d", k=KV),
                                    W("k").rearrange("p (k a d) -> p k a d", k=KV, a=1)
                                    .to_broadcast([128, KV, HEADS // KV, HD]), W("na"), 1.0, ALU.mult, ALU.mult)
            nc.gpsimd.tensor_scalar(wv_sb[:, :], W("v"), W("na"), 1.0, ALU.mult, ALU.mult)
            nc.gpsimd.tensor_scalar(wgate_sb[:, :], W("gate"), W("nf"), 1.0, ALU.mult, ALU.mult)
            nc.gpsimd.tensor_scalar(wup_sb[:, :], W("up"), W("nf"), 1.0, ALU.mult, ALU.mult)
            nc.gpsimd.tensor_scalar(wdown_sb[:, :, :].rearrange("p h n -> p (h n)"), W("down"), 0.5, 1.0, ALU.mult,
                                    ALU.mult)
            nc.gpsimd.tensor_copy(identb[:, :], C("ident"))
            nc.gpsimd.tensor_copy(maskb[:, :], C("mask")).then_inc(setup_pool, 1)
            with pool.Fori(0, BATCH) as b:
                count = turns(b)
                pool.wait_ge(S["delta_ready"], count("delta_ready", 2))
                nc.gpsimd.tensor_tensor(du_sb[:, 1, :, :], delta_sb[:, 1, :, :], xs_sb[:, 1, :, :],
                                        ALU.mult).then_inc(S["du1_ready"], 1)
                for k in range(32):
                    _, c, ng, _ = scan_tile(2 * k)
                    pool.wait_ge(S["state_ready"], count("state_ready", 2 * k + 2))
                    if k in (0, 2):
                        pool.wait_ge(S["crep0_stored"], count("crep0_stored", 1 + k // 2))
                    if k == 4:
                        pool.wait_ge(S["crep1_stored"], count("crep1_stored", 2))
                    if k >= 2:
                        pool.wait_ge(S["hc_summed"], count("hc_summed", 2 * k - 2))
                    st, slot = 2 * k % NST, 2 * k % NHC
                    nc.gpsimd.tensor_tensor(hc_sb[:, slot:slot + 2, :], state_sb[:, st:st + 2, :],
                                            twice(crep_sb[:, c, ng, :]), ALU.mult).then_inc(S["hc_ready"], 1)
                for c in range(NC):
                    at = slice(c * CT, (c + 1) * CT)
                    pool.wait_ge(S["part2_ready"], count("part2_ready", c + 1))
                    nc.gpsimd.tensor_tensor(part_sb[2][:, :, at], rest_sb[:, c, :, :], part_sb[1][:, :, at],
                                            ALU.subtract).then_inc(S["part3_ready"], 1)
                for c in range(NC):
                    pool.wait_ge(S["ln1_ready"], count("ln1_ready", c + 1))
                    nc.gpsimd.tensor_tensor(s_sb[:, c, :], ln1_sb[:, c, :], b2_sb[:, :].to_broadcast([128, CT]),
                                            ALU.add).then_inc(S["ln1bias_ready"], 1)

        @block.scalar
        def _(act):
            act.wait_ge(setup_pool, 1)

            def squares(src, k):
                nc.scalar.activation(sq_sb[:, k % 2, :], src, ACT.Square).then_inc(S["square_ready"], 1)

            def rstd(count, k, eps):
                act.wait_ge(S["meansq_ready"], count("meansq_ready", k + 1))
                nc.scalar.activation(log_sb[:, k % 2, :], bank(MEANSQ[k]), ACT.Ln,
                                     bias=eps_sb[:, eps:eps + 1]).then_inc(S["log_ready"], 1)
                act.wait_ge(S["log_ready"], count("log_ready", k + 1))
                nc.scalar.activation(rstd_sb[:, k % 2, :], log_sb[:, k % 2, :], ACT.Exp,
                                     scale=-0.5).then_inc(S["rstd_ready"], 1)

            def first_squares(x_loads, k):
                act.wait_ge(x_loaded, x_loads)
                for c in range(NC):
                    squares(x_sb[:, c * CT:(c + 1) * CT], k + c)

            act.preload_act_table_set(LN_EXP)
            first_squares(16, 0)
            for c in range(NC):
                rstd(turns(0), c, 0)
            with act.Fori(0, BATCH) as b:
                count = turns(b)
                act.wait_ge(loaded, 32)
                nc.scalar.activation(a_sb[:, :], W("alog"), ACT.Exp).then_inc(S["a_ready"], 1)
                act.preload_act_table_set("exp_and_others")
                act.wait_ge(setup_dve, N_SETUP_DVE)
                def tanh_x(u):
                    act.wait_ge(S["inproj_ready"], count("inproj_ready", u + 1))
                    half = u % 2
                    nc.scalar.activation(v_sb[:, u, :], bank(IN_BANK[u]), ACT.Identity, bias=W("cb", half, half + 1))
                    nc.scalar.activation(th_sb[:, u, :], bank(IN_BANK[u]), ACT.Tanh, scale=0.5,
                                         bias=cbh_sb[:, half:half + 1]).then_inc(S["tanh_ready"], 1)

                def tanh_z(u):
                    act.wait_ge(S["inproj_ready"], count("inproj_ready", u + 1))
                    nc.scalar.activation(zs_sb[:, u // 2 - 2, u % 2, :], bank(IN_BANK[u]), ACT.Tanh,
                                         scale=0.5).then_inc(S["tanh_ready"], 1)

                def bc_part1(c):
                    act.wait_ge(S["bcraw_ready"], count("bcraw_ready", c + 1))
                    nc.scalar.activation(bc1_sb[0:96, c, :], bank(XPROJ_BANK[c], rows=slice(0, 96)),
                                         ACT.Copy).then_inc(S["bc1_ready"], 1)

                def bc_part2(c):
                    act.wait_ge(S["bcrest_ready"], count("bcrest_ready", c + 1))
                    nc.scalar.activation(bc2_sb[0:96, c, :], bcrest_sb[0:96, c, :],
                                         ACT.Copy).then_inc(S["bc2_ready"], 1)

                def abs_exp(c, between):
                    act.wait_ge(S["dtpre_ready"], count("dtpre_ready", 2 * c + 2))
                    nc.scalar.activation(l_sb[:, c, :, :], dt_sb[:, c, :, :], ACT.Abs).then_inc(S["abs_ready"], 1)
                    between(c)
                    act.wait_ge(S["abs_ready"], count("abs_ready", c + 1))
                    nc.scalar.activation(e_sb[:, c, :, :], l_sb[:, c, :, :], ACT.Exp,
                                         scale=-1.0).then_inc(S["expabs_ready"], 1)

                def log1p(c):
                    act.wait_ge(S["expabs_ready"], count("expabs_ready", c + 1))
                    nc.scalar.activation(l_sb[:, c, :, :], e_sb[:, c, :, :], ACT.Ln,
                                         bias=C("ones")[:, 0:1]).then_inc(S["log1p_ready"], 1)

                def store_b(k):
                    c, g = k // 2, 2 * (k % 2)
                    act.wait_ge(S["brep_ready"], count("brep_ready", k + 1))
                    nc.scalar.activation(brep_sb[:, c, g:g + 2, :], banks(B_BANK[k], 2),
                                         ACT.Copy).then_inc(S["brep_stored"], 1)

                def store_c1(k):
                    act.wait_ge(S["crep_ready"], count("crep_ready", k + 1))
                    nc.scalar.activation(crep_sb[:, 1, 2 * (k % 2):2 * (k % 2) + 2, :], banks(C_BANK[k], 2),
                                         ACT.Copy).then_inc(S["crep1_stored"], 1)

                for u in range(3):
                    tanh_x(u)
                act.wait_ge(consts_loaded, 16)
                abs_exp(0, bc_part1)
                bc_part2(0)
                tanh_x(3)
                tanh_z(4)
                act.preload_act_table_set(LN_EXP)
                log1p(0)
                store_b(0)
                store_b(1)
                abs_exp(1, bc_part1)
                bc_part2(1)
                log1p(1)
                act.preload_act_table_set("exp_and_others")
                act.wait_ge(out_free, 16 * b + 16)
                act.wait_ge(S["nega_ready"], count("nega_ready", 1))
                for i in range(64):
                    pr, c, ng, s = scan_tile(i)
                    if ng == 0:
                        act.wait_ge(S["drep_ready"], count("drep_ready", i // 8 + 1))
                    if i >= NDEC:
                        act.wait_ge(S["state_ready"], count("state_ready", i - NDEC + 1))
                    col = (2 * pr + s) * NG + ng
                    nc.scalar.activation(decay_sb[:, i % NDEC, :], bank(s), ACT.Exp,
                                         scale=nega_sb[:, col:col + 1]).then_inc(S["decay_ready"], 1)
                    if i == 1:
                        store_b(2)
                        tanh_z(5)
                    if i == 3:
                        store_c1(2)
                        store_b(3)
                    if i == 5:
                        store_c1(3)
                    if i == 9:
                        tanh_z(6)
                    if i == 16:
                        tanh_z(7)
                        act.preload_act_table_set(LN_EXP)
                def part1(c):
                    act.wait_ge(S["qk_ready"], count("qk_ready", c + 1))
                    nc.scalar.activation(part_sb[0][:, :, c * CT:(c + 1) * CT], banks(2 * c, 2),
                                         ACT.Copy).then_inc(S["part1_ready"], 1)

                def part2(c):
                    act.wait_ge(S["rest1_ready"], count("rest1_ready", c + 1))
                    nc.scalar.activation(part_sb[1][:, :, c * CT:(c + 1) * CT], rest_sb[:, c, :, :],
                                         ACT.Copy).then_inc(S["part2_ready"], 1)

                def store_stack(u):
                    act.wait_ge(S["stack_ready"], count("stack_ready", u + 1))
                    nc.scalar.activation(stack_target(u), banks(4 + 2 * (u % 2), 2, rows=slice(0, 96)),
                                         ACT.Copy).then_inc(S["stack_a_stored"], 1)

                act.wait_ge(S["h1_ready"], count("h1_ready", 1))
                squares(h1_sb[:, 0:CT], 2)
                rstd(count, 2, 0)
                part1(0)
                part2(0)
                act.wait_ge(S["h1_ready"], count("h1_ready", 2))
                squares(h1_sb[:, CT:], 3)
                store_stack(0)
                rstd(count, 3, 0)
                store_stack(2)
                part1(1)
                store_stack(3)
                part2(1)
                for u in (5, 6, 8, 9, 10, 11):
                    store_stack(u)

                def max_rows(c):
                    act.wait_ge(S["scores_ready"], count("scores_ready", 19 + 15 * c))
                    nc.scalar.activation(qstack[96:98, 0, 0:2, c * CT:(c + 1) * CT],
                                         banks(ROW_BANK[c], 2, rows=slice(96, 98)), ACT.Copy).then_inc(S["maxrow_a_stored"], 1)

                def exponential(v):
                    c, j, h, q0 = st_unit(v)
                    act.wait_ge(S["scorest_ready"], count("scorest_ready", v + 1))
                    if v >= 8:
                        act.wait_ge(S["pv_ready"], count("pv_ready", v // 4 - 1))
                    if v >= 24:
                        act.wait_ge(S["probsum_ready"], count("probsum_ready", v // 4 - 5))
                    nc.scalar.activation(pt_sb[:, v // 4 % 2, h, q0:CT], bank(st_bank(v), q0, CT),
                                         ACT.Exp).then_inc(S["probs_ready"], 1)

                def inverse_sum(c):
                    if c == 0:
                        act.wait_ge(S["pv_ready"], count("pv_ready", 4))
                    else:
                        act.wait_ge(S["den_ready"], count("den_ready", 1))
                    nc.scalar.activation(log_sb[:, c, :], bank(7), ACT.Ln).then_inc(S["logden_ready"], 1)
                    act.wait_ge(S["logden_ready"], count("logden_ready", c + 1))
                    nc.scalar.activation(rden_sb[:, c, :], log_sb[:, c, :], ACT.Exp,
                                         scale=-1.0).then_inc(S["rden_ready"], 1)

                max_rows(0)
                for v in range(16):
                    exponential(v)
                max_rows(1)
                inverse_sum(0)
                for v in range(16, 48):
                    exponential(v)
                inverse_sum(1)
                for c in range(NC):
                    act.wait_ge(S["h2_ready"], count("h2_ready", c + 1))
                    squares(h2_sb[:, c * CT:(c + 1) * CT], 4 + c)
                    rstd(count, 4 + c, 0)
                act.preload_act_table_set("exp_and_others")
                for u in range(6):
                    rows = slice(0, FM[u % 3])
                    act.wait_ge(S["gateup_ready"], count("gateup_ready", u + 1))
                    if u >= 4:
                        act.wait_ge(S["gsilu_ready"], count("gsilu_ready", u - 3))
                    nc.scalar.activation(th_sb[rows, u % 4, :], bank(2 * (u % 2), rows=rows), ACT.Tanh,
                                         scale=0.5).then_inc(S["gtanh_ready"], 1)
                act.preload_act_table_set(LN_EXP)
                for c in range(NC):
                    act.wait_ge(S["centered_ready"], count("centered_ready", c + 1))
                    squares(bank(4 + c), 6 + c)
                for c in range(NC):
                    rstd(count, 6 + c, 1)
                for u in range(8):
                    m = u % MM
                    if u == 4:
                        first_squares(16 * b + 32, 8)
                    act.wait_ge(S["mlp_ready"], count("mlp_ready", u + 1))
                    nc.scalar.activation(gelu_sb[:, u // MM, m, :], bank(u % 4), ACT.Gelu,
                                         bias=W("b1", m, m + 1)).then_inc(S["gelu_ready"], 1)
                act.preload_act_table_set(LN_EXP)
                for c in range(NC):
                    rstd(count, 8 + c, 0)
                act.wait_ge(S["meanvar_ready"], count("meanvar_ready", 8))
                nc.scalar.activation(lv_sb[:, :], mv_sb[:, :, 1], ACT.Ln,
                                     bias=eps_sb[:, 1:2]).then_inc(S["logvar_ready"], 1)
                act.wait_ge(S["logvar_ready"], count("logvar_ready", 1))
                nc.scalar.activation(rs2_sb[:, :], lv_sb[:, :], ACT.Exp,
                                     scale=-0.5).then_inc(S["rstd2_ready"], 1)

        @block.vector
        def _(dve):
            nc.vector.memset(kstack[96:98, 0, :, :], 1.0)
            dve.wait_ge(loaded, 32)
            nc.vector.tensor_scalar(win_sb[:, :], W("in"), W("nm"), None, ALU.mult).then_inc(setup_dve, 1)
            nc.vector.tensor_scalar(cbh_sb[:, :], W("cb"), 0.5, None, ALU.mult).then_inc(setup_dve, 1)
            dve.wait_ge(setup_dve, 2)
            for j in range(DCONV):
                last = nc.vector.tensor_tensor(wconv_sb[:, j, :], win_sb[:, 0:DI], convw_sb[:, j, :], ALU.mult)
            last.then_inc(setup_dve, 1)
            assert N_SETUP_DVE == 3

            def first_norm(count, x_loads, k):
                dve.wait_ge(x_loaded, x_loads)
                for c in range(NC):
                    dve.wait_ge(S["rstd_ready"], count("rstd_ready", k + c + 1))
                    nc.vector.tensor_tensor(xn_sb[:, DCONV - 1 + c * CT:DCONV - 1 + (c + 1) * CT],
                                            x_sb[:, c * CT:(c + 1) * CT], rstd_sb[:, c, :],
                                            ALU.mult).then_inc(S["xn_ready"], 1)

            first_norm(turns(0), 16, 0)
            with dve.Fori(0, BATCH) as b:
                count = turns(b)
                dve.wait_ge(setup_pool, 2)
                def gate_x(u):
                    dve.wait_ge(S["tanh_ready"], count("tanh_ready", u + 1))
                    nc.vector.scalar_tensor_tensor(out=xs_sb[:, u // 2, u % 2, :], in0=th_sb[:, u, :], scalar=1.0,
                                                   in1=v_sb[:, u, :], op0=ALU.add,
                                                   op1=ALU.mult).then_inc(S["gated_ready"], 1)

                def gate_z(u):
                    dve.wait_ge(S["tanh_ready"], count("tanh_ready", u + 1))
                    zs = zs_sb[:, u // 2 - 2, u % 2, :]
                    nc.vector.scalar_tensor_tensor(out=zs, in0=zs, scalar=1.0, in1=bank(IN_BANK[u]), op0=ALU.add,
                                                   op1=ALU.mult).then_inc(S["gated_ready"], 1)

                def dt(c):
                    dve.wait_ge(S["dtraw_ready"], count("dtraw_ready", c + 1))
                    for h in range(NH):
                        nc.vector.tensor_scalar(dt_sb[:, c, h, :], bank(XPROJ_BANK[c] + 1), W("dtw", h, h + 1),
                                                W("dtb", h, h + 1), ALU.mult, ALU.add).then_inc(S["dtpre_ready"], 1)

                def bc_rest(c):
                    dve.wait_ge(S["bc1_ready"], count("bc1_ready", c + 1))
                    nc.vector.scalar_tensor_tensor(out=bcrest_sb[0:96, c, :], in0=bc1_sb[0:96, c, :],
                                                   scalar=C("less1")[0:96, :],
                                                   in1=bank(XPROJ_BANK[c], rows=slice(0, 96)), op0=ALU.mult,
                                                   op1=ALU.add).then_inc(S["bcrest_ready"], 1)

                def bc_parts(c):
                    dve.wait_ge(S["bc2_ready"], count("bc2_ready", c + 1))
                    nc.vector.scalar_tensor_tensor(out=bc_sb[0:96, c, :], in0=bc2_sb[0:96, c, :],
                                                   scalar=C("less2")[0:96, :], in1=bcrest_sb[0:96, c, :],
                                                   op0=ALU.mult, op1=ALU.add).then_inc(S["bcparts_ready"], 1)

                def store_c0(k):
                    dve.wait_ge(S["crep_ready"], count("crep_ready", k + 1))
                    nc.vector.tensor_copy(crep_sb[:, 0, 2 * k:2 * k + 2, :],
                                          banks(C_BANK[k], 2)).then_inc(S["crep0_stored"], 1)

                def round_u(c):
                    dve.wait_ge(S["expabs_ready"], count("expabs_ready", c + 1))
                    nc.vector.tensor_scalar(u_sb[:, c, :, :], e_sb[:, c, :, :], 1.0, None,
                                            ALU.add).then_inc(S["u_ready"], 1)

                def residue(c):
                    dve.wait_ge(S["u_ready"], count("u_ready", c + 1))
                    nc.vector.scalar_tensor_tensor(out=u_sb[:, c, :, :], in0=u_sb[:, c, :, :], scalar=-1.0,
                                                   in1=e_sb[:, c, :, :], op0=ALU.add,
                                                   op1=ALU.subtract).then_inc(S["resid_ready"], 1)

                def relu_log(c):
                    dve.wait_ge(S["log1p_ready"], count("log1p_ready", c + 1))
                    nc.vector.scalar_tensor_tensor(out=delta_sb[:, c, :, :], in0=dt_sb[:, c, :, :], scalar=0.0,
                                                   in1=l_sb[:, c, :, :], op0=ALU.max,
                                                   op1=ALU.add).then_inc(S["relulog_ready"], 1)

                def delta(c):
                    dve.wait_ge(S["relulog_ready"], count("relulog_ready", c + 1))
                    nc.vector.tensor_tensor(delta_sb[:, c, :, :], delta_sb[:, c, :, :], u_sb[:, c, :, :],
                                            ALU.subtract).then_inc(S["delta_ready"], 1)

                dve.wait_ge(S["a_ready"], count("a_ready", 1))
                nc.vector.tensor_scalar(nega_sb[:, :], a_sb[:, :], -1.0, None, ALU.mult).then_inc(S["nega_ready"], 1)
                for u in range(3):
                    gate_x(u)
                dt(0)
                bc_rest(0)
                round_u(0)
                gate_x(3)
                residue(0)
                bc_parts(0)
                gate_z(4)
                relu_log(0)
                dt(1)
                delta(0)
                dve.wait_ge(S["delta_ready"], count("delta_ready", 1))
                nc.vector.tensor_tensor(du_sb[:, 0, :, :], delta_sb[:, 0, :, :], xs_sb[:, 0, :, :],
                                        ALU.mult).then_inc(S["du0_ready"], 1)
                store_c0(0)
                bc_rest(1)
                store_c0(1)
                round_u(1)
                bc_parts(1)
                residue(1)

                def drive(k):
                    _, c, ng, _ = scan_tile(2 * k)
                    if ng == 0:
                        dve.wait_ge(S["durep_ready"], count("durep_ready", k // 4 + 1))
                    if k in (0, 4):
                        dve.wait_ge(S["brep_stored"], count("brep_stored", 2 * c + 2))
                    if k >= 2:
                        dve.wait_ge(S["state_ready"], count("state_ready", 2 * k - 2))
                    slot = 2 * k % NDRV
                    nc.vector.tensor_tensor(drive_sb[:, slot:slot + 2, :], banks(DU_BANK[k // 4 % 2], 2),
                                            twice(brep_sb[:, c, ng, :]), ALU.mult).then_inc(S["drive_ready"], 1)

                def finish_y(k):
                    h, c = k // NC, k % NC
                    dve.wait_ge(S["hc_summed"], count("hc_summed", 32 * h + 8 * c + 24))
                    nc.vector.scalar_tensor_tensor(out=y_sb[:, c, h, :], in0=xs_sb[:, c, h, :],
                                                   scalar=dskh_sb[:, h:h + 1], in1=bank(4 + c), op0=ALU.mult,
                                                   op1=ALU.add).then_inc(S["yskip_ready"], 1)
                    dve.wait_ge(S["yskip_ready"], count("yskip_ready", k + 1))
                    nc.vector.tensor_tensor(y_sb[:, c, h, :], y_sb[:, c, h, :], zs_sb[:, c, h, :],
                                            ALU.mult).then_inc(S["y_ready"], 1)

                def add_mamba(c):
                    dve.wait_ge(S["outproj_ready"], count("outproj_ready", c + 1))
                    nc.vector.tensor_tensor(h1_sb[:, c * CT:(c + 1) * CT], x_sb[:, c * CT:(c + 1) * CT], bank(2 + c),
                                            ALU.add).then_inc(S["h1_ready"], 1)

                drive(0)
                for i in range(64):
                    _, c, _, _ = scan_tile(i)
                    if i % 2 == 0 and i + 2 < 64:
                        drive(i // 2 + 1)
                    dve.wait_ge(S["decay_ready"], count("decay_ready", i + 1))
                    if i % 2 == 0:
                        dve.wait_ge(S["drive_ready"], count("drive_ready", i // 2 + 1))
                    if i >= NST and i % 2 == 0:
                        dve.wait_ge(S["hc_ready"], count("hc_ready", (i - NST) // 2 + 1))
                    first = 0.0
                    if c:
                        dve.wait_ge(S["state_ready"], count("state_ready", i - 7))
                        first = state_sb[:, (i - 8) % NST, CT - 1:CT]
                    nc.vector.tensor_tensor_scan(state_sb[:, i % NST, :], decay_sb[:, i % NDEC, :],
                                                 drive_sb[:, i % NDRV, :], first,
                                                 ALU.mult, ALU.add).then_inc(S["state_ready"], 1)
                    if i == 0:
                        relu_log(1)
                    if i == 1:
                        delta(1)
                    if i in (2, 9, 14):
                        gate_z(5 + (2, 9, 14).index(i))
                    if i in (29, 37, 59):
                        finish_y((29, 37, 59).index(i))
                    if i == 61:
                        add_mamba(0)
                def attention_norm(c):
                    dve.wait_ge(S["rstd_ready"], count("rstd_ready", 2 + c + 1))
                    nc.vector.tensor_tensor(xn2_sb[:, c * CT:(c + 1) * CT], h1_sb[:, c * CT:(c + 1) * CT],
                                            rstd_sb[:, c, :], ALU.mult).then_inc(S["xn2_ready"], 1)

                def rest(c):
                    dve.wait_ge(S["part1_ready"], count("part1_ready", c + 1))
                    nc.vector.tensor_tensor(rest_sb[:, c, :, :], banks(2 * c, 2),
                                            part_sb[0][:, :, c * CT:(c + 1) * CT],
                                            ALU.subtract).then_inc(S["rest1_ready"], 1)

                def store_stack(u):
                    dve.wait_ge(S["stack_ready"], count("stack_ready", u + 1))
                    nc.vector.tensor_copy(stack_target(u), banks(4 + 2 * (u % 2), 2, rows=slice(0, 96))
                                          ).then_inc(S["stack_b_stored"], 1)

                attention_norm(0)
                finish_y(3)
                rest(0)
                add_mamba(1)
                store_stack(1)
                attention_norm(1)

                def max_parts(c):
                    m = negmax_sb[:, 16 * c:16 * c + 16]
                    dve.wait_ge(S["max_ready"], count("max_ready", 16 * c + 16))
                    nc.vector.tensor_copy(maxpart_sb[:, c, :, 0], m).then_inc(S["maxpart_ready"], 1)
                    dve.wait_ge(S["maxpart_ready"], count("maxpart_ready", 2 * c + 1))
                    nc.vector.tensor_tensor(maxpart_sb[:, c, :, 1], m, maxpart_sb[:, c, :, 0],
                                            ALU.subtract).then_inc(S["maxpart_ready"], 1)

                def max_rows(c):
                    dve.wait_ge(S["scores_ready"], count("scores_ready", 19 + 15 * c))
                    nc.vector.tensor_copy(qstack[96:98, 0, 2:4, c * CT:(c + 1) * CT],
                                          banks(ROW_BANK[c] + 2, 2, rows=slice(96, 98))
                                          ).then_inc(S["maxrow_b_stored"], 1)

                def weighted_values(c):
                    dve.wait_ge(S["rden_ready"], count("rden_ready", c + 1))
                    nc.vector.tensor_tensor(attn_sb[:, c * CT:(c + 1) * CT], rden_sb[:, c, :], bank(6),
                                            ALU.mult).then_inc(S["attn_stored"], 1)

                for n in range(QT * HEADS):
                    K = (n // HEADS + 1) * 128
                    dve.wait_ge(S["scores_ready"], count("scores_ready", n + n // 18 + 1))
                    nc.vector.tensor_reduce(negmax_sb[:, n:n + 1], ps[:, scores_bank(n) * CT:scores_bank(n) * CT + K], AX.X,
                                            ALU.max, negate=True).then_inc(S["max_ready"], 1)
                    if n in (4, 7):
                        store_stack(n)
                    if n == 3:
                        rest(1)
                    if n == 14:
                        dve.wait_ge(S["v_ready"], count("v_ready", 1))
                        nc.vector.tensor_copy(vt_sb[:, :, :].rearrange("p a n -> p (a n)"),
                                              bank(4)).then_inc(S["v_stored"], 1)
                    if n % 16 == 15:
                        max_parts(n // 16)
                    if n == 16:
                        max_rows(0)
                max_rows(1)
                weighted_values(0)
                for g in range(4, 12):
                    _, _, _, q0 = st_unit(4 * g)
                    probs = pt_sb[:, g % 2, :, q0:CT]
                    dve.wait_ge(S["probs_ready"], count("probs_ready", 4 * g + 4))
                    if g == 4:
                        nc.vector.tensor_copy(probsum_sb[:, :, :], probs).then_inc(S["probsum_ready"], 1)
                    else:
                        dve.wait_ge(S["probsum_ready"], count("probsum_ready", g - 4))
                        nc.vector.tensor_tensor(probsum_sb[:, :, q0:CT], probsum_sb[:, :, q0:CT], probs,
                                                ALU.add).then_inc(S["probsum_ready"], 1)
                weighted_values(1)
                for c in range(NC):
                    dve.wait_ge(S["oproj_ready"], count("oproj_ready", c + 1))
                    nc.vector.tensor_tensor(h2_sb[:, c * CT:(c + 1) * CT], h1_sb[:, c * CT:(c + 1) * CT], bank(c),
                                            ALU.add).then_inc(S["h2_ready"], 1)
                for c in range(NC):
                    dve.wait_ge(S["rstd_ready"], count("rstd_ready", 4 + c + 1))
                    nc.vector.tensor_tensor(xn2_sb[:, c * CT:(c + 1) * CT], h2_sb[:, c * CT:(c + 1) * CT],
                                            rstd_sb[:, c, :], ALU.mult).then_inc(S["xn3_ready"], 1)
                for u in range(6):
                    c, m = u // 3, u % 3
                    rows = slice(0, FM[m])
                    dve.wait_ge(S["gtanh_ready"], count("gtanh_ready", u + 1))
                    nc.vector.scalar_tensor_tensor(out=v_sb[rows, u % 4, :], in0=th_sb[rows, u % 4, :], scalar=1.0,
                                                   in1=bank(2 * (u % 2), rows=rows), op0=ALU.add,
                                                   op1=ALU.mult).then_inc(S["gsilu_ready"], 1)
                    dve.wait_ge(S["gsilu_ready"], count("gsilu_ready", u + 1))
                    nc.vector.tensor_tensor(swi_sb[rows, c, m, :], v_sb[rows, u % 4, :],
                                            bank(2 * (u % 2) + 1, rows=rows), ALU.mult).then_inc(S["swiglu_ready"], 1)
                for c in range(NC):
                    dve.wait_ge(S["down_ready"], count("down_ready", c + 1))
                    nc.vector.tensor_tensor(s_sb[:, c, :], h2_sb[:, c * CT:(c + 1) * CT], bank(6 + c),
                                            ALU.add).then_inc(S["h3_ready"], 1)
                    dve.wait_ge(S["h3_ready"], count("h3_ready", c + 1))
                    nc.vector.tensor_tensor(s_sb[:, c, :], s_sb[:, c, :], x_sb[:, c * CT:(c + 1) * CT],
                                            ALU.add).then_inc(S["sum_ready"], 1)
                for c in range(NC):
                    dve.wait_ge(S["rstd_ready"], count("rstd_ready", 6 + c + 1))
                    nc.vector.tensor_tensor(ln1_sb[:, c, :], rstd_sb[:, c, :], bank(4 + c),
                                            ALU.mult).then_inc(S["ln1_ready"], 1)
                for t in range(QT):
                    dve.wait_ge(S["mlpout_ready"], count("mlpout_ready", t // 4 + 1))
                    nc.vector.bn_stats(stats_sb[:, t, :], bank(6 + t // 4, (t % 4) * 128, (t % 4) * 128 + 128)
                                       ).then_inc(S["stats_ready"], 1)
                dve.wait_ge(S["stats_ready"], count("stats_ready", QT))
                nc.vector.memset(spare_sb[:, :], 0.0)
                for t in range(QT):
                    nc.vector.bn_aggr(mv_sb[:, t, :], stats_sb[:, t, :]).then_inc(S["meanvar_ready"], 1)
                first_norm(count, 16 * b + 32, 8)
                dve.wait_ge(S["rstd2_ready"], count("rstd2_ready", 1))
                dve.wait_ge(S["meanvar_ready"], count("meanvar_ready", 8))
                dve.wait_ge(out_free, 16 * b + 16)
                for t in range(QT):
                    last = nc.vector.tensor_scalar(out_sb[:, t, :],
                                                   bank(6 + t // 4, (t % 4) * 128, (t % 4) * 128 + 128),
                                                   mv_sb[:, t, 0:1], rs2_sb[:, t:t + 1], ALU.subtract, ALU.mult)
                last.then_inc(S["out_ready"], 1)

        @block.tensor
        def _(pe):
            mm = nc.tensor.matmul

            def meansq(count, k):
                pe.wait_ge(S["square_ready"], count("square_ready", k + 1))
                mm(bank(MEANSQ[k]), C("mean"), sq_sb[:, k % 2, :], start=True,
                   stop=True).then_inc(S["meansq_ready"], 1)

            pe.wait_ge(consts_loaded, 16)
            for c in range(NC):
                meansq(turns(0), c)
            with pe.Fori(0, BATCH) as b:
                count = turns(b)
                pe.wait_ge(setup_dve, N_SETUP_DVE)
                def in_proj(u):
                    c, half = u // 2 % 2, u % 2
                    pe.wait_ge(S["xn_ready"], count("xn_ready", c + 1))
                    if u == 4:
                        pe.wait_ge(S["tanh_ready"], count("tanh_ready", 3))
                    if u == 5:
                        pe.wait_ge(S["crep0_stored"], count("crep0_stored", 2))
                    if u > 5:
                        pe.wait_ge(S["gated_ready"], count("gated_ready", u))
                    if u < 4:
                        for j in range(DCONV):
                            last = mm(bank(IN_BANK[u]), wconv_sb[:, j, half * 128:(half + 1) * 128],
                                      xn_sb[:, c * CT + j:c * CT + j + CT], start=(j == 0), stop=(j == DCONV - 1))
                    else:
                        last = mm(bank(IN_BANK[u]), win_sb[:, DI + half * 128:DI + (half + 1) * 128],
                                  xn_sb[:, DCONV - 1 + c * CT:DCONV - 1 + (c + 1) * CT], start=True, stop=True)
                    last.then_inc(S["inproj_ready"], 1)

                def x_proj_dt(c):
                    pe.wait_ge(S["gated_ready"], count("gated_ready", 2 * c + 2))
                    for h in range(NH):
                        last = mm(bank(XPROJ_BANK[c] + 1), wdt_sb[:, h, :], xs_sb[:, c, h, :], start=(h == 0),
                                  stop=(h == NH - 1))
                    last.then_inc(S["dtraw_ready"], 1)

                def x_proj_bc(c):
                    for h in range(NH):
                        last = mm(bank(XPROJ_BANK[c], rows=slice(0, 96)),
                                  wbc_sb[:, h, :, :].rearrange("p a n -> p (a n)"), xs_sb[:, c, h, :],
                                  start=(h == 0), stop=(h == NH - 1))
                    last.then_inc(S["bcraw_ready"], 1)

                def spread_b(k):
                    c = k // 2
                    if k == 0:
                        pe.wait_ge(S["gated_ready"], count("gated_ready", 5))
                    if k == 3:
                        pe.wait_ge(S["crep1_stored"], count("crep1_stored", 1))
                    if k % 2 == 0:
                        pe.wait_ge(S["bcparts_ready"], count("bcparts_ready", c + 1))
                    for w in range(2):
                        n = 4 * (2 * (k % 2) + w)
                        last = mm(bank(B_BANK[k] + w), selbc_sb[0:96, n:n + 4, :].rearrange("p n r -> p (n r)"),
                                  bc_sb[0:96, c, :], start=True, stop=True)
                    last.then_inc(S["brep_ready"], 1)

                def spread_c(k):
                    c = k // 2
                    if k == 0:
                        pe.wait_ge(S["dtpre_ready"], count("dtpre_ready", 2))
                    if k == 1:
                        pe.wait_ge(S["crep0_stored"], count("crep0_stored", 1))
                    if k >= 2:
                        pe.wait_ge(S["brep_stored"], count("brep_stored", k + 1))
                    for w in range(2):
                        n = 16 + 4 * (2 * (k % 2) + w)
                        last = mm(bank(C_BANK[k] + w), selbc_sb[0:96, n:n + 4, :].rearrange("p n r -> p (n r)"),
                                  bc_sb[0:96, c, :], start=True, stop=True)
                    last.then_inc(S["crep_ready"], 1)

                for u in range(3):
                    in_proj(u)
                pe.wait_ge(setup_pool, 2)
                x_proj_dt(0)
                x_proj_bc(0)
                in_proj(3)
                in_proj(4)
                x_proj_dt(1)
                spread_b(0)
                spread_b(1)
                spread_c(0)
                x_proj_bc(1)

                def spread(q, k, src, ready):
                    pr, c, _, _ = scan_tile(8 * q)
                    for s in range(2):
                        h, j = (2 * pr + s) // 4, (2 * pr + s) % 4
                        last = mm(bank(k + s), C("selD")[:, 128 * j:128 * j + 128], src[:, c, h, :], start=True,
                                  stop=True)
                    last.then_inc(S[ready], 1)

                def out_proj(c):
                    if c == 0:
                        pe.wait_ge(setup_pool, 3)
                        pe.wait_ge(S["drive_ready"], count("drive_ready", 28))
                    pe.wait_ge(S["y_ready"], count("y_ready", NC + c + 1))
                    for h in range(NH):
                        last = mm(bank(2 + c), wout_sb[:, h, :], y_sb[:, c, h, :], start=(h == 0), stop=(h == NH - 1))
                    last.then_inc(S["outproj_ready"], 1)

                def qk(c):
                    if c == 0:
                        pe.wait_ge(S["decay_ready"], count("decay_ready", 64))
                    pe.wait_ge(S["xn2_ready"], count("xn2_ready", c + 1))
                    xn2 = xn2_sb[:, c * CT:(c + 1) * CT]
                    mm(bank(2 * c), wq_sb[:, :], xn2, start=True, stop=True)
                    mm(bank(2 * c + 1), wk_sb[:, :, :].rearrange("p a n -> p (a n)"), xn2, start=True,
                       stop=True).then_inc(S["qk_ready"], 1)

                def values():
                    pe.wait_ge(S["stack_a_stored"], count("stack_a_stored", 8))
                    for t in range(QT):
                        last = mm(bank(4, 64 * t, 64 * t + 64), xn2_sb[:, t * 128:(t + 1) * 128], wv_sb[:, :],
                                  start=True, stop=True)
                    last.then_inc(S["v_ready"], 1)

                pe.wait_ge(S["delta_ready"], count("delta_ready", 1))
                pe.wait_ge(S["brep_stored"], count("brep_stored", 2))
                spread(0, 0, delta_sb, "drep_ready")
                pe.wait_ge(S["du0_ready"], count("du0_ready", 1))
                spread(0, DU_BANK[0], du_sb, "durep_ready")
                spread_c(1)
                pe.wait_ge(S["dtpre_ready"], count("dtpre_ready", 4))
                spread_b(2)
                in_proj(5)
                spread_c(2)
                spread_b(3)
                spread_c(3)
                pe.wait_ge(S["du1_ready"], count("du1_ready", 1))
                pe.wait_ge(S["crep1_stored"], count("crep1_stored", 2))
                spread(1, DU_BANK[1], du_sb, "durep_ready")
                for i in range(64):
                    pr, c, ng, s = scan_tile(i)
                    dg = 2 * pr + s
                    h, j = dg // 4, dg % 4
                    q = i // 8 + 1
                    if i == 2:
                        pe.wait_ge(S["decay_ready"], count("decay_ready", 8))
                        spread(1, 0, delta_sb, "drep_ready")
                    if i == 4:
                        in_proj(6)
                    if i == 6:
                        in_proj(7)
                    if i == 58:
                        out_proj(0)
                    if i == 60:
                        meansq(count, 2)
                    if i % 8 == 4 and q < 7:
                        pe.wait_ge(S["drive_ready"], count("drive_ready", 4 * q))
                        spread(q + 1, DU_BANK[(q + 1) % 2], du_sb, "durep_ready")
                    if i % 8 == 0 and 1 < q < 8:
                        pe.wait_ge(S["decay_ready"], count("decay_ready", 8 * q))
                        spread(q, 0, delta_sb, "drep_ready")
                    if i == 8:
                        pe.wait_ge(S["gated_ready"], count("gated_ready", 8))
                    if pr == 2 and ng == 0 and s == 0:
                        pe.wait_ge(S["yskip_ready"], count("yskip_ready", c + 1))
                    pe.wait_ge(S["hc_ready"], count("hc_ready", i // 2 + 1))
                    mm(bank(4 + c, rows=slice(32 * j, 32 * j + 32)), C("sum"), hc_sb[:, i % NHC, :],
                       start=(ng == 0), stop=(ng == NG - 1)).then_inc(S["hc_summed"], 1)
                qk(0)
                out_proj(1)

                def scores(n):
                    i, h = n // HEADS, n % HEADS
                    K = (i + 1) * 128
                    if n == 0:
                        pe.wait_ge(S["stack_a_stored"], count("stack_a_stored", 2))
                        pe.wait_ge(S["stack_b_stored"], count("stack_b_stored", 1))
                    if n == 6:
                        pe.wait_ge(S["rest1_ready"], count("rest1_ready", NC))
                    if n == 16:
                        pe.wait_ge(S["stack_a_stored"], count("stack_a_stored", 6))
                        pe.wait_ge(S["stack_b_stored"], count("stack_b_stored", 3))
                    if 8 <= n < 16:
                        pe.wait_ge(S["max_ready"], count("max_ready", n - 3))
                    elif n in (16, 17):
                        pe.wait_ge(S["max_ready"], count("max_ready", 2 * n - 18))
                    elif 2 <= n < 6 or n >= 18:
                        pe.wait_ge(S["max_ready"], count("max_ready", n - 1))
                    for k0 in range(0, K, CT):
                        k1 = min(k0 + CT, K)
                        mm(bank(scores_bank(n) + k0 // CT, 0, k1 - k0), qstack[0:96, 0, h, i * 128:(i + 1) * 128],
                           kstack[0:96, 0, h // 2, k0:k1], start=True, stop=(k1 < K))
                    mm(bank(scores_bank(n) + k0 // CT, k1 - k0 - 128, k1 - k0), identb[:, :], maskb[:, :],
                       start=False, stop=True).then_inc(S["scores_ready"], 1)

                def max_rows(c):
                    pe.wait_ge(S["maxpart_ready"], count("maxpart_ready", 2 * c + 2))
                    if c == 0:
                        pe.wait_ge(S["stack_a_stored"], count("stack_a_stored", 9))
                        pe.wait_ge(S["v_stored"], count("v_stored", 1))
                    for h in range(HEADS):
                        for i in range(4):
                            last = mm(bank(ROW_BANK[c] + h, i * 128, (i + 1) * 128, rows=slice(96, 98)),
                                      maxpart_sb[:, c, i * HEADS + h, :], identb[:, :], start=True, stop=True)
                    last.then_inc(S["scores_ready"], 1)

                def scores_t(v):
                    c, j, h, q0 = st_unit(v)
                    if v in (0, 16):
                        pe.wait_ge(S["maxrow_a_stored"], count("maxrow_a_stored", c + 1))
                        pe.wait_ge(S["maxrow_b_stored"], count("maxrow_b_stored", c + 1))
                        pe.wait_ge(S["stack_a_stored"], count("stack_a_stored", 5 * c + 4))
                        pe.wait_ge(S["stack_b_stored"], count("stack_b_stored", c + 2))
                        pe.wait_ge(S["v_stored"], count("v_stored", 1))
                    if 2 <= v < 16:
                        pe.wait_ge(S["probs_ready"], count("probs_ready", v - 1))
                    elif v >= 22:
                        pe.wait_ge(S["probs_ready"], count("probs_ready", v - 5))
                    elif v >= 20:
                        pe.wait_ge(S["probs_ready"], count("probs_ready", 16))
                    o = bank(st_bank(v), q0, CT)
                    at = slice(c * CT + q0, (c + 1) * CT)
                    mm(o, kstack[0:98, 0, h // 2, j * 128:(j + 1) * 128], qstack[0:98, 0, h, at], start=True,
                       stop=False)
                    last = mm(o, kstack[0:96, 1, h // 2, j * 128:(j + 1) * 128], qstack[0:96, 1, h, at], start=False,
                              stop=(j < 4 * c))
                    if j >= 4 * c:
                        last = mm(bank(st_bank(v), q0, q0 + 128), maskb[:, :], identb[:, :], start=False, stop=True)
                    last.then_inc(S["scorest_ready"], 1)

                def weighted(g):
                    c, j, _, q0 = st_unit(4 * g)
                    pe.wait_ge(S["probs_ready"], count("probs_ready", 4 * g + 4))
                    if g == 4:
                        pe.wait_ge(S["attn_stored"], count("attn_stored", 1))
                    for k in (6, 7) if c == 0 else (6,):
                        for h in range(HEADS):
                            kv = h // (HEADS // KV)
                            last = mm(bank(k, q0, CT, rows=slice(32 * h, 32 * h + 32)),
                                      vt_sb[:, j, kv * HD:(kv + 1) * HD] if k == 6 else C("ones")[:, 0:32],
                                      pt_sb[:, g % 2, h, q0:CT], start=(j == 0), stop=(j == 4 * c + 3))
                    last.then_inc(S["pv_ready"], 1)

                def stack(u):
                    c, m, pair = stack_unit(u)
                    which, parts = (1, K_PARTS) if pair == 0 else (0, Q_PARTS)
                    pe.wait_ge(S["part3_ready" if m else "part2_ready"], count("part3_ready" if m else "part2_ready", c + 1))
                    if u >= 2:
                        pe.wait_ge(S[stack_reader(u - 2)], count(stack_reader(u - 2), stack_reads(u - 2)))
                    for e in range(2):
                        row = 64 * e if pair == 0 else 64 * (pair - 1) + 32 * e
                        rows = slice(row, row + 32)
                        for g, n in enumerate(parts[m]):
                            last = mm(bank(4 + 2 * (u % 2) + e, rows=slice(32 * g, 32 * g + 32)), identb[:, rows],
                                      part_sb[n][:, which, c * CT:(c + 1) * CT], start=True, stop=True)
                    last.then_inc(S["stack_ready"], 1)

                for u in range(3):
                    stack(u)
                meansq(count, 3)
                qk(1)
                for n in range(18):
                    scores(n)
                    if 3 <= n < 12:
                        stack(n)
                    if n == 12:
                        values()
                max_rows(0)
                for v in range(16):
                    scores_t(v)
                    if v + 18 < 32:
                        scores(v + 18)
                    if v % 4 == 3 and v > 3:
                        weighted(v // 4 - 1)
                max_rows(1)
                weighted(3)
                for g in range(4, 12):
                    for v in range(4 * g, 4 * g + 4):
                        scores_t(v)
                    if g > 4:
                        weighted(g - 1)
                weighted(11)
                pe.wait_ge(S["probsum_ready"], count("probsum_ready", 8))
                for h in range(HEADS):
                    last = mm(bank(7, rows=slice(32 * h, 32 * h + 32)), C("ones")[:, 0:32], probsum_sb[:, h, :],
                              start=True, stop=True)
                last.then_inc(S["den_ready"], 1)
                for c in range(NC):
                    pe.wait_ge(S["attn_stored"], count("attn_stored", c + 1))
                    mm(bank(c), W("o"), attn_sb[:, c * CT:(c + 1) * CT], start=True,
                       stop=True).then_inc(S["oproj_ready"], 1)
                for c in range(NC):
                    meansq(count, 4 + c)
                for u in range(6):
                    c, m = u // 3, u % 3
                    rows = slice(0, FM[m])
                    pe.wait_ge(S["xn3_ready"], count("xn3_ready", c + 1))
                    pe.wait_ge(S["h2_ready"], count("h2_ready", 2))
                    if u >= 2:
                        pe.wait_ge(S["swiglu_ready"], count("swiglu_ready", u - 1))
                    xn3 = xn2_sb[:, c * CT:(c + 1) * CT]
                    mm(bank(2 * (u % 2), rows=rows), wgate_sb[:, m * 128:m * 128 + FM[m]], xn3, start=True, stop=True)
                    mm(bank(2 * (u % 2) + 1, rows=rows), wup_sb[:, m * 128:m * 128 + FM[m]], xn3, start=True,
                       stop=True).then_inc(S["gateup_ready"], 1)
                for c in range(NC):
                    for m in range(3):
                        pe.wait_ge(S["swiglu_ready"], count("swiglu_ready", 3 * c + m + 1))
                        last = mm(bank(6 + c), wdown_sb[0:FM[m], m, :], swi_sb[0:FM[m], c, m, :], start=(m == 0),
                                  stop=(m == 2))
                    last.then_inc(S["down_ready"], 1)
                for c in range(NC):
                    pe.wait_ge(S["sum_ready"], count("sum_ready", c + 1))
                    mm(bank(4 + c), C("center"), s_sb[:, c, :], start=True,
                       stop=True).then_inc(S["centered_ready"], 1)
                for c in range(NC):
                    meansq(count, 6 + c)
                for u in range(8):
                    c, m = u // MM, u % MM
                    pe.wait_ge(S["ln1_ready"], count("ln1_ready", c + 1))
                    if u >= 4:
                        pe.wait_ge(S["gelu_ready"], count("gelu_ready", u - 3))
                    mm(bank(u % 4), W("w1", m * 128, (m + 1) * 128), ln1_sb[:, c, :], start=True,
                       stop=True).then_inc(S["mlp_ready"], 1)
                for c in range(NC):
                    meansq(count, 8 + c)
                for c in range(NC):
                    pe.wait_ge(S["gelu_ready"], count("gelu_ready", MM * (c + 1)))
                    pe.wait_ge(S["ln1bias_ready"], count("ln1bias_ready", c + 1))
                    for t in range(4):
                        o = bank(6 + c, t * 128, (t + 1) * 128)
                        for m in range(MM):
                            mm(o, gelu_sb[:, c, m, t * 128:(t + 1) * 128], W("w2", m * 128, (m + 1) * 128),
                               start=(m == 0), stop=False)
                        last = mm(o, s_sb[:, c, t * 128:(t + 1) * 128], C("ident"), start=False, stop=True)
                    last.then_inc(S["mlpout_ready"], 1)


def scan_tile(i):
    return i // 16, (i // 8) % 2, (i // 2) % 4, i % 2


def stack_unit(u):
    return u // 6, u // 3 % 2, u % 3


def stack_reader(u):
    return "stack_b_stored" if u in (1, 4, 7) else "stack_a_stored"


def stack_reads(u):
    return sum(stack_reader(v) == stack_reader(u) for v in range(u + 1))


def scores_bank(n):
    if n < 4:
        return n % 2
    return n % 4 if n < 16 else 2 * (n % 2)


def st_bank(v):
    return 4 + v % 2 if v < 16 else (v - 16) % 6


def st_unit(v):
    c, g = (0, v // 4) if v < 16 else (1, v // 4 - 4)
    return c, g, v % 4, max(0, (g - 4 * c) * 128)


def kernel(**inputs):
    import numpy as np
    import concourse.bacc as bacc
    from concourse.bass_utils import run_bass_kernel_spmd

    f = {k.replace("L0_", ""): np.asarray(v) for k, v in inputs.items()}

    def halves(a, n):
        return a.reshape(n, 128, -1).transpose(1, 0, 2).reshape(128, -1)

    down = np.zeros((384, D), np.float32)
    down[:FFN] = f["attn_down_w"].T
    alog = f["attn_A_log"].reshape(DG, DS, NG, NS).transpose(3, 1, 0, 2).reshape(128, DG * NG)
    parts = {
        "in": f["attn_in_proj_w"].T, "xp": halves(f["attn_x_proj_w"].T, 2), "out": halves(f["attn_out_proj_w"].T, 2),
        "q": f["attn_q_w"].T, "k": f["attn_k_w"].T, "v": f["attn_v_w"].T, "o": f["attn_o_w"].T,
        "gate": f["attn_gate_w"].T, "up": f["attn_up_w"].T, "down": halves(down, 3),
        "w1": f["ffn_w1"], "w2": halves(f["ffn_w2"], 4),
        "nm": f["attn_norm_m_w"][:, None], "na": f["attn_norm_attn_w"][:, None], "nf": f["attn_norm_ffn_w"][:, None],
        "cb": f["attn_conv_b"].reshape(2, 128).T, "dtw": f["attn_dt_w"].reshape(2, 128).T,
        "dtb": f["attn_dt_b"].reshape(2, 128).T, "dsk": f["attn_D_skip"].reshape(2, 128).T,
        "b1": f["ffn_b1"].reshape(4, 128).T, "alog": alog,
    }
    wts = np.ascontiguousarray(np.concatenate([parts[k] for k in W_COLS], axis=1))
    p, q = np.arange(128)[:, None], np.arange(128)[None, :]
    eye = (p == q).astype(np.float32)
    consts = {
        "ident": eye, "center": eye - np.float32(1 / 128), "mean": np.full((128, 128), 1 / 128, np.float32),
        "selD": np.concatenate([(p % 32 == q % 32) & (p // 32 == j) for j in range(4)], axis=1),
        "sum": (p % 32 == np.arange(32)[None, :]).astype(np.float32),
        "mask": np.where(q > p, np.float32(-1e30), np.float32(0)),
        "ones": np.ones((128, 128), np.float32),
        "less1": -(p // 32 >= 1).astype(np.float32), "less2": -(p // 32 >= 2).astype(np.float32),
    }
    cst = np.ascontiguousarray(np.concatenate([consts[k] for k in C_COLS], axis=1).astype(np.float32))
    arrays = {
        "x": np.ascontiguousarray(f["attn_x"].reshape(BATCH * SEQ, D).T), "wts": wts, "cst": cst,
        "convw": np.ascontiguousarray(f["attn_conv_w"][:, 0, :].T.reshape(1, -1)), "b2": f["ffn_b2"].reshape(D, 1),
    }
    nc = bacc.Bacc("TRN2", target_bir_lowering=False, num_devices=1)
    args = [nc.dram_tensor(n, a.shape, mybir.dt.float32, kind="ExternalInput").ap() for n, a in arrays.items()]
    out = nc.dram_tensor("out", (128, BATCH * QT, D), mybir.dt.float32, kind="ExternalOutput").ap()
    build(nc, *args, out)
    r = run_bass_kernel_spmd(nc, [arrays], core_ids=[0])
    return np.ascontiguousarray(r.results[0]["out"].transpose(1, 0, 2)).reshape(BATCH, SEQ, D)
```

```python
import concourse.bass as bass
from concourse import mybir
from contextlib import ExitStack

BATCH, SEQ, D = 2, 1024, 128
DI, NSTATE, DCONV = 256, 16, 4
HEADS, KV, HD = 4, 2, 32
FFN, MLP = 341, 512
CT = 512
NC = SEQ // CT
NH = DI // 128
NS, DS = 4, 32
NG, DG = NSTATE // NS, DI // DS
QT = SEQ // 128
FM = [128, 128, FFN - 256]
MM = MLP // 128
EPS_RMS, EPS_LN = 1e-6, 1e-5

W_COLS = {"in": 512, "xp": 2 * 33, "nm": 1, "na": 1, "nf": 1, "cb": 2, "taps": DCONV, "dtw": 2, "dtb": 2, "dsk": 2,
          "b1": 4, "alog": 32, "out": 256, "q": 128, "k": 64, "v": 64, "o": 128, "gate": FFN,
          "up": FFN, "down": 384, "w1": 512, "w2": 512}
C_COLS = {"ident": 128, "center": 128, "mean": 128, "selD": 4 * 128, "sum": 32, "mask": 128, "ones": 128,
          "less1": 1, "less2": 1}


def offsets(cols):
    at, out = 0, {}
    for name, n in cols.items():
        out[name] = (at, n)
        at += n
    return out, at


W_AT, W_ALL = offsets(W_COLS)
C_AT, C_ALL = offsets(C_COLS)
W_FIRST = W_AT["out"][0]

SIGNALS = {
    "a_ready": 1, "nega_ready": 1, "square_ready": 8, "meansq_ready": 8, "log_ready": 8, "rstd_ready": 8, "xn_ready": 2,
    "inproj_ready": 8, "tap_ready": 2 * DCONV, "tanh_ready": 8, "gated_ready": 8,
    "dtraw_ready": 2, "bcraw_ready": 2, "bc1_ready": 2, "bcrest_ready": 2, "bc2_ready": 2, "bcparts_ready": 2,
    "dtpre_ready": 4, "abs_ready": 2, "expabs_ready": 2, "log1p_ready": 2,
    "u_ready": 2, "resid_ready": 2, "relulog_ready": 2, "delta0_ready": 1, "delta1_ready": 1, "du0_ready": 1, "du1_ready": 1,
    "brep_ready": 4, "crep_ready": 4, "brep_stored": 4, "crep0_stored": 2, "crep1_stored": 2,
    "drep_ready": 8, "durep_ready": 8, "decay_ready": 64, "drive_ready": 32, "state_ready": 64,
    "hc_ready": 32, "hc_summed": 64, "yskip_ready": 4, "y_ready": 4,
    "outproj_ready": 2, "h1_ready": 2, "xn2_ready": 2, "qk_ready": 2, "v_ready": 1, "v_stored": 1,
    "part1_ready": 2, "rest1_ready": 2, "part2_ready": 2, "part3_ready": 2,
    "pad_ready": 1, "stack_ready": 12, "stack_a_stored": 9, "stack_b_stored": 3,
    "scores_ready": 34,
    "max_ready": 32, "maxpart_ready": 4, "maxrow_a_stored": 2,
    "maxrow_b_stored": 2, "scorest_ready": 48, "probs_ready": 48, "pv_ready": 12, "probsum_ready": 8, "den_ready": 1, "logden_ready": 2,
    "rden_ready": 2, "attn_stored": 2,
    "oproj_ready": 2, "h2_ready": 2, "xn3_ready": 2,
    "gateup_ready": 6, "gtanh_ready": 6, "gsilu_ready": 6, "swiglu_ready": 6,
    "down_ready": 2, "h3_ready": 2, "sum_ready": 2, "centered_ready": 2, "ln1_ready": 2, "ln1bias_ready": 2,
    "mlp_ready": 8, "gelu_ready": 8, "mlpout_ready": 2, "stats_ready": 8, "meanvar_ready": 8,
    "logvar_ready": 2, "rstd2_ready": 2, "out_ready": 2,
}


def build(nc, x, wts, cst, convw, b2, out):
    fp32, bf16 = mybir.dt.float32, mybir.dt.bfloat16
    ALU, ACT, AX = mybir.AluOpType, mybir.ActivationFunctionType, mybir.AxisListType
    LN_EXP = "natural_log_exp_and_others"

    ctx = ExitStack()
    with ctx:
        def sb(name, shape, dt=fp32):
            return ctx.enter_context(nc.sbuf_tensor(name, shape, dt))

        def sem(name):
            return ctx.enter_context(nc.semaphore(name))

        w_sb = sb("w_sb", [128, W_ALL])
        c_sb = sb("c_sb", [128, C_ALL])

        def W(name, a=0, b=None):
            at, n = W_AT[name]
            return w_sb[:, at + a:at + (n if b is None else b)]

        def C(name):
            at, n = C_AT[name]
            return c_sb[:, at:at + n]

        b2_sb = sb("b2_sb", [D, 1])
        win_sb = sb("win_sb", [128, 2 * DI])
        wconv_sb = sb("wconv_sb", [128, DCONV, 128])
        wbc_sb = sb("wbc_sb", [128, NH, 3, 32])
        wdt_sb = sb("wdt_sb", [128, NH, 128])
        wout_sb = sb("wout_sb", [128, NH, D])
        wq_sb = sb("wq_sb", [128, D])
        wk_sb = sb("wk_sb", [128, HEADS, HD])
        wv_sb = sb("wv_sb", [128, KV * HD])
        wgate_sb = sb("wgate_sb", [128, FFN])
        wup_sb = sb("wup_sb", [128, FFN])
        wdown_sb = sb("wdown_sb", [128, 3, D])
        a_sb = sb("a_sb", [128, DG * NG])
        nega_sb = sb("nega_sb", [128, DG * NG])
        cbh_sb = sb("cbh_sb", [128, NH])
        dskh_sb = sb("dskh_sb", [128, NH])
        identb = sb("identb", [128, 128], bf16)
        maskb = sb("maskb", [128, 128], bf16)
        eps_sb = sb("eps_sb", [128, 2])

        x_sb = sb("x_sb", [128, SEQ])
        rstd_sb = sb("rstd_sb", [128, NC, CT])
        xn_sb = sb("xn_sb", [128, DCONV - 1 + SEQ])
        xs_sb = sb("xs_sb", [128, NC, NH, CT])
        zs_sb = sb("zs_sb", [128, NC, NH, CT])
        bc_sb = sb("bc_sb", [128, NC, CT], bf16)
        selbc_sb = sb("selbc_sb", [128, 32, 32], bf16)
        dt_sb = sb("dt_sb", [128, NC, NH, CT])
        e_sb = sb("e_sb", [128, NC, NH, CT])
        l_sb = sb("l_sb", [128, NC, NH, CT])
        delta_sb = sb("delta_sb", [128, NC, NH, CT])
        du_sb = sb("du_sb", [128, NC, NH, CT])
        brep_sb = sb("brep_sb", [128, NC, NG, CT])
        crep_sb = sb("crep_sb", [128, NC, NG, CT])
        NDEC, NDRV, NST, NHC = 6, 4, 12, 4
        decay_sb = sb("decay_sb", [128, NDEC, CT])
        drive_sb = sb("drive_sb", [128, NDRV, CT])
        state_sb = sb("state_sb", [128, NST, CT])
        hc_sb = sb("hc_sb", [128, NHC, CT])
        y_sb = dt_sb
        convw_sb = decay_sb[:, 0:2, :].rearrange("p a t -> p (a t)").rearrange("p (j d) -> p j d", j=DCONV)
        v_sb, th_sb = drive_sb, state_sb[:, 0:4, :]
        u_sb = du_sb
        hc_b = hc_sb[:, :, :].rearrange("p a t -> p (a t)").bitcast(bf16).rearrange("p (a t) -> p a t", t=CT)
        bc1_sb, bc2_sb = hc_b[:, 0:2, :], hc_b[:, 2:4, :]
        bcrest_sb = hc_sb[:, 2:4, :]
        out_sb = decay_sb[:, 2:4, :].rearrange("p a t -> p (a t)").rearrange("p (t d) -> p t d", t=QT)
        h1_sb = zs_sb[:, 0, :, :].rearrange("p a t -> p (a t)")
        xn2_sb = e_sb[:, 0, :, :].rearrange("p a t -> p (a t)")
        attn_sb = l_sb[:, 1, :, :].rearrange("p a t -> p (a t)")
        vt_sb = sb("vt_sb", [128, QT, KV * HD])
        crep_b = crep_sb[:, :, :, :].rearrange("p c g t -> p (c g t)").bitcast(bf16)
        part_sb = [crep_b[:, 2 * SEQ * n:2 * SEQ * (n + 1)].rearrange("p (w t) -> p w t", w=2) for n in range(3)]
        rest_sb = drive_sb[:, :, :].rearrange("p (c w) t -> p c w t", c=NC)
        state_b = state_sb[:, :, :].rearrange("p a t -> p (a t)").bitcast(bf16)
        qstack = state_b[:, 0:2 * HEADS * SEQ].rearrange("p (m h t) -> p m h t", m=2, h=HEADS)
        kstack = sb("kstack", [128, 2, KV, SEQ], bf16)
        Q_PARTS = [(0, 0, 1), (1, 0, 2)]
        K_PARTS = [(0, 1, 0), (1, 2, 0)]
        sq_sb = sb("sq_sb", [128, 2, CT])
        log_sb = sb("log_sb", [128, 2, CT])
        pt_sb = brep_sb[:, :, :, :]
        probsum_sb = decay_sb[:, 0:4, :]
        negmax_sb = sb("negmax_sb", [128, QT * HEADS])
        maxpart_sb = sb("maxpart_sb", [128, NC, 16, 2], bf16)
        rden_sb = rstd_sb
        h2_sb = du_sb[:, 0, :, :].rearrange("p a t -> p (a t)")
        swi_sb = brep_sb[:, :, 0:3, :]
        s_sb = delta_sb[:, 0, :, :]
        ln1_sb = delta_sb[:, 1, :, :]
        gelu_sb = crep_sb
        stats_sb = sb("stats_sb", [128, QT, 6])
        mv_sb = sb("mv_sb", [128, QT, 2])
        lv_sb = sb("lv_sb", [128, QT])
        spare_sb = sb("spare_sb", [128, 1])
        rs2_sb = sb("rs2_sb", [128, QT])

        ps = ctx.enter_context(nc.psum_tensor("ps", [128, 8 * CT], fp32))

        def bank(k, a=0, b=CT, rows=slice(0, 128)):
            return ps[rows, k * CT + a:k * CT + b]

        DU_BANK = [2, 6]
        XPROJ_BANK = [4, 6]
        B_BANK, C_BANK = [0, 2, 6, 6], [4, 4, 6, 6]
        IN_BANK = [0, 1, 3, 2, 0, 5, 5, 5]
        X_ORDER = [1, 0, 3, 2]
        SILU_ORDER = [0, 1, 3, 2]
        def banks(k, n, rows=slice(0, 128)):
            return ps[rows, k * CT:(k + n) * CT].rearrange("p (w t) -> p w t", w=n)

        OPROJ_BANK = [7, 6]
        ROW_BANK = [4, 0]
        MEANSQ = [4, 5, 4, 2, 7, 7, 6, 7, 1, 0]

        loaded = sem("loaded")
        rest_loaded = sem("rest_loaded")
        consts_loaded = sem("consts_loaded")
        x_loaded = sem("x_loaded")
        out_free = sem("out_free")
        setup_dve = sem("setup_dve")
        setup_pool = sem("setup_pool")
        setup_pad = sem("setup_pad")
        S = {name: sem(name) for name in SIGNALS}

        def twice(tile):
            return tile.rearrange("p (w t) -> p w t", w=1).to_broadcast([128, 2, CT])

        def turns(b):
            return lambda name, k: b * SIGNALS[name] + k

        def stack_target(u):
            c, m, pair = stack_unit(u)
            at = slice(c * CT, (c + 1) * CT)
            return kstack[0:96, m, :, at] if pair == 0 else qstack[0:96, m, 2 * pair - 2:2 * pair, at]

        block = ctx.enter_context(nc.Block())
        N_SETUP_DVE = 3

        @block.sync
        def _(sp):
            sp.dma_start(x_sb[:, :], x[:, 0:SEQ]).then_inc(x_loaded, 16)
            sp.dma_start(c_sb[:, :], cst).then_inc(consts_loaded, 16)
            sp.dma_start(w_sb[:, 0:W_FIRST], wts[:, 0:W_FIRST]).then_inc(loaded, 16)
            sp.dma_start(convw_sb[:, :, :].rearrange("p j d -> p (j d)"),
                         convw.to_broadcast([128, DCONV * DI])).then_inc(loaded, 16)
            sp.dma_start(b2_sb[:, :], b2).then_inc(out_free, 16)
            sp.dma_start(w_sb[:, W_FIRST:], wts[:, W_FIRST:]).then_inc(rest_loaded, 16)
            for b in range(BATCH):
                n = (b + 1) % BATCH
                sp.wait_ge(S["sum_ready"], NC * (b + 1))
                sp.dma_start(x_sb[:, :], x[:, n * SEQ:(n + 1) * SEQ]).then_inc(x_loaded, 16)
                for c in range(NC):
                    sp.wait_ge(S["out_ready"], NC * b + c + 1)
                    sp.dma_start(out[:, b * QT + 4 * c:b * QT + 4 * c + 4, :],
                                 out_sb[:, 4 * c:4 * c + 4, :]).then_inc(out_free, 16)
            sp.wait_ge(out_free, 16 + 16 * NC * BATCH)

        @block.gpsimd
        def _(pool):
            nc.gpsimd.memset(xn_sb[:, 0:DCONV - 1], 0.0)
            nc.gpsimd.memset(eps_sb[:, 0:1], EPS_RMS)
            nc.gpsimd.memset(eps_sb[:, 1:2], EPS_LN).then_inc(setup_pool, 1)
            pool.wait_ge(loaded, 32)
            nc.gpsimd.tensor_scalar(wbc_sb[:, :, :, :],
                                    W("xp").rearrange("p (h n) -> p h n", h=NH)[:, :, 0:32]
                                    .rearrange("p h (a n) -> p h a n", a=1).to_broadcast([128, NH, 3, 32]),
                                    0.5, 1.0, ALU.mult, ALU.mult)
            for h in range(NH):
                nc.gpsimd.tensor_scalar(wdt_sb[:, h, :], W("xp", 33 * h + 32, 33 * h + 33).to_broadcast([128, 128]),
                                        0.5, 1.0, ALU.mult, ALU.mult)
            nc.gpsimd.tensor_scalar(dskh_sb[:, :], W("dsk"), 0.5, 1.0, ALU.mult, ALU.mult)
            pool.wait_ge(consts_loaded, 16)
            for n, scale in ((0, 0.5), (1, 1.0)):
                last = nc.gpsimd.tensor_scalar(selbc_sb[:, 16 * n:16 * n + 16, :],
                                               C("sum")[:, 16 * n:16 * n + 16].rearrange("p (n a) -> p n a", a=1)
                                               .to_broadcast([128, 16, 32]), scale, 1.0, ALU.mult, ALU.mult)
            last.then_inc(setup_pool, 1)
            pool.wait_ge(rest_loaded, 16)
            pool.wait_ge(consts_loaded, 16)
            nc.gpsimd.tensor_scalar(wout_sb[:, :, :].rearrange("p h n -> p (h n)"), W("out"), 0.5, 1.0, ALU.mult,
                                    ALU.mult)
            nc.gpsimd.tensor_scalar(wq_sb[:, :], W("q"), W("na"), float(HD) ** -0.5, ALU.mult, ALU.mult)
            nc.gpsimd.tensor_scalar(wk_sb[:, :, :].rearrange("p (k r) d -> p k r d", k=KV),
                                    W("k").rearrange("p (k a d) -> p k a d", k=KV, a=1)
                                    .to_broadcast([128, KV, HEADS // KV, HD]), W("na"), 1.0, ALU.mult, ALU.mult)
            nc.gpsimd.tensor_scalar(wv_sb[:, :], W("v"), W("na"), 1.0, ALU.mult, ALU.mult)
            nc.gpsimd.tensor_scalar(wgate_sb[:, :], W("gate"), W("nf"), 1.0, ALU.mult, ALU.mult)
            nc.gpsimd.tensor_scalar(wup_sb[:, :], W("up"), W("nf"), 1.0, ALU.mult, ALU.mult)
            nc.gpsimd.tensor_scalar(wdown_sb[:, :, :].rearrange("p h n -> p (h n)"), W("down"), 0.5, 1.0, ALU.mult,
                                    ALU.mult)
            nc.gpsimd.tensor_copy(identb[:, :], C("ident"))
            nc.gpsimd.tensor_copy(maskb[:, :], C("mask")).then_inc(setup_pool, 1)
            with pool.Fori(0, BATCH) as b:
                count = turns(b)
                pool.wait_ge(S["resid_ready"], count("resid_ready", 2))
                pool.wait_ge(S["relulog_ready"], count("relulog_ready", 2))
                nc.gpsimd.tensor_tensor(delta_sb[:, 1, :, :], delta_sb[:, 1, :, :], u_sb[:, 1, :, :],
                                        ALU.subtract).then_inc(S["delta1_ready"], 1)
                pool.wait_ge(S["delta1_ready"], count("delta1_ready", 1))
                nc.gpsimd.tensor_tensor(du_sb[:, 1, :, :], delta_sb[:, 1, :, :], xs_sb[:, 1, :, :],
                                        ALU.mult).then_inc(S["du1_ready"], 1)
                for k in range(32):
                    _, c, ng, _ = scan_tile(2 * k)
                    pool.wait_ge(S["state_ready"], count("state_ready", 2 * k + 2))
                    if k in (0, 2):
                        pool.wait_ge(S["crep0_stored"], count("crep0_stored", 1 + k // 2))
                    if k == 4:
                        pool.wait_ge(S["crep1_stored"], count("crep1_stored", 2))
                    if k >= 2:
                        pool.wait_ge(S["hc_summed"], count("hc_summed", 2 * k - 2))
                    st, slot = 2 * k % NST, 2 * k % NHC
                    nc.gpsimd.tensor_tensor(hc_sb[:, slot:slot + 2, :], state_sb[:, st:st + 2, :],
                                            twice(crep_sb[:, c, ng, :]), ALU.mult).then_inc(S["hc_ready"], 1)
                for c in range(NC):
                    at = slice(c * CT, (c + 1) * CT)
                    pool.wait_ge(S["part2_ready"], count("part2_ready", c + 1))
                    nc.gpsimd.tensor_tensor(part_sb[2][:, :, at], rest_sb[:, c, :, :], part_sb[1][:, :, at],
                                            ALU.subtract).then_inc(S["part3_ready"], 1)
                for c in range(NC):
                    pool.wait_ge(S["ln1_ready"], count("ln1_ready", c + 1))
                    nc.gpsimd.tensor_tensor(s_sb[:, c, :], ln1_sb[:, c, :], b2_sb[:, :].to_broadcast([128, CT]),
                                            ALU.add).then_inc(S["ln1bias_ready"], 1)

        @block.scalar
        def _(act):
            act.wait_ge(setup_pool, 1)

            def squares(src, k):
                nc.scalar.activation(sq_sb[:, k % 2, :], src, ACT.Square).then_inc(S["square_ready"], 1)

            def rstd(count, k, eps):
                act.wait_ge(S["meansq_ready"], count("meansq_ready", k + 1))
                nc.scalar.activation(log_sb[:, k % 2, :], bank(MEANSQ[k]), ACT.Ln,
                                     bias=eps_sb[:, eps:eps + 1]).then_inc(S["log_ready"], 1)
                act.wait_ge(S["log_ready"], count("log_ready", k + 1))
                nc.scalar.activation(rstd_sb[:, k % 2, :], log_sb[:, k % 2, :], ACT.Exp,
                                     scale=-0.5).then_inc(S["rstd_ready"], 1)

            def first_squares(x_loads, k):
                act.wait_ge(x_loaded, x_loads)
                for c in range(NC):
                    squares(x_sb[:, c * CT:(c + 1) * CT], k + c)

            act.preload_act_table_set(LN_EXP)
            first_squares(16, 0)
            for c in range(NC):
                rstd(turns(0), c, 0)
            with act.Fori(0, BATCH) as b:
                count = turns(b)
                act.wait_ge(loaded, 32)
                nc.scalar.activation(a_sb[:, :], W("alog"), ACT.Exp).then_inc(S["a_ready"], 1)
                act.preload_act_table_set("exp_and_others")
                act.wait_ge(setup_dve, N_SETUP_DVE)
                def tanh_x(n):
                    u = SILU_ORDER[n]
                    if u % 2:
                        act.wait_ge(S["tap_ready"], count("tap_ready", DCONV * (u // 2 + 1)))
                        nc.scalar.activation(th_sb[:, u, :], v_sb[:, u, :], ACT.Tanh,
                                             scale=0.5).then_inc(S["tanh_ready"], 1)
                    else:
                        act.wait_ge(S["inproj_ready"], count("inproj_ready", u + 2))
                        nc.scalar.activation(v_sb[:, u, :], bank(IN_BANK[u]), ACT.Identity, bias=W("cb", 0, 1))
                        nc.scalar.activation(th_sb[:, u, :], bank(IN_BANK[u]), ACT.Tanh, scale=0.5,
                                             bias=cbh_sb[:, 0:1]).then_inc(S["tanh_ready"], 1)

                def tanh_z(u):
                    act.wait_ge(S["inproj_ready"], count("inproj_ready", u + 1))
                    nc.scalar.activation(zs_sb[:, u // 2 - 2, u % 2, :], bank(IN_BANK[u]), ACT.Tanh,
                                         scale=0.5).then_inc(S["tanh_ready"], 1)

                def bc_part1(c):
                    act.wait_ge(S["bcraw_ready"], count("bcraw_ready", c + 1))
                    nc.scalar.activation(bc1_sb[0:96, c, :], bank(XPROJ_BANK[c], rows=slice(0, 96)),
                                         ACT.Copy).then_inc(S["bc1_ready"], 1)

                def bc_part2(c):
                    act.wait_ge(S["bcrest_ready"], count("bcrest_ready", c + 1))
                    nc.scalar.activation(bc2_sb[0:96, c, :], bcrest_sb[0:96, c, :],
                                         ACT.Copy).then_inc(S["bc2_ready"], 1)

                def abs_exp(c):
                    act.wait_ge(S["dtraw_ready"], count("dtraw_ready", c + 1))
                    for h in range(NH):
                        last = nc.scalar.activation(l_sb[:, c, h, :], bank(XPROJ_BANK[c] + 1), ACT.Abs,
                                                    scale=W("dtw", h, h + 1), bias=W("dtb", h, h + 1))
                    last.then_inc(S["abs_ready"], 1)
                    act.wait_ge(S["abs_ready"], count("abs_ready", c + 1))
                    nc.scalar.activation(e_sb[:, c, :, :], l_sb[:, c, :, :], ACT.Exp,
                                         scale=-1.0).then_inc(S["expabs_ready"], 1)

                def log1p(c):
                    act.wait_ge(S["expabs_ready"], count("expabs_ready", c + 1))
                    nc.scalar.activation(l_sb[:, c, :, :], e_sb[:, c, :, :], ACT.Ln,
                                         bias=C("ones")[:, 0:1]).then_inc(S["log1p_ready"], 1)

                def store_b(k):
                    c, g = k // 2, 2 * (k % 2)
                    act.wait_ge(S["brep_ready"], count("brep_ready", k + 1))
                    nc.scalar.activation(brep_sb[:, c, g:g + 2, :], banks(B_BANK[k], 2),
                                         ACT.Copy).then_inc(S["brep_stored"], 1)

                def store_c1(k):
                    act.wait_ge(S["crep_ready"], count("crep_ready", k + 1))
                    nc.scalar.activation(crep_sb[:, 1, 2 * (k % 2):2 * (k % 2) + 2, :], banks(C_BANK[k], 2),
                                         ACT.Copy).then_inc(S["crep1_stored"], 1)

                for n in range(2):
                    tanh_x(n)
                act.wait_ge(consts_loaded, 16)
                abs_exp(0)
                tanh_x(2)
                tanh_x(3)
                tanh_z(4)
                act.preload_act_table_set(LN_EXP)
                bc_part1(0)
                log1p(0)
                bc_part2(0)
                abs_exp(1)
                bc_part1(1)
                log1p(1)
                store_b(0)
                store_b(1)
                bc_part2(1)
                act.preload_act_table_set("exp_and_others")
                act.wait_ge(out_free, 16 * NC * b + 16)
                act.wait_ge(S["nega_ready"], count("nega_ready", 1))
                for i in range(64):
                    pr, c, ng, s = scan_tile(i)
                    if ng == 0:
                        act.wait_ge(S["drep_ready"], count("drep_ready", i // 8 + 1))
                    if i >= NDEC:
                        act.wait_ge(S["state_ready"], count("state_ready", i - NDEC + 1))
                    col = (2 * pr + s) * NG + ng
                    nc.scalar.activation(decay_sb[:, i % NDEC, :], bank(s), ACT.Exp,
                                         scale=nega_sb[:, col:col + 1]).then_inc(S["decay_ready"], 1)
                    if i == 1:
                        store_b(2)
                        tanh_z(5)
                        store_c1(2)
                    if i == 3:
                        store_b(3)
                        store_c1(3)
                    if i == 9:
                        tanh_z(6)
                    if i == 16:
                        tanh_z(7)
                        act.preload_act_table_set(LN_EXP)
                def part1(c):
                    act.wait_ge(S["qk_ready"], count("qk_ready", c + 1))
                    nc.scalar.activation(part_sb[0][:, :, c * CT:(c + 1) * CT], banks(2 * c, 2),
                                         ACT.Copy).then_inc(S["part1_ready"], 1)

                def part2(c):
                    act.wait_ge(S["rest1_ready"], count("rest1_ready", c + 1))
                    nc.scalar.activation(part_sb[1][:, :, c * CT:(c + 1) * CT], rest_sb[:, c, :, :],
                                         ACT.Copy).then_inc(S["part2_ready"], 1)

                def store_stack(u):
                    act.wait_ge(S["stack_ready"], count("stack_ready", u + 1))
                    nc.scalar.activation(stack_target(u), banks(4 + 2 * (u % 2), 2, rows=slice(0, 96)),
                                         ACT.Copy).then_inc(S["stack_a_stored"], 1)

                act.wait_ge(S["h1_ready"], count("h1_ready", 1))
                squares(h1_sb[:, 0:CT], 2)
                rstd(count, 2, 0)
                part1(0)
                part2(0)
                act.wait_ge(S["h1_ready"], count("h1_ready", 2))
                squares(h1_sb[:, CT:], 3)
                store_stack(0)
                rstd(count, 3, 0)
                store_stack(2)
                part1(1)
                store_stack(3)
                part2(1)
                for u in (5, 6, 8, 9, 10, 11):
                    store_stack(u)

                def max_rows(c):
                    act.wait_ge(S["scores_ready"], count("scores_ready", 19 + 15 * c))
                    nc.scalar.activation(qstack[96:98, 0, 0:2, c * CT:(c + 1) * CT],
                                         banks(ROW_BANK[c], 2, rows=slice(96, 98)), ACT.Copy).then_inc(S["maxrow_a_stored"], 1)

                def exponential(v):
                    c, j, h, q0 = st_unit(v)
                    act.wait_ge(S["scorest_ready"], count("scorest_ready", v + 1))
                    if v >= 8:
                        act.wait_ge(S["pv_ready"], count("pv_ready", v // 4 - 1))
                    if v >= 24:
                        act.wait_ge(S["probsum_ready"], count("probsum_ready", v // 4 - 5))
                    nc.scalar.activation(pt_sb[:, v // 4 % 2, h, q0:CT], bank(st_bank(v), q0, CT),
                                         ACT.Exp).then_inc(S["probs_ready"], 1)

                def inverse_sum(c):
                    if c == 0:
                        act.wait_ge(S["pv_ready"], count("pv_ready", 4))
                    else:
                        act.wait_ge(S["den_ready"], count("den_ready", 1))
                    nc.scalar.activation(log_sb[:, c, :], bank(7), ACT.Ln).then_inc(S["logden_ready"], 1)
                    act.wait_ge(S["logden_ready"], count("logden_ready", c + 1))
                    nc.scalar.activation(rden_sb[:, c, :], log_sb[:, c, :], ACT.Exp,
                                         scale=-1.0).then_inc(S["rden_ready"], 1)

                max_rows(0)
                for v in range(16):
                    exponential(v)
                max_rows(1)
                inverse_sum(0)
                def swiglu_squares(c):
                    act.wait_ge(S["h2_ready"], count("h2_ready", c + 1))
                    squares(h2_sb[:, c * CT:(c + 1) * CT], 4 + c)

                for v in range(16, 48):
                    exponential(v)
                    if v == 27:
                        swiglu_squares(0)
                    if v == 35:
                        rstd(count, 4, 0)
                inverse_sum(1)

                def gate_tanh(u):
                    rows = slice(0, FM[u % 3])
                    act.wait_ge(S["gateup_ready"], count("gateup_ready", u + 1))
                    if u >= 4:
                        act.wait_ge(S["gsilu_ready"], count("gsilu_ready", u - 3))
                    nc.scalar.activation(th_sb[rows, u % 4, :], bank(2 * (u % 3), rows=rows), ACT.Tanh,
                                         scale=0.5).then_inc(S["gtanh_ready"], 1)

                act.preload_act_table_set("exp_and_others")
                gate_tanh(0)
                swiglu_squares(1)
                gate_tanh(1)
                act.preload_act_table_set(LN_EXP)
                rstd(count, 5, 0)
                act.preload_act_table_set("exp_and_others")
                for u in range(2, 6):
                    gate_tanh(u)
                act.preload_act_table_set(LN_EXP)
                for c in range(NC):
                    act.wait_ge(S["centered_ready"], count("centered_ready", c + 1))
                    squares(bank(c), 6 + c)
                    rstd(count, 6 + c, 1)
                for u in range(8):
                    m = u % MM
                    if u == 4:
                        first_squares(16 * b + 32, 8)
                    act.wait_ge(S["mlp_ready"], count("mlp_ready", u + 1))
                    nc.scalar.activation(gelu_sb[:, u // MM, m, :], bank(2 + u % 4), ACT.Gelu,
                                         bias=W("b1", m, m + 1)).then_inc(S["gelu_ready"], 1)
                act.preload_act_table_set(LN_EXP)
                for c in range(NC):
                    rstd(count, 8 + c, 0)
                for c in range(NC):
                    tiles = slice(4 * c, 4 * c + 4)
                    act.wait_ge(S["meanvar_ready"], count("meanvar_ready", 4 * c + 4))
                    nc.scalar.activation(lv_sb[:, tiles], mv_sb[:, tiles, 1], ACT.Ln,
                                         bias=eps_sb[:, 1:2]).then_inc(S["logvar_ready"], 1)
                    act.wait_ge(S["logvar_ready"], count("logvar_ready", c + 1))
                    nc.scalar.activation(rs2_sb[:, tiles], lv_sb[:, tiles], ACT.Exp,
                                         scale=-0.5).then_inc(S["rstd2_ready"], 1)

        @block.vector
        def _(dve):
            nc.vector.memset(kstack[96:128, 0, :, :], 0.0).then_inc(setup_pad, 1)
            dve.wait_ge(setup_pad, 1)
            nc.vector.memset(kstack[96:98, 0, :, :], 1.0)
            dve.wait_ge(loaded, 32)
            nc.vector.tensor_scalar(win_sb[:, :], W("in"), W("nm"), None, ALU.mult).then_inc(setup_dve, 1)
            nc.vector.tensor_scalar(cbh_sb[:, :], W("cb"), 0.5, None, ALU.mult).then_inc(setup_dve, 1)
            dve.wait_ge(setup_dve, 2)
            for j in range(DCONV):
                last = nc.vector.tensor_tensor(wconv_sb[:, j, :], win_sb[:, 0:128], convw_sb[:, j, 0:128], ALU.mult)
            last.then_inc(setup_dve, 1)
            assert N_SETUP_DVE == 3

            def first_norm(count, x_loads, k):
                dve.wait_ge(x_loaded, x_loads)
                for c in range(NC):
                    dve.wait_ge(S["rstd_ready"], count("rstd_ready", k + c + 1))
                    nc.vector.tensor_tensor(xn_sb[:, DCONV - 1 + c * CT:DCONV - 1 + (c + 1) * CT],
                                            x_sb[:, c * CT:(c + 1) * CT], rstd_sb[:, c, :],
                                            ALU.mult).then_inc(S["xn_ready"], 1)

            first_norm(turns(0), 16, 0)
            with dve.Fori(0, BATCH) as b:
                count = turns(b)
                dve.wait_ge(setup_pool, 2)
                def convolve(c, taps):
                    for j in taps:
                        back = DCONV - 1 - j
                        lo = back if c == 0 else 0
                        v = v_sb[:, 2 * c + 1, lo:CT]
                        at = IN_BANK[2 * c + 1] * CT
                        raw = ps[:, at + lo - back:at + CT - back]
                        if back == 0:
                            dve.wait_ge(S["inproj_ready"], count("inproj_ready", 2 * c + 1))
                            nc.vector.tensor_scalar(v, raw, W("taps", j, j + 1), W("cb", 1, 2), ALU.mult,
                                                    ALU.add).then_inc(S["tap_ready"], 1)
                        else:
                            dve.wait_ge(S["tap_ready"], count("tap_ready", DCONV * c + back))
                            nc.vector.scalar_tensor_tensor(out=v, in0=raw, scalar=W("taps", j, j + 1), in1=v,
                                                           op0=ALU.mult, op1=ALU.add).then_inc(S["tap_ready"], 1)

                def gate_x(n):
                    u = SILU_ORDER[n]
                    dve.wait_ge(S["tanh_ready"], count("tanh_ready", n + 1))
                    nc.vector.scalar_tensor_tensor(out=xs_sb[:, u // 2, u % 2, :], in0=th_sb[:, u, :], scalar=1.0,
                                                   in1=v_sb[:, u, :], op0=ALU.add,
                                                   op1=ALU.mult).then_inc(S["gated_ready"], 1)

                def gate_z(u):
                    dve.wait_ge(S["tanh_ready"], count("tanh_ready", u + 1))
                    zs = zs_sb[:, u // 2 - 2, u % 2, :]
                    nc.vector.scalar_tensor_tensor(out=zs, in0=zs, scalar=1.0, in1=bank(IN_BANK[u]), op0=ALU.add,
                                                   op1=ALU.mult).then_inc(S["gated_ready"], 1)

                def dt(c):
                    dve.wait_ge(S["abs_ready"], count("abs_ready", c + 1))
                    for h in range(NH):
                        nc.vector.tensor_scalar(dt_sb[:, c, h, :], bank(XPROJ_BANK[c] + 1), W("dtw", h, h + 1),
                                                W("dtb", h, h + 1), ALU.mult, ALU.add).then_inc(S["dtpre_ready"], 1)

                def bc_rest(c):
                    dve.wait_ge(S["bc1_ready"], count("bc1_ready", c + 1))
                    nc.vector.scalar_tensor_tensor(out=bcrest_sb[0:96, c, :], in0=bc1_sb[0:96, c, :],
                                                   scalar=C("less1")[0:96, :],
                                                   in1=bank(XPROJ_BANK[c], rows=slice(0, 96)), op0=ALU.mult,
                                                   op1=ALU.add).then_inc(S["bcrest_ready"], 1)

                def bc_parts(c):
                    dve.wait_ge(S["bc2_ready"], count("bc2_ready", c + 1))
                    nc.vector.scalar_tensor_tensor(out=bc_sb[0:96, c, :], in0=bc2_sb[0:96, c, :],
                                                   scalar=C("less2")[0:96, :], in1=bcrest_sb[0:96, c, :],
                                                   op0=ALU.mult, op1=ALU.add).then_inc(S["bcparts_ready"], 1)

                def store_c0(k):
                    dve.wait_ge(S["crep_ready"], count("crep_ready", k + 1))
                    nc.vector.tensor_copy(crep_sb[:, 0, 2 * k:2 * k + 2, :],
                                          banks(C_BANK[k], 2)).then_inc(S["crep0_stored"], 1)

                def round_u(c):
                    dve.wait_ge(S["expabs_ready"], count("expabs_ready", c + 1))
                    nc.vector.tensor_scalar(u_sb[:, c, :, :], e_sb[:, c, :, :], 1.0, None,
                                            ALU.add).then_inc(S["u_ready"], 1)

                def residue(c):
                    dve.wait_ge(S["u_ready"], count("u_ready", c + 1))
                    nc.vector.scalar_tensor_tensor(out=u_sb[:, c, :, :], in0=u_sb[:, c, :, :], scalar=-1.0,
                                                   in1=e_sb[:, c, :, :], op0=ALU.add,
                                                   op1=ALU.subtract).then_inc(S["resid_ready"], 1)

                def relu_log(c):
                    dve.wait_ge(S["dtpre_ready"], count("dtpre_ready", 2 * c + 2))
                    dve.wait_ge(S["log1p_ready"], count("log1p_ready", c + 1))
                    nc.vector.scalar_tensor_tensor(out=delta_sb[:, c, :, :], in0=dt_sb[:, c, :, :], scalar=0.0,
                                                   in1=l_sb[:, c, :, :], op0=ALU.max,
                                                   op1=ALU.add).then_inc(S["relulog_ready"], 1)

                dve.wait_ge(S["a_ready"], count("a_ready", 1))
                nc.vector.tensor_scalar(nega_sb[:, :], a_sb[:, :], -1.0, None, ALU.mult).then_inc(S["nega_ready"], 1)
                convolve(0, (3, 2, 1, 0))
                gate_x(0)
                gate_x(1)
                convolve(1, (3, 2, 1, 0))
                dt(0)
                round_u(0)
                gate_x(2)
                residue(0)
                gate_x(3)
                gate_z(4)
                bc_rest(0)
                relu_log(0)
                bc_parts(0)
                dve.wait_ge(S["relulog_ready"], count("relulog_ready", 1))
                nc.vector.tensor_tensor(delta_sb[:, 0, :, :], delta_sb[:, 0, :, :], u_sb[:, 0, :, :],
                                        ALU.subtract).then_inc(S["delta0_ready"], 1)
                dve.wait_ge(S["delta0_ready"], count("delta0_ready", 1))
                nc.vector.tensor_tensor(du_sb[:, 0, :, :], delta_sb[:, 0, :, :], xs_sb[:, 0, :, :],
                                        ALU.mult).then_inc(S["du0_ready"], 1)
                store_c0(0)
                bc_rest(1)
                dt(1)
                round_u(1)
                relu_log(1)
                residue(1)
                store_c0(1)
                bc_parts(1)

                def drive(k):
                    _, c, ng, _ = scan_tile(2 * k)
                    if ng == 0:
                        dve.wait_ge(S["durep_ready"], count("durep_ready", k // 4 + 1))
                    if k in (0, 4):
                        dve.wait_ge(S["brep_stored"], count("brep_stored", 2 * c + 2))
                    if k >= 2:
                        dve.wait_ge(S["state_ready"], count("state_ready", 2 * k - 2))
                    slot = 2 * k % NDRV
                    nc.vector.tensor_tensor(drive_sb[:, slot:slot + 2, :], banks(DU_BANK[k // 4 % 2], 2),
                                            twice(brep_sb[:, c, ng, :]), ALU.mult).then_inc(S["drive_ready"], 1)

                def finish_y(k):
                    h, c = k // NC, k % NC
                    dve.wait_ge(S["hc_summed"], count("hc_summed", 32 * h + 8 * c + 24))
                    nc.vector.scalar_tensor_tensor(out=y_sb[:, c, h, :], in0=xs_sb[:, c, h, :],
                                                   scalar=dskh_sb[:, h:h + 1], in1=bank(4 + c), op0=ALU.mult,
                                                   op1=ALU.add).then_inc(S["yskip_ready"], 1)
                    dve.wait_ge(S["yskip_ready"], count("yskip_ready", k + 1))
                    nc.vector.tensor_tensor(y_sb[:, c, h, :], y_sb[:, c, h, :], zs_sb[:, c, h, :],
                                            ALU.mult).then_inc(S["y_ready"], 1)

                def add_mamba(c):
                    dve.wait_ge(S["outproj_ready"], count("outproj_ready", c + 1))
                    nc.vector.tensor_tensor(h1_sb[:, c * CT:(c + 1) * CT], x_sb[:, c * CT:(c + 1) * CT], bank(2 + c),
                                            ALU.add).then_inc(S["h1_ready"], 1)

                drive(0)
                for i in range(64):
                    _, c, _, _ = scan_tile(i)
                    if i % 2 == 0 and i + 2 < 64:
                        drive(i // 2 + 1)
                    dve.wait_ge(S["decay_ready"], count("decay_ready", i + 1))
                    if i % 2 == 0:
                        dve.wait_ge(S["drive_ready"], count("drive_ready", i // 2 + 1))
                    if i >= NST and i % 2 == 0:
                        dve.wait_ge(S["hc_ready"], count("hc_ready", (i - NST) // 2 + 1))
                    first = 0.0
                    if c:
                        dve.wait_ge(S["state_ready"], count("state_ready", i - 7))
                        first = state_sb[:, (i - 8) % NST, CT - 1:CT]
                    nc.vector.tensor_tensor_scan(state_sb[:, i % NST, :], decay_sb[:, i % NDEC, :],
                                                 drive_sb[:, i % NDRV, :], first,
                                                 ALU.mult, ALU.add).then_inc(S["state_ready"], 1)
                    if i in (2, 9, 14):
                        gate_z(5 + (2, 9, 14).index(i))
                    if i in (29, 37, 59):
                        finish_y((29, 37, 59).index(i))
                    if i == 61:
                        add_mamba(0)
                def attention_norm(c):
                    dve.wait_ge(S["rstd_ready"], count("rstd_ready", 2 + c + 1))
                    nc.vector.tensor_tensor(xn2_sb[:, c * CT:(c + 1) * CT], h1_sb[:, c * CT:(c + 1) * CT],
                                            rstd_sb[:, c, :], ALU.mult).then_inc(S["xn2_ready"], 1)

                def rest(c):
                    dve.wait_ge(S["part1_ready"], count("part1_ready", c + 1))
                    nc.vector.tensor_tensor(rest_sb[:, c, :, :], banks(2 * c, 2),
                                            part_sb[0][:, :, c * CT:(c + 1) * CT],
                                            ALU.subtract).then_inc(S["rest1_ready"], 1)

                def store_stack(u):
                    dve.wait_ge(S["stack_ready"], count("stack_ready", u + 1))
                    nc.vector.tensor_copy(stack_target(u), banks(4 + 2 * (u % 2), 2, rows=slice(0, 96))
                                          ).then_inc(S["stack_b_stored"], 1)

                attention_norm(0)
                finish_y(3)
                nc.vector.memset(qstack[96:128, 0, :, :], 0.0).then_inc(S["pad_ready"], 1)
                rest(0)
                add_mamba(1)
                store_stack(1)
                attention_norm(1)

                def max_parts(c):
                    m = negmax_sb[:, 16 * c:16 * c + 16]
                    dve.wait_ge(S["max_ready"], count("max_ready", 16 * c + 16))
                    nc.vector.tensor_copy(maxpart_sb[:, c, :, 0], m).then_inc(S["maxpart_ready"], 1)
                    dve.wait_ge(S["maxpart_ready"], count("maxpart_ready", 2 * c + 1))
                    nc.vector.tensor_tensor(maxpart_sb[:, c, :, 1], m, maxpart_sb[:, c, :, 0],
                                            ALU.subtract).then_inc(S["maxpart_ready"], 1)

                def max_rows(c):
                    dve.wait_ge(S["scores_ready"], count("scores_ready", 19 + 15 * c))
                    nc.vector.tensor_copy(qstack[96:98, 0, 2:4, c * CT:(c + 1) * CT],
                                          banks(ROW_BANK[c] + 2, 2, rows=slice(96, 98))
                                          ).then_inc(S["maxrow_b_stored"], 1)

                def weighted_values(c):
                    dve.wait_ge(S["rden_ready"], count("rden_ready", c + 1))
                    nc.vector.tensor_tensor(attn_sb[:, c * CT:(c + 1) * CT], rden_sb[:, c, :], bank(6),
                                            ALU.mult).then_inc(S["attn_stored"], 1)

                for n in range(QT * HEADS):
                    K = (n // HEADS + 1) * 128
                    dve.wait_ge(S["scores_ready"], count("scores_ready", n + n // 18 + 1))
                    nc.vector.tensor_reduce(negmax_sb[:, n:n + 1], ps[:, scores_bank(n) * CT:scores_bank(n) * CT + K], AX.X,
                                            ALU.max, negate=True).then_inc(S["max_ready"], 1)
                    if n in (4, 7):
                        store_stack(n)
                    if n == 3:
                        rest(1)
                    if n == 14:
                        dve.wait_ge(S["v_ready"], count("v_ready", 1))
                        nc.vector.tensor_copy(vt_sb[:, :, :].rearrange("p a n -> p (a n)"),
                                              bank(4)).then_inc(S["v_stored"], 1)
                    if n % 16 == 15:
                        max_parts(n // 16)
                    if n == 16:
                        max_rows(0)
                max_rows(1)
                def add_attention(c):
                    dve.wait_ge(S["oproj_ready"], count("oproj_ready", c + 1))
                    nc.vector.tensor_tensor(h2_sb[:, c * CT:(c + 1) * CT], h1_sb[:, c * CT:(c + 1) * CT],
                                            bank(OPROJ_BANK[c]), ALU.add).then_inc(S["h2_ready"], 1)

                def swiglu_norm(c):
                    dve.wait_ge(S["rstd_ready"], count("rstd_ready", 4 + c + 1))
                    nc.vector.tensor_tensor(xn2_sb[:, c * CT:(c + 1) * CT], h2_sb[:, c * CT:(c + 1) * CT],
                                            rstd_sb[:, c, :], ALU.mult).then_inc(S["xn3_ready"], 1)

                def swiglu(u):
                    c, m = u // 3, u % 3
                    rows = slice(0, FM[m])
                    dve.wait_ge(S["gtanh_ready"], count("gtanh_ready", u + 1))
                    nc.vector.scalar_tensor_tensor(out=v_sb[rows, u % 4, :], in0=th_sb[rows, u % 4, :], scalar=1.0,
                                                   in1=bank(2 * (u % 3), rows=rows), op0=ALU.add,
                                                   op1=ALU.mult).then_inc(S["gsilu_ready"], 1)
                    dve.wait_ge(S["gsilu_ready"], count("gsilu_ready", u + 1))
                    nc.vector.tensor_tensor(swi_sb[rows, c, m, :], v_sb[rows, u % 4, :],
                                            bank(2 * (u % 3) + 1, rows=rows), ALU.mult).then_inc(S["swiglu_ready"], 1)

                def add_residuals(c):
                    dve.wait_ge(S["down_ready"], count("down_ready", c + 1))
                    nc.vector.tensor_tensor(s_sb[:, c, :], h2_sb[:, c * CT:(c + 1) * CT], bank(6 + c),
                                            ALU.add).then_inc(S["h3_ready"], 1)
                    dve.wait_ge(S["h3_ready"], count("h3_ready", c + 1))
                    nc.vector.tensor_tensor(s_sb[:, c, :], s_sb[:, c, :], x_sb[:, c * CT:(c + 1) * CT],
                                            ALU.add).then_inc(S["sum_ready"], 1)

                weighted_values(0)
                for g in range(4, 12):
                    _, _, _, q0 = st_unit(4 * g)
                    probs = pt_sb[:, g % 2, :, q0:CT]
                    dve.wait_ge(S["probs_ready"], count("probs_ready", 4 * g + 4))
                    if g == 4:
                        nc.vector.tensor_copy(probsum_sb[:, :, :], probs).then_inc(S["probsum_ready"], 1)
                    else:
                        dve.wait_ge(S["probsum_ready"], count("probsum_ready", g - 4))
                        nc.vector.tensor_tensor(probsum_sb[:, :, q0:CT], probsum_sb[:, :, q0:CT], probs,
                                                ALU.add).then_inc(S["probsum_ready"], 1)
                    if g == 5:
                        add_attention(0)
                    if g == 9:
                        swiglu_norm(0)
                weighted_values(1)
                add_attention(1)
                for u in range(6):
                    if u == 2:
                        swiglu_norm(1)
                    if u == 4:
                        add_residuals(0)
                    swiglu(u)
                add_residuals(1)
                for c in range(NC):
                    dve.wait_ge(S["rstd_ready"], count("rstd_ready", 6 + c + 1))
                    nc.vector.tensor_tensor(ln1_sb[:, c, :], rstd_sb[:, c, :], bank(c),
                                            ALU.mult).then_inc(S["ln1_ready"], 1)
                first_norm(count, 16 * b + 32, 8)
                for c in range(NC):
                    tiles = range(4 * c, 4 * c + 4)
                    for t in tiles:
                        dve.wait_ge(S["mlpout_ready"], count("mlpout_ready", c + 1))
                        nc.vector.bn_stats(stats_sb[:, t, :], bank(6 + c, (t % 4) * 128, (t % 4) * 128 + 128)
                                           ).then_inc(S["stats_ready"], 1)
                    dve.wait_ge(S["stats_ready"], count("stats_ready", 4 * c + 4))
                    nc.vector.memset(spare_sb[:, :], 0.0)
                    for t in tiles:
                        nc.vector.bn_aggr(mv_sb[:, t, :], stats_sb[:, t, :]).then_inc(S["meanvar_ready"], 1)
                    dve.wait_ge(S["rstd2_ready"], count("rstd2_ready", c + 1))
                    dve.wait_ge(S["meanvar_ready"], count("meanvar_ready", 4 * c + 4))
                    dve.wait_ge(out_free, 16 * NC * b + 16)
                    for t in tiles:
                        last = nc.vector.tensor_scalar(out_sb[:, t, :],
                                                       bank(6 + c, (t % 4) * 128, (t % 4) * 128 + 128),
                                                       mv_sb[:, t, 0:1], rs2_sb[:, t:t + 1], ALU.subtract, ALU.mult)
                    last.then_inc(S["out_ready"], 1)

        @block.tensor
        def _(pe):
            mm = nc.tensor.matmul

            def meansq(count, k):
                pe.wait_ge(S["square_ready"], count("square_ready", k + 1))
                mm(bank(MEANSQ[k]), C("mean"), sq_sb[:, k % 2, :], start=True,
                   stop=True).then_inc(S["meansq_ready"], 1)

            pe.wait_ge(consts_loaded, 16)
            for c in range(NC):
                meansq(turns(0), c)
            with pe.Fori(0, BATCH) as b:
                count = turns(b)
                pe.wait_ge(setup_dve, N_SETUP_DVE)
                def in_proj(u):
                    c, half = u // 2 % 2, u % 2
                    pe.wait_ge(S["xn_ready"], count("xn_ready", 1 if u == 1 else 2))
                    if u == 4:
                        pe.wait_ge(S["tanh_ready"], count("tanh_ready", 1))
                    if u == 5:
                        pe.wait_ge(S["crep0_stored"], count("crep0_stored", 2))
                    if u > 5:
                        pe.wait_ge(S["gated_ready"], count("gated_ready", u))
                    if u in (0, 2):
                        for j in range(DCONV):
                            last = mm(bank(IN_BANK[u]), wconv_sb[:, j, :], xn_sb[:, c * CT + j:c * CT + j + CT],
                                      start=(j == 0), stop=(j == DCONV - 1))
                    else:
                        at = 128 if u < 4 else DI + half * 128
                        last = mm(bank(IN_BANK[u]), win_sb[:, at:at + 128],
                                  xn_sb[:, DCONV - 1 + c * CT:DCONV - 1 + (c + 1) * CT], start=True, stop=True)
                    last.then_inc(S["inproj_ready"], 1)

                def x_proj_dt(c):
                    pe.wait_ge(S["gated_ready"], count("gated_ready", 2 * c + 2))
                    for h in range(NH):
                        last = mm(bank(XPROJ_BANK[c] + 1), wdt_sb[:, h, :], xs_sb[:, c, h, :], start=(h == 0),
                                  stop=(h == NH - 1))
                    last.then_inc(S["dtraw_ready"], 1)

                def x_proj_bc(c):
                    for h in range(NH):
                        last = mm(bank(XPROJ_BANK[c], rows=slice(0, 96)),
                                  wbc_sb[:, h, :, :].rearrange("p a n -> p (a n)"), xs_sb[:, c, h, :],
                                  start=(h == 0), stop=(h == NH - 1))
                    last.then_inc(S["bcraw_ready"], 1)

                def spread_b(k):
                    c = k // 2
                    if k == 0:
                        pe.wait_ge(S["gated_ready"], count("gated_ready", 5))
                    if k == 3:
                        pe.wait_ge(S["crep1_stored"], count("crep1_stored", 1))
                    if k % 2 == 0:
                        pe.wait_ge(S["bcparts_ready"], count("bcparts_ready", c + 1))
                    for w in range(2):
                        n = 4 * (2 * (k % 2) + w)
                        last = mm(bank(B_BANK[k] + w), selbc_sb[0:96, n:n + 4, :].rearrange("p n r -> p (n r)"),
                                  bc_sb[0:96, c, :], start=True, stop=True)
                    last.then_inc(S["brep_ready"], 1)

                def spread_c(k):
                    c = k // 2
                    if k == 0:
                        pe.wait_ge(S["dtpre_ready"], count("dtpre_ready", 2))
                    if k == 1:
                        pe.wait_ge(S["crep0_stored"], count("crep0_stored", 1))
                    if k >= 2:
                        pe.wait_ge(S["brep_stored"], count("brep_stored", k + 1))
                    for w in range(2):
                        n = 16 + 4 * (2 * (k % 2) + w)
                        last = mm(bank(C_BANK[k] + w), selbc_sb[0:96, n:n + 4, :].rearrange("p n r -> p (n r)"),
                                  bc_sb[0:96, c, :], start=True, stop=True)
                    last.then_inc(S["crep_ready"], 1)

                for n in range(3):
                    in_proj(X_ORDER[n])
                pe.wait_ge(setup_pool, 2)
                x_proj_dt(0)
                in_proj(X_ORDER[3])
                in_proj(4)
                x_proj_bc(0)
                x_proj_dt(1)
                x_proj_bc(1)
                spread_b(0)
                spread_b(1)
                spread_c(0)

                def spread(q, k, src, ready):
                    pr, c, _, _ = scan_tile(8 * q)
                    for s in range(2):
                        h, j = (2 * pr + s) // 4, (2 * pr + s) % 4
                        last = mm(bank(k + s), C("selD")[:, 128 * j:128 * j + 128], src[:, c, h, :], start=True,
                                  stop=True)
                    last.then_inc(S[ready], 1)

                def out_proj(c):
                    if c == 0:
                        pe.wait_ge(setup_pool, 3)
                        pe.wait_ge(S["drive_ready"], count("drive_ready", 28))
                    pe.wait_ge(S["y_ready"], count("y_ready", NC + c + 1))
                    for h in range(NH):
                        last = mm(bank(2 + c), wout_sb[:, h, :], y_sb[:, c, h, :], start=(h == 0), stop=(h == NH - 1))
                    last.then_inc(S["outproj_ready"], 1)

                def qk(c):
                    if c == 0:
                        pe.wait_ge(S["decay_ready"], count("decay_ready", 64))
                    pe.wait_ge(S["xn2_ready"], count("xn2_ready", c + 1))
                    xn2 = xn2_sb[:, c * CT:(c + 1) * CT]
                    mm(bank(2 * c), wq_sb[:, :], xn2, start=True, stop=True)
                    mm(bank(2 * c + 1), wk_sb[:, :, :].rearrange("p a n -> p (a n)"), xn2, start=True,
                       stop=True).then_inc(S["qk_ready"], 1)

                def values():
                    pe.wait_ge(S["stack_a_stored"], count("stack_a_stored", 8))
                    for t in range(QT):
                        last = mm(bank(4, 64 * t, 64 * t + 64), xn2_sb[:, t * 128:(t + 1) * 128], wv_sb[:, :],
                                  start=True, stop=True)
                    last.then_inc(S["v_ready"], 1)

                pe.wait_ge(S["delta0_ready"], count("delta0_ready", 1))
                pe.wait_ge(S["brep_stored"], count("brep_stored", 1))
                spread(0, 0, delta_sb, "drep_ready")
                spread_c(1)
                pe.wait_ge(S["du0_ready"], count("du0_ready", 1))
                pe.wait_ge(S["brep_stored"], count("brep_stored", 2))
                spread(0, DU_BANK[0], du_sb, "durep_ready")
                pe.wait_ge(S["dtpre_ready"], count("dtpre_ready", 4))
                spread_b(2)
                in_proj(5)
                spread_c(2)
                spread_b(3)
                spread_c(3)
                pe.wait_ge(S["du1_ready"], count("du1_ready", 1))
                pe.wait_ge(S["crep1_stored"], count("crep1_stored", 2))
                spread(1, DU_BANK[1], du_sb, "durep_ready")
                for i in range(64):
                    pr, c, ng, s = scan_tile(i)
                    dg = 2 * pr + s
                    h, j = dg // 4, dg % 4
                    q = i // 8 + 1
                    if i == 0:
                        pe.wait_ge(S["decay_ready"], count("decay_ready", 8))
                        spread(1, 0, delta_sb, "drep_ready")
                    if i == 4:
                        in_proj(6)
                    if i == 6:
                        in_proj(7)
                    if i == 58:
                        out_proj(0)
                    if i == 60:
                        meansq(count, 2)
                    if i % 8 == 4 and q < 7:
                        pe.wait_ge(S["drive_ready"], count("drive_ready", 4 * q))
                        spread(q + 1, DU_BANK[(q + 1) % 2], du_sb, "durep_ready")
                    if i % 8 == 0 and 1 < q < 8:
                        pe.wait_ge(S["decay_ready"], count("decay_ready", 8 * q))
                        spread(q, 0, delta_sb, "drep_ready")
                    if i == 8:
                        pe.wait_ge(S["gated_ready"], count("gated_ready", 8))
                    if pr == 2 and ng == 0 and s == 0:
                        pe.wait_ge(S["yskip_ready"], count("yskip_ready", c + 1))
                    pe.wait_ge(S["hc_ready"], count("hc_ready", i // 2 + 1))
                    mm(bank(4 + c, rows=slice(32 * j, 32 * j + 32)), C("sum"), hc_sb[:, i % NHC, :],
                       start=(ng == 0), stop=(ng == NG - 1)).then_inc(S["hc_summed"], 1)
                qk(0)
                out_proj(1)

                def scores(n):
                    i, h = n // HEADS, n % HEADS
                    K = (i + 1) * 128
                    if n == 0:
                        pe.wait_ge(S["pad_ready"], count("pad_ready", 1))
                        pe.wait_ge(S["stack_a_stored"], count("stack_a_stored", 2))
                        pe.wait_ge(S["stack_b_stored"], count("stack_b_stored", 1))
                    if n == 6:
                        pe.wait_ge(S["rest1_ready"], count("rest1_ready", NC))
                    if n == 16:
                        pe.wait_ge(S["stack_a_stored"], count("stack_a_stored", 6))
                        pe.wait_ge(S["stack_b_stored"], count("stack_b_stored", 3))
                    if 8 <= n < 16:
                        pe.wait_ge(S["max_ready"], count("max_ready", n - 3))
                    elif n in (16, 17):
                        pe.wait_ge(S["max_ready"], count("max_ready", 2 * n - 18))
                    elif 2 <= n < 6 or n >= 18:
                        pe.wait_ge(S["max_ready"], count("max_ready", n - 1))
                    for k0 in range(0, K, CT):
                        k1 = min(k0 + CT, K)
                        mm(bank(scores_bank(n) + k0 // CT, 0, k1 - k0), qstack[:, 0, h, i * 128:(i + 1) * 128],
                           kstack[:, 0, h // 2, k0:k1], start=True, stop=(k1 < K))
                    mm(bank(scores_bank(n) + k0 // CT, k1 - k0 - 128, k1 - k0), identb[:, :], maskb[:, :],
                       start=False, stop=True).then_inc(S["scores_ready"], 1)

                def max_rows(c):
                    pe.wait_ge(S["maxpart_ready"], count("maxpart_ready", 2 * c + 2))
                    if c == 0:
                        pe.wait_ge(S["stack_a_stored"], count("stack_a_stored", 9))
                        pe.wait_ge(S["v_stored"], count("v_stored", 1))
                    for h in range(HEADS):
                        for i in range(4):
                            last = mm(bank(ROW_BANK[c] + h, i * 128, (i + 1) * 128, rows=slice(96, 98)),
                                      maxpart_sb[:, c, i * HEADS + h, :], identb[:, :], start=True, stop=True)
                    last.then_inc(S["scores_ready"], 1)

                def scores_t(v):
                    c, j, h, q0 = st_unit(v)
                    if v in (0, 16):
                        pe.wait_ge(S["maxrow_a_stored"], count("maxrow_a_stored", c + 1))
                        pe.wait_ge(S["maxrow_b_stored"], count("maxrow_b_stored", c + 1))
                        pe.wait_ge(S["stack_a_stored"], count("stack_a_stored", 5 * c + 4))
                        pe.wait_ge(S["stack_b_stored"], count("stack_b_stored", c + 2))
                        pe.wait_ge(S["v_stored"], count("v_stored", 1))
                    if 2 <= v < 16:
                        pe.wait_ge(S["probs_ready"], count("probs_ready", v - 1))
                    elif v >= 22:
                        pe.wait_ge(S["probs_ready"], count("probs_ready", v - 5))
                    elif v >= 20:
                        pe.wait_ge(S["probs_ready"], count("probs_ready", 16))
                    o = bank(st_bank(v), q0, CT)
                    at = slice(c * CT + q0, (c + 1) * CT)
                    mm(o, kstack[:, 0, h // 2, j * 128:(j + 1) * 128], qstack[:, 0, h, at], start=True,
                       stop=False)
                    last = mm(o, kstack[0:96, 1, h // 2, j * 128:(j + 1) * 128], qstack[0:96, 1, h, at], start=False,
                              stop=(j < 4 * c))
                    if j >= 4 * c:
                        last = mm(bank(st_bank(v), q0, q0 + 128), maskb[:, :], identb[:, :], start=False, stop=True)
                    last.then_inc(S["scorest_ready"], 1)

                def weighted(g):
                    c, j, _, q0 = st_unit(4 * g)
                    pe.wait_ge(S["probs_ready"], count("probs_ready", 4 * g + 4))
                    if g == 4:
                        pe.wait_ge(S["attn_stored"], count("attn_stored", 1))
                    for k in (6, 7) if c == 0 else (6,):
                        for h in range(HEADS):
                            kv = h // (HEADS // KV)
                            last = mm(bank(k, q0, CT, rows=slice(32 * h, 32 * h + 32)),
                                      vt_sb[:, j, kv * HD:(kv + 1) * HD] if k == 6 else C("ones")[:, 0:32],
                                      pt_sb[:, g % 2, h, q0:CT], start=(j == 0), stop=(j == 4 * c + 3))
                    last.then_inc(S["pv_ready"], 1)

                def stack(u):
                    c, m, pair = stack_unit(u)
                    which, parts = (1, K_PARTS) if pair == 0 else (0, Q_PARTS)
                    pe.wait_ge(S["part3_ready" if m else "part2_ready"], count("part3_ready" if m else "part2_ready", c + 1))
                    if u >= 2:
                        pe.wait_ge(S[stack_reader(u - 2)], count(stack_reader(u - 2), stack_reads(u - 2)))
                    for e in range(2):
                        row = 64 * e if pair == 0 else 64 * (pair - 1) + 32 * e
                        rows = slice(row, row + 32)
                        for g, n in enumerate(parts[m]):
                            last = mm(bank(4 + 2 * (u % 2) + e, rows=slice(32 * g, 32 * g + 32)), identb[:, rows],
                                      part_sb[n][:, which, c * CT:(c + 1) * CT], start=True, stop=True)
                    last.then_inc(S["stack_ready"], 1)

                def o_proj(c):
                    pe.wait_ge(S["attn_stored"], count("attn_stored", c + 1))
                    mm(bank(OPROJ_BANK[c]), W("o"), attn_sb[:, c * CT:(c + 1) * CT], start=True,
                       stop=True).then_inc(S["oproj_ready"], 1)

                def gate_up(u):
                    c, m = u // 3, u % 3
                    rows = slice(0, FM[m])
                    pe.wait_ge(S["xn3_ready"], count("xn3_ready", c + 1))
                    if u >= 3:
                        pe.wait_ge(S["swiglu_ready"], count("swiglu_ready", u - 2))
                    xn3 = xn2_sb[:, c * CT:(c + 1) * CT]
                    mm(bank(2 * (u % 3), rows=rows), wgate_sb[:, m * 128:m * 128 + FM[m]], xn3, start=True, stop=True)
                    mm(bank(2 * (u % 3) + 1, rows=rows), wup_sb[:, m * 128:m * 128 + FM[m]], xn3, start=True,
                       stop=True).then_inc(S["gateup_ready"], 1)

                def down(c):
                    for m in range(3):
                        pe.wait_ge(S["swiglu_ready"], count("swiglu_ready", 3 * c + m + 1))
                        last = mm(bank(6 + c), wdown_sb[0:FM[m], m, :], swi_sb[0:FM[m], c, m, :], start=(m == 0),
                                  stop=(m == 2))
                    last.then_inc(S["down_ready"], 1)

                def center(c):
                    pe.wait_ge(S["sum_ready"], count("sum_ready", c + 1))
                    mm(bank(c), C("center"), s_sb[:, c, :], start=True,
                       stop=True).then_inc(S["centered_ready"], 1)

                for u in range(3):
                    stack(u)
                meansq(count, 3)
                qk(1)
                for n in range(18):
                    scores(n)
                    if 3 <= n < 12:
                        stack(n)
                    if n == 12:
                        values()
                max_rows(0)
                for v in range(16):
                    scores_t(v)
                    if v + 18 < 32:
                        scores(v + 18)
                    if v % 4 == 3 and v > 3:
                        weighted(v // 4 - 1)
                max_rows(1)
                weighted(3)
                for g in range(4, 12):
                    for v in range(4 * g, 4 * g + 4):
                        scores_t(v)
                    if g > 4:
                        weighted(g - 1)
                    if g == 5:
                        o_proj(0)
                    if g == 7:
                        meansq(count, 4)
                weighted(11)
                pe.wait_ge(S["probsum_ready"], count("probsum_ready", 8))
                pe.wait_ge(S["xn3_ready"], count("xn3_ready", 1))
                for h in range(HEADS):
                    last = mm(bank(7, rows=slice(32 * h, 32 * h + 32)), C("ones")[:, 0:32], probsum_sb[:, h, :],
                              start=True, stop=True)
                last.then_inc(S["den_ready"], 1)
                gate_up(0)
                o_proj(1)
                gate_up(1)
                meansq(count, 5)
                gate_up(2)
                gate_up(3)
                down(0)
                gate_up(4)
                gate_up(5)
                center(0)
                down(1)
                meansq(count, 6)
                center(1)

                def mlp_first(u):
                    c, m = u // MM, u % MM
                    pe.wait_ge(S["ln1_ready"], count("ln1_ready", c + 1))
                    if u >= 4:
                        pe.wait_ge(S["gelu_ready"], count("gelu_ready", u - 3))
                    mm(bank(2 + u % 4), W("w1", m * 128, (m + 1) * 128), ln1_sb[:, c, :], start=True,
                       stop=True).then_inc(S["mlp_ready"], 1)

                mlp_first(0)
                meansq(count, 7)
                for u in range(1, 8):
                    mlp_first(u)
                for c in range(NC):
                    meansq(count, 8 + c)
                for c in range(NC):
                    pe.wait_ge(S["gelu_ready"], count("gelu_ready", MM * (c + 1)))
                    pe.wait_ge(S["ln1bias_ready"], count("ln1bias_ready", c + 1))
                    for t in range(4):
                        o = bank(6 + c, t * 128, (t + 1) * 128)
                        for m in range(MM):
                            mm(o, gelu_sb[:, c, m, t * 128:(t + 1) * 128], W("w2", m * 128, (m + 1) * 128),
                               start=(m == 0), stop=False)
                        last = mm(o, s_sb[:, c, t * 128:(t + 1) * 128], C("ident"), start=False, stop=True)
                    last.then_inc(S["mlpout_ready"], 1)


def scan_tile(i):
    return i // 16, (i // 8) % 2, (i // 2) % 4, i % 2


def stack_unit(u):
    return u // 6, u // 3 % 2, u % 3


def stack_reader(u):
    return "stack_b_stored" if u in (1, 4, 7) else "stack_a_stored"


def stack_reads(u):
    return sum(stack_reader(v) == stack_reader(u) for v in range(u + 1))


def scores_bank(n):
    if n < 4:
        return n % 2
    return n % 4 if n < 16 else 2 * (n % 2)


def st_bank(v):
    return 4 + v % 2 if v < 16 else (v - 16) % 6


def st_unit(v):
    c, g = (0, v // 4) if v < 16 else (1, v // 4 - 4)
    return c, g, v % 4, max(0, (g - 4 * c) * 128)


def kernel(**inputs):
    import numpy as np
    import concourse.bacc as bacc
    from concourse.bass_utils import run_bass_kernel_spmd

    f = {k.replace("L0_", ""): np.asarray(v) for k, v in inputs.items()}

    def halves(a, n):
        return a.reshape(n, 128, -1).transpose(1, 0, 2).reshape(128, -1)

    down = np.zeros((384, D), np.float32)
    down[:FFN] = f["attn_down_w"].T
    alog = f["attn_A_log"].reshape(DG, DS, NG, NS).transpose(3, 1, 0, 2).reshape(128, DG * NG)
    parts = {
        "in": f["attn_in_proj_w"].T, "xp": halves(f["attn_x_proj_w"].T, 2), "out": halves(f["attn_out_proj_w"].T, 2),
        "q": f["attn_q_w"].T, "k": f["attn_k_w"].T, "v": f["attn_v_w"].T, "o": f["attn_o_w"].T,
        "gate": f["attn_gate_w"].T, "up": f["attn_up_w"].T, "down": halves(down, 3),
        "w1": f["ffn_w1"], "w2": halves(f["ffn_w2"], 4),
        "nm": f["attn_norm_m_w"][:, None], "na": f["attn_norm_attn_w"][:, None], "nf": f["attn_norm_ffn_w"][:, None],
        "cb": f["attn_conv_b"].reshape(2, 128).T, "taps": f["attn_conv_w"][128:, 0, :],
        "dtw": f["attn_dt_w"].reshape(2, 128).T,
        "dtb": f["attn_dt_b"].reshape(2, 128).T, "dsk": f["attn_D_skip"].reshape(2, 128).T,
        "b1": f["ffn_b1"].reshape(4, 128).T, "alog": alog,
    }
    wts = np.ascontiguousarray(np.concatenate([parts[k] for k in W_COLS], axis=1))
    p, q = np.arange(128)[:, None], np.arange(128)[None, :]
    eye = (p == q).astype(np.float32)
    consts = {
        "ident": eye, "center": eye - np.float32(1 / 128), "mean": np.full((128, 128), 1 / 128, np.float32),
        "selD": np.concatenate([(p % 32 == q % 32) & (p // 32 == j) for j in range(4)], axis=1),
        "sum": (p % 32 == np.arange(32)[None, :]).astype(np.float32),
        "mask": np.where(q > p, np.float32(-1e30), np.float32(0)),
        "ones": np.ones((128, 128), np.float32),
        "less1": -(p // 32 >= 1).astype(np.float32), "less2": -(p // 32 >= 2).astype(np.float32),
    }
    cst = np.ascontiguousarray(np.concatenate([consts[k] for k in C_COLS], axis=1).astype(np.float32))
    arrays = {
        "x": np.ascontiguousarray(f["attn_x"].reshape(BATCH * SEQ, D).T), "wts": wts, "cst": cst,
        "convw": np.ascontiguousarray(f["attn_conv_w"][:, 0, :].T.reshape(1, -1)), "b2": f["ffn_b2"].reshape(D, 1),
    }
    nc = bacc.Bacc("TRN2", target_bir_lowering=False, num_devices=1)
    args = [nc.dram_tensor(n, a.shape, mybir.dt.float32, kind="ExternalInput").ap() for n, a in arrays.items()]
    out = nc.dram_tensor("out", (128, BATCH * QT, D), mybir.dt.float32, kind="ExternalOutput").ap()
    build(nc, *args, out)
    r = run_bass_kernel_spmd(nc, [arrays], core_ids=[0])
    return np.ascontiguousarray(r.results[0]["out"].transpose(1, 0, 2)).reshape(BATCH, SEQ, D)
```
